# Optimizing a Trainium2 kernel written in Bass

```python
import numpy as np
import jax
import jax.numpy as jnp

def _softmax(x, axis=-1):
    return jax.nn.softmax(x, axis=axis)

def _gelu(x):
    return jax.nn.gelu(x, approximate=True)

def _silu(x):
    return jax.nn.silu(x)

def _sigmoid(x):
    return jax.nn.sigmoid(x)

def _layernorm(x, axis=-1, eps=1e-05):
    m = jnp.mean(x, axis=axis, keepdims=True)
    v = jnp.var(x, axis=axis, keepdims=True)
    return (x - m) / jnp.sqrt(v + eps)

def _scatter_add(tgt, idx, src, axis=0):
    return tgt.at[idx].add(src)

def _segment_sum(src, seg, n):
    return jax.ops.segment_sum(src, seg, n)
kernel_name = 'mk_gnn_ffn_d1_gnn_r32_8581ef'

def setup_inputs(seed: int=0):
    np.random.seed(seed)
    _w = jnp.asarray

    def _rec_inputs():
        import jax
        import jax.numpy as jnp
        _gk = jax.random.key(seed)
        x = -0.0003713 + 1 * jax.random.normal(jax.random.fold_in(_gk, 1), (3125, 256), jnp.float32)
        src = jax.random.randint(jax.random.fold_in(_gk, 2), (50000,), 0, 3125, jnp.int32)
        dst = jax.random.randint(jax.random.fold_in(_gk, 3), (50000,), 0, 3125, jnp.int32)
        _o = jnp.argsort(dst, stable=True)
        src = src[_o]
        dst = dst[_o]
        return (x, src, dst)
    x, src, dst = _rec_inputs()

    def _L0_gnn_setup():
        import jax, jax.numpy as jnp
        import numpy as np
        N = 50000
        E = 12500
        D_IN = 256
        D_HID = 256
        D_OUT = 256

        def _sage_conv(x, edge_index, W_l, W_r, b):
            src, dst = (edge_index[0], edge_index[1])
            msgs = x[src]
            agg_sum = jax.ops.segment_sum(msgs, dst, num_segments=x.shape[0])
            deg = jax.ops.segment_sum(jnp.ones((edge_index.shape[1],), x.dtype), dst, num_segments=x.shape[0])
            agg = agg_sum / jnp.maximum(deg, 1.0)[:, None]
            return agg @ W_l + x @ W_r + b
        key = jax.random.key(seed)
        ks = jax.random.split(key, 8)
        x = jax.random.normal(ks[0], (N, D_IN), dtype=jnp.float32)
        edge_index = jax.random.randint(ks[1], (2, E), 0, N, dtype=jnp.int64)

        def glorot(k, fan_in, fan_out):
            lim = float(np.sqrt(6.0 / (fan_in + fan_out)))
            return jax.random.uniform(k, (fan_in, fan_out), jnp.float32, -lim, lim)
        return {'x': x, 'edge_index': edge_index, 'W1_l': glorot(ks[2], D_IN, D_HID), 'W1_r': glorot(ks[3], D_IN, D_HID), 'b1': jnp.zeros((D_HID,), jnp.float32), 'W2_l': glorot(ks[4], D_HID, D_OUT), 'W2_r': glorot(ks[5], D_HID, D_OUT), 'b2': jnp.zeros((D_OUT,), jnp.float32)}
    _L0_gnn_all = _L0_gnn_setup()
    _L0_gnn_in = {k: v for k, v in _L0_gnn_all.items() if k in ('W1_l', 'W1_r', 'b1', 'W2_l', 'W2_r', 'b2')}
    del _L0_gnn_all

    def _L0_ffn_setup():
        import jax, jax.numpy as jnp
        import numpy as np
        NUM_EXPERTS = 8
        TOP_K = 2
        B, S, D = (8, 256, 256)

        def _moe(tokens, router_w, w1, b1, w2, b2):
            N = tokens.shape[0]
            E = router_w.shape[0]
            logits = tokens.astype(jnp.float32) @ router_w.astype(jnp.float32).T
            probs = jax.nn.softmax(logits, axis=-1)
            rw, re = jax.lax.top_k(probs, TOP_K)
            if TOP_K > 1:
                rw = rw / jnp.maximum(rw.sum(-1, keepdims=True), 1e-12)
            rw = rw.astype(tokens.dtype)
            combine = jnp.zeros((N, E), tokens.dtype).at[jnp.arange(N)[:, None], re].set(rw)
            out = tokens
            for e in range(E):
                h = jax.nn.gelu(tokens @ w1[e] + b1[e], approximate=False)
                y = h @ w2[e] + b2[e]
                out = out + combine[:, e:e + 1] * y
            return out
        key = jax.random.key(seed)
        ks = jax.random.split(key, 4)
        scale = 1.0 / np.sqrt(D).astype(np.float32)
        return {'input_embeddings': jax.random.normal(ks[0], (B, S, D), jnp.float32), 'router_w': jax.random.normal(ks[1], (NUM_EXPERTS, D), jnp.float32) * scale, 'w1': jax.random.normal(ks[2], (NUM_EXPERTS, D, D), jnp.float32) * scale, 'b1': jnp.zeros((NUM_EXPERTS, D), jnp.float32), 'w2': jax.random.normal(ks[3], (NUM_EXPERTS, D, D), jnp.float32) * scale, 'b2': jnp.zeros((NUM_EXPERTS, D), jnp.float32)}
    _L0_ffn_all = _L0_ffn_setup()
    _L0_ffn_in = {k: v for k, v in _L0_ffn_all.items() if k in ('router_w', 'w1', 'b1', 'w2', 'b2')}
    del _L0_ffn_all
    return {'x': x, 'src': src, 'dst': dst, 'L0_gnn_W1_l': _L0_gnn_in['W1_l'], 'L0_gnn_W1_r': _L0_gnn_in['W1_r'], 'L0_gnn_b1': _L0_gnn_in['b1'], 'L0_gnn_W2_l': _L0_gnn_in['W2_l'], 'L0_gnn_W2_r': _L0_gnn_in['W2_r'], 'L0_gnn_b2': _L0_gnn_in['b2'], 'L0_ffn_router_w': _L0_ffn_in['router_w'], 'L0_ffn_w1': _L0_ffn_in['w1'], 'L0_ffn_b1': _L0_ffn_in['b1'], 'L0_ffn_w2': _L0_ffn_in['w2'], 'L0_ffn_b2': _L0_ffn_in['b2']}

def reference(x, src, dst, L0_gnn_W1_l, L0_gnn_W1_r, L0_gnn_b1, L0_gnn_W2_l, L0_gnn_W2_r, L0_gnn_b2, L0_ffn_router_w, L0_ffn_w1, L0_ffn_b1, L0_ffn_w2, L0_ffn_b2):
    import jax
    import jax.numpy as jnp

    def _L0_gnn_ref(x, edge_index, W1_l, W1_r, b1, W2_l, W2_r, b2):
        import jax, jax.numpy as jnp
        import numpy as np
        N = 50000
        E = 12500
        D_IN = 256
        D_HID = 256
        D_OUT = 256

        def _sage_conv(x, edge_index, W_l, W_r, b):
            src, dst = (edge_index[0], edge_index[1])
            msgs = x[src]
            agg_sum = jax.ops.segment_sum(msgs, dst, num_segments=x.shape[0])
            deg = jax.ops.segment_sum(jnp.ones((edge_index.shape[1],), x.dtype), dst, num_segments=x.shape[0])
            agg = agg_sum / jnp.maximum(deg, 1.0)[:, None]
            return agg @ W_l + x @ W_r + b
        h = _sage_conv(x, edge_index, W1_l, W1_r, b1)
        h = jax.nn.relu(h)
        out = _sage_conv(h, edge_index, W2_l, W2_r, b2)
        return out

    def _L0_ffn_ref(input_embeddings, router_w, w1, b1, w2, b2):
        import jax, jax.numpy as jnp
        import numpy as np
        NUM_EXPERTS = 8
        TOP_K = 2
        B, S, D = (8, 256, 256)

        def _moe(tokens, router_w, w1, b1, w2, b2):
            N = tokens.shape[0]
            E = router_w.shape[0]
            logits = tokens.astype(jnp.float32) @ router_w.astype(jnp.float32).T
            probs = jax.nn.softmax(logits, axis=-1)
            rw, re = jax.lax.top_k(probs, TOP_K)
            if TOP_K > 1:
                rw = rw / jnp.maximum(rw.sum(-1, keepdims=True), 1e-12)
            rw = rw.astype(tokens.dtype)
            combine = jnp.zeros((N, E), tokens.dtype).at[jnp.arange(N)[:, None], re].set(rw)
            out = tokens
            for e in range(E):
                h = jax.nn.gelu(tokens @ w1[e] + b1[e], approximate=False)
                y = h @ w2[e] + b2[e]
                out = out + combine[:, e:e + 1] * y
            return out
        b, s, d = input_embeddings.shape
        tokens = input_embeddings.reshape(b * s, d)
        return _moe(tokens, router_w, w1, b1, w2, b2).reshape(b, s, d)
    edge_index = jnp.stack([src, dst])
    x = x + _L0_gnn_ref(_layernorm(x, axis=-1), edge_index, L0_gnn_W1_l, L0_gnn_W1_r, L0_gnn_b1, L0_gnn_W2_l, L0_gnn_W2_r, L0_gnn_b2)
    x = x + _L0_ffn_ref(_layernorm(x, axis=-1)[None], L0_ffn_router_w, L0_ffn_w1, L0_ffn_b1, L0_ffn_w2, L0_ffn_b2)[0]
    return x

_drawn_inputs = setup_inputs


def setup_inputs(seed=0):
    import zlib

    import numpy as np

    out = dict(_drawn_inputs(seed))
    spreads = {'L0_gnn_b1': (0.0, 0.1),
     'L0_gnn_b2': (0.0, 0.1),
     'L0_ffn_b1': (0.0, 0.378),
     'L0_ffn_b2': (0.0, 0.1)}
    factors = {}
    for name, (base, spread) in spreads.items():
        noise = np.random.default_rng([zlib.crc32(name.encode()), seed]).standard_normal(out[name].shape)
        drawn = base * np.exp(spread * noise) if base else spread * noise
        out[name] = jnp.asarray(drawn.astype(out[name].dtype))
    for name, factor in factors.items():
        out[name] = (out[name] * factor).astype(out[name].dtype)
    return out
```

```python
from contextlib import ExitStack

import concourse.bass as bass
from concourse import mybir

F32 = mybir.dt.float32
F16 = mybir.dt.float16
I32 = mybir.dt.int32
U32 = mybir.dt.uint32
ALU = mybir.AluOpType
ACT = mybir.ActivationFunctionType
AX = mybir.AxisListType
RMAX = bass.bass_isa.ReduceOp.max

P = 128
EPS = 1e-5
EXPONENT_AT = 23


def build(nc, x, src, dst, w1l, w1r, b1, w2l, w2r, b2, router_w, ew1, eb1, ew2, eb2, out):
    N, D = x.shape
    E = src.shape[0]
    KD = D // P
    NT = -(-N // P)
    LAST = N - (NT - 1) * P
    WD = 12
    KEYS = NT * WD
    WPG = 88
    NG = 3
    NW = NG * WPG
    NPAIR = NW // 2
    RUN = 250
    JE = RUN // 2
    PAIRS_PER_TILE = 4
    CHUNK = 400
    NCH = E // CHUNK
    AC = NT * P
    YW = 2 * D + 2
    NE = router_w.shape[0]
    TOPK = 2
    REGION = N + P + (-(N + P)) % 16
    MAX_TILES = (TOPK * N) // P + NE
    MIN_TILES = (TOPK * N) // P
    YS_TILES = MAX_TILES + 1
    SPARE = YS_TILES - MIN_TILES
    MIN_PAIRS = (TOPK * N) // P // 2
    NTAB = MAX_TILES + 5
    assert NCH <= P and NCH * CHUNK == E and NW * WD >= N and KEYS <= 512 and NW * WD <= AC

    with ExitStack() as ctx:
        def sb(name, shape, dt):
            return ctx.enter_context(nc.sbuf_tensor(name, shape, dt))

        def sem(name):
            return ctx.enter_context(nc.semaphore(name))

        bank = [ctx.enter_context(nc.psum_tensor(f"bank{i}", [P, 512], F32)) for i in range(4, 8)]
        counts_ps = ctx.enter_context(nc.psum_tensor("counts_ps", [P, 4, 512], F32))

        z1_dram = nc.dram_tensor("z1_dram", (NT * P, D), F32, kind="Internal").ap()
        z2_dram = nc.dram_tensor("z2_dram", (NT * P, D), F32, kind="Internal").ap()
        y2_dram = nc.dram_tensor("y2_dram", (NT * P, 2 * D), F16, kind="Internal").ap()
        u_dram = nc.dram_tensor("u_dram", (NT * P, D), F32, kind="Internal").ap()
        xs_dram = nc.dram_tensor("xs_dram", (NE * REGION, D), F32, kind="Internal").ap()
        ys_dram = nc.dram_tensor("ys_dram", ((YS_TILES + SPARE) * P, D), F32, kind="Internal").ap()
        ys_rows = ys_dram[0:YS_TILES * P, :]

        adj = sb("adj", [P, NT, AC], F16)
        y = sb("y", [P, NT, YW], F16)
        w = sb("w", [P, KD, 2 * D], F32)
        b1b = sb("b1b", [P, D], F32)
        b2b = sb("b2b", [P, D], F32)
        ident = sb("ident", [P, P], F32)
        ones = sb("ones", [P, P], F32)
        iota_h = sb("iota_h", [P, KEYS], F16)
        oh_src = sb("oh_src", [P, 2, 4, P], F16)
        oh_key = sb("oh_key", [P, 2, 4, KEYS], F16)
        key_t = sb("key_t", [P, 2, NW], F32)
        lo_t = sb("lo_t", [P, 2, NW], F32)
        rows = sb("rows", [P, 4 * D], F32)
        xt, nrm, nrm_t, zi = (rows[:, k * D:(k + 1) * D] for k in range(4))
        zt = sb("zt", [P, D], F32)
        yo = sb("yo", [P, 2 * D], F16)
        stat = sb("stat", [P, 16], F32)
        rdeg = sb("rdeg", [P, NT], F32)
        scl = sb("scl", [P, 16], F32)
        scl_i = sb("scl_i", [P, 16], I32)
        flag = sb("flag", [P, 8], F32)
        flag_all = sb("flag_all", [P, 8], F32)
        flag_i = sb("flag_i", [P, 2], I32)

        edge_i = rows[0:NCH, 0:CHUNK].bitcast(I32)
        edge_lo = rows[0:NCH, 2 * D:2 * D + CHUNK]
        edge_dst = key_t[0:NCH, :, :].rearrange("p a b -> p (a b)")[:, 0:CHUNK]
        edge_blk = lo_t[0:NCH, :, :].rearrange("p a b -> p (a b)")[:, 0:CHUNK]
        w_flat = w[:, :, :].rearrange("p k n -> p (k n)")
        edge_key = w_flat[0:NCH, 0:CHUNK]
        edge_rel = w_flat[0:NCH, CHUNK:2 * CHUNK]
        zero_h = yo[0:NCH, 0:P]
        window_at = stat[0:NCH, 15:16]
        STEP = 4
        STEPS = CHUNK // STEP

        used = [0]
        adj_flat = adj[:, :, :].rearrange("p b c -> p (b c)")

        def early(shape, dt, parts=P):
            n = 1
            for d in shape:
                n *= d
            a = adj_flat[0:parts, used[0]:used[0] + 2 * n].bitcast(dt)
            used[0] += 2 * n
            assert used[0] <= NT * AC - AC
            return a.rearrange("p (a b) -> p a b", b=shape[1]) if len(shape) == 2 else a

        dchunk = early([CHUNK], I32, NCH)
        dchunk_f = early([CHUNK], F32, NCH)
        dnext = early([2], I32, NCH)
        dnext_f = early([2], F32, NCH)
        falls = early([CHUNK], F32, NCH)
        wstart = early([NW], I32, NCH)
        below = early([NW], F32, NCH)
        wlo_i = early([4], I32, WPG)
        wlo = early([4], F32, WPG)
        row_f = early([NG], F32, WPG)
        row_u = early([NG], U32, WPG)
        crow = early([NG, CHUNK], I32, WPG)
        cless = early([NG, CHUNK], F32, WPG)
        start_f = early([NG], F32, WPG)
        start_u = early([NG], U32, WPG)
        cnt_f = early([NG], F32, WPG)
        run_d = early([NG, RUN], I32, WPG)
        run_s = early([NG, RUN], I32, WPG)
        rel = early([NG, RUN], F32, WPG)
        valid = early([NG, RUN], F32, WPG)
        inside = early([NG, RUN], F32, WPG)
        blk_i = early([NG, RUN], I32, WPG)
        lo_i = early([NG, RUN], I32, WPG)
        key_f = early([NG, RUN], F32, WPG)
        key1 = early([NG, RUN], F32, WPG)
        lo1 = early([NG, RUN], F32, WPG)
        last_in = early([NG], F32, WPG)
        not_end = early([NG], F32, WPG)
        b1sq = early([D], F32)
        w2_early = early([KD, 2 * D], F32)
        wsq = [early([KD, 2 * D], F32) for _ in range(2)]

        oh_flat = oh_key[:, :, :, :].rearrange("p a b c -> p (a b c)")
        oh_used = [0]

        def later(shape, dt, flat=oh_flat, used=oh_used):
            n = 1
            for d in shape:
                n *= d
            a = flat[:, used[0]:used[0] + 2 * n].bitcast(dt)
            used[0] += 2 * n
            if len(shape) == 2:
                a = a.rearrange("p (a b) -> p a b", b=shape[1])
            if len(shape) == 3:
                a = a.rearrange("p (a b c) -> p a b c", b=shape[1], c=shape[2])
            return a

        tok = [nrm[:, :], later([D], F32)]
        uo = later([D], F32)
        tri = later([P], F32)
        rw_t = later([KD, NE], F32)
        iota_e = later([NE], F32)
        iota_ei = later([NE], I32)
        lg = later([NE], F32)
        mx = later([NE], F32)
        mix = later([NE], U32)
        neg = later([1], F32)
        pick = later([TOPK], F32)
        mask = later([TOPK, NE], F32)
        both = later([NE], F32)
        ex = later([NE], F32)
        esum = later([2], F32)
        prob = later([TOPK + 2], F32)
        base_e = later([NE], F32)
        pos = later([NE], F32)
        posm = later([TOPK, NE], F32)
        slot_f = later([TOPK], F32)
        slot_u = [later([TOPK], U32) for _ in range(2)]
        coef = later([NT, TOPK], F32)
        slots = later([NT, TOPK], U32)
        assert oh_used[0] <= 2 * 4 * KEYS

        moe_used = [0]

        def expert(shape, dt):
            a = later(shape, dt, adj_flat, moe_used)
            assert moe_used[0] <= NT * AC
            return a

        ew1_sb = expert([NE, KD, D], F32)
        ew2_sb = expert([NE, KD, D], F32)
        eb1_sb = expert([NE, D], F32)
        eb2_sb = expert([NE, D], F32)
        zero_t = expert([SPARE, D], F32)
        xe = [expert([D], F32) for _ in range(2)]
        xe_t = [expert([D], F32) for _ in range(2)]
        hb = [expert([D], F32) for _ in range(2)]
        ge = [expert([D], F32) for _ in range(2)]
        ge_t = [expert([D], F32) for _ in range(2)]
        ye = [expert([D], F32) for _ in range(2)]
        cnt = expert([NE], F32)
        end_i = expert([NE], I32)
        nt_i = expert([NE], I32)
        nt_f = expert([NE], F32)
        cum = [expert([NE], F32) for _ in range(4)]
        jump = expert([NE], F32)
        first_row = expert([NE], F32)
        iota_j = expert([NTAB], I32)
        jf = expert([NTAB], F32)
        tab_e = expert([NTAB], F32)
        tab_r = expert([NTAB], F32)
        past = expert([NTAB], F32)
        stay = expert([NTAB], F32)
        tab_ei = expert([NTAB], I32)
        tab_ri = expert([NTAB], I32)
        npair_i = expert([2], I32)
        ends_i = expert([2], I32)
        slots_f = expert([NT * TOPK], F32)
        moved = expert([NT * TOPK], F32)
        slots_y = expert([NT, TOPK], U32)
        place_f = [expert([NT * TOPK], F32) for _ in range(2)]
        RING = 3
        assert (NT - 1) % RING == 0
        yg = expert([RING * TOPK, D], F32)
        ug = expert([RING, D], F32)
        og = expert([RING, D], F32)
        gix = expert([RING, TOPK], U32)

        names = ["edges_in", "x_in", "w_in", "consts", "iota", "first_ge", "firsts", "chunk_ix", "chunk_in", "start_ix",
                 "run_in", "keys", "keys_tr", "keys_in", "onehot", "counted", "adj_in", "wsq", "wnorm", "wsum", "wroot",
                 "scaled", "var_in", "rstd_in", "normed", "nrm_tr", "nrm_t_in", "projected", "hi_in", "yz_in", "z_out",
                 "agg", "z_in", "h_in", "y2_out", "x2_in", "out_sem", "pad_ok", "flag_in", "flag_all",
                 "tri_in", "rw_in", "u_ready", "u_out", "logits", "top", "expd", "masks", "prefix", "slots", "scattered",
                 "flag_out", "all_in", "all_free", "all_keys", "all_onehot", "all_counted", "all_open", "all_window", "all_kept",
                 "all_done", "held", "pool_held", "table", "padded", "zeros", "ew_in", "xe_in", "xe_tr", "xe_t_in", "hid", "hb_in", "ge_in", "ge_tr",
                 "ge_t_in", "ye_ps", "ye_in", "ye_out", "gix_in", "yg_in", "ug_in", "og_in", "og_out"]
        S = {n: sem(n) for n in names}
        NQ = 5
        y2_in = [sem(f"y2_in{c}") for c in range(NQ)]
        chain = sem("dve_chain")
        xe_in = [sem(f"xe_in{h}") for h in range(2)]
        ye_out = [sem(f"ye_out{h}") for h in range(2)]
        sum_out_of = [sem(f"sum_out{q}") for q in range(RING)]
        yg_in = [sem(f"yg_in{q}") for q in range(RING)]
        ug_in = [sem(f"ug_in{q}") for q in range(RING)]

        block = ctx.enter_context(nc.Block())
        runs_src = src[0:E].rearrange("(p c) -> p c", c=RUN)
        runs_dst = dst[0:E].rearrange("(p c) -> p c", c=RUN)
        chunks = dst.rearrange("(p c) -> p c", c=CHUNK)

        def tile_rows(ap, t):
            return ap[bass.ds(t * P, P), :]

        @block.sync
        def _(sp):
            sp.dma_start(dchunk, chunks).then_inc(S["edges_in"], 16)
            sp.dma_start(dnext[0:NCH - 1, 0:1], chunks[1:NCH, 0:1]).then_inc(S["edges_in"], 16)
            sp.dma_start(xt[:, :], x[0:P, :]).then_inc(S["x_in"], 16)
            for to, (l, r) in ((w, (w1l, w1r)), (w2_early, (w2l, w2r))):
                sp.dma_start(to[:, :, 0:D], l.rearrange("(k p) n -> p k n", p=P)).then_inc(S["w_in"], 16)
                sp.dma_start(to[:, :, D:2 * D], r.rearrange("(k p) n -> p k n", p=P)).then_inc(S["w_in"], 16)
            for b, v in ((b1b, b1), (b2b, b2)):
                sp.dma_start(b[:, :], v.rearrange("(a n) -> a n", a=1).to_broadcast((P, D))).then_inc(S["w_in"], 16)
            with sp.Fori(0, NT - 2) as t:
                sp.wait_ge(S["normed"], t + 1)
                sp.dma_start(xt[:, :], tile_rows(x, t + 1)).then_inc(S["x_in"], 16)
                sp.wait_ge(S["yz_in"], t + 1)
                sp.dma_start(tile_rows(z1_dram, t), zt[:, :]).then_inc(S["z_out"], 16)
            sp.wait_ge(S["pad_ok"], 1)
            sp.dma_start(xt[0:LAST, :], x[(NT - 1) * P:N, :]).then_inc(S["x_in"], 16)
            for t in range(NT - 2, NT):
                sp.wait_ge(S["yz_in"], t + 1)
                sp.dma_start(z1_dram[t * P:(t + 1) * P, :], zt[:, :]).then_inc(S["z_out"], 16)
            sp.wait_ge(S["flag_out"], 1)
            with sp.If(sp.value_load(flag_i[0:1, 0:1], min_val=0, max_val=1) == 1):
                sp.wait_ge(S["projected"], NT)
                sp.wait_ge(S["adj_in"], NPAIR)
                sp.dma_start(edge_i, chunks).then_inc(S["all_in"], 16)
                sp.wait_ge(S["all_free"], 1)
                sp.dma_start(edge_i, src.rearrange("(p c) -> p c", c=CHUNK)).then_inc(S["all_in"], 16)
                sp.wait_ge(S["all_done"], 1)
            sp.wait_ge(S["projected"], NT)
            sp.dma_start(w[:, :, 0:D], w2l.rearrange("(k p) n -> p k n", p=P)).then_inc(S["w_in"], 16)
            sp.dma_start(w[:, :, D:2 * D], w2r.rearrange("(k p) n -> p k n", p=P)).then_inc(S["w_in"], 16)
            sp.wait_ge(S["z_out"], 16 * NT)
            sp.dma_start(zi[:, :], z1_dram[0:P, :]).then_inc(S["z_in"], 16)
            with sp.Fori(0, NT - 1) as t:
                sp.wait_ge(S["h_in"], t + 1)
                sp.dma_start(zi[:, :], tile_rows(z1_dram, t + 1)).then_inc(S["z_in"], 16)
                sp.wait_ge(S["yz_in"], t + 1 + NT)
                sp.dma_start(tile_rows(z2_dram, t), zt[:, :]).then_inc(S["y2_out"], 16)
                sp.dma_start(tile_rows(y2_dram, t), yo[:, :]).then_inc(S["y2_out"], 16)
            sp.wait_ge(S["yz_in"], 2 * NT)
            sp.dma_start(z2_dram[(NT - 1) * P:, :], zt[:, :]).then_inc(S["y2_out"], 16)
            sp.dma_start(y2_dram[(NT - 1) * P:, :], yo[:, :]).then_inc(S["y2_out"], 16)
            sp.wait_ge(S["y2_out"], 32 * NT)
            y2v = y2_dram.rearrange("(t p) c -> p t c", p=P)
            for c in range(NQ):
                sp.dma_start(y[:, NT // NQ * c:NT // NQ * (c + 1), 0:2 * D], y2v[:, NT // NQ * c:NT // NQ * (c + 1), :]
                             ).then_inc(y2_in[c], 16)
                if c == 0:
                    sp.dma_start(zi[:, :], z2_dram[0:P, :]).then_inc(S["z_in"], 16)
                    sp.dma_start(xt[:, :], x[0:P, :]).then_inc(S["x_in"], 16)
            for k in range(KD):
                sp.dma_start(rw_t[:, k, :], router_w[:, k * P:(k + 1) * P].rearrange("e p -> p e")
                             ).then_inc(S["rw_in"], 16)
            with sp.Fori(0, NT - 2) as t:
                sp.wait_ge(S["x2_in"], t + 1)
                sp.dma_start(zi[:, :], tile_rows(z2_dram, t + 1)).then_inc(S["z_in"], 16)
                sp.dma_start(xt[:, :], tile_rows(x, t + 1)).then_inc(S["x_in"], 16)
                sp.wait_ge(S["u_ready"], t + 1)
                sp.dma_start(tile_rows(u_dram, t), uo).then_inc(S["u_out"], 16)
            sp.wait_ge(S["x2_in"], NT - 1)
            sp.dma_start(zi[:, :], z2_dram[(NT - 1) * P:, :]).then_inc(S["z_in"], 16)
            sp.dma_start(xt[0:LAST, :], x[(NT - 1) * P:N, :]).then_inc(S["x_in"], 16)
            for t in range(NT - 2, NT):
                sp.wait_ge(S["u_ready"], t + 1)
                sp.dma_start(u_dram[t * P:(t + 1) * P, :], uo).then_inc(S["u_out"], 16)
            sp.wait_ge(S["agg"], 2 * NT)
            for to, w_e in ((ew1_sb, ew1), (ew2_sb, ew2)):
                for e in range(NE):
                    sp.dma_start(to[:, e, :, :], w_e[e].rearrange("(k p) n -> p k n", p=P)).then_inc(S["ew_in"], 16)
            for to, b_e in ((eb1_sb, eb1), (eb2_sb, eb2)):
                sp.dma_start(to, b_e.rearrange("(a e) n -> a e n", a=1).to_broadcast((P, NE, D))
                             ).then_inc(S["ew_in"], 16)
            sp.wait_ge(S["table"], 1)
            sp.wait_ge(S["zeros"], 1)
            for e in range(NE):
                end = sp.value_load(end_i[0:1, e:e + 1], min_val=e * REGION, max_val=e * REGION + N)
                sp.dma_start(xs_dram[bass.ds(end, P), :], zero_t[:, 0, :]).then_inc(S["padded"], 16)
            end = sp.value_load(ends_i[0:1, 0:1], min_val=MIN_TILES * P, max_val=YS_TILES * P)
            sp.dma_start(ys_dram[bass.ds(end, SPARE * P), :].rearrange("(t p) n -> p t n", p=P), zero_t
                         ).then_inc(S["padded"], 16)
            sp.wait_ge(S["padded"], 16 * (NE + 1))
            sp.wait_ge(S["scattered"], 16 * TOPK * NT)
            pairs = sp.value_load(npair_i[0:1, 0:1], min_val=MIN_PAIRS, max_val=(MAX_TILES + 1) // 2)

            def load_pair(i):
                for h in range(2):
                    row = sp.value_load(tab_ri[0:1, bass.ds(i * 2 + h, 1)], min_val=0, max_val=NE * REGION - P)
                    sp.dma_start(xe[h], xs_dram[bass.ds(row, P), :]).then_inc(xe_in[h], 16)

            load_pair(0)
            with sp.Fori(0, pairs) as i:
                sp.wait_ge(S["xe_tr"], i + 1)
                load_pair(i + 1)
            sp.wait_ge(S["u_out"], 16 * NT)
            for t in range(RING):
                sp.dma_start(ug[:, t, :], u_dram[t * P:(t + 1) * P, :]).then_inc(ug_in[t], 16)

            def sum_out(t, s, more=True):
                sp.wait_ge(S["og_in"], t + 1)
                sp.dma_start(tile_rows(out, t), og[:, s, :]).then_inc(sum_out_of[s], 16)
                if more:
                    sp.dma_start(ug[:, s, :], tile_rows(u_dram, t + RING)).then_inc(ug_in[s], 16)

            sum_out(0, 0)
            with sp.Fori(0, NT // RING - 1) as i:
                for q in range(RING):
                    sum_out(i * RING + (q + 1), (q + 1) % RING)
            for t in range(NT - RING, NT - 1):
                sum_out(t, t % RING, False)
            sp.wait_ge(S["og_in"], NT)
            sp.dma_start(out[(NT - 1) * P:N, :], og[0:LAST, (NT - 1) % RING, :]
                         ).then_inc(sum_out_of[(NT - 1) % RING], 16)
            for q in range(RING):
                sp.wait_ge(sum_out_of[q], 16 * len(range(q, NT, RING)))

        @block.gpsimd
        def _(pool):
            g = nc.gpsimd
            g.iota(wstart, [[WD, NW]], base=0, channel_multiplier=0).then_inc(S["iota"], 1)
            g.iota(wlo_i[:, 0:NG], [[WD * WPG, NG]], base=0, channel_multiplier=WD).then_inc(S["iota"], 1)
            g.iota(iota_h[:, :], [[1, KEYS]], base=1, channel_multiplier=0,
                   allow_small_or_imprecise_dtypes=True).then_inc(S["iota"], 1)
            pool.wait_ge(S["consts"], 1)
            g.affine_select(out=ident[:, :], in_=ident[:, :], compare_op=ALU.not_equal, fill=1.0, base=0,
                            pattern=[[-1, P]], channel_multiplier=1).then_inc(S["iota"], 1)
            pool.wait_ge(S["chunk_ix"], 1)
            for k in range(NG):
                g.indirect_dma_start(crow[:, k, :], None, chunks,
                                     bass.IndirectOffsetOnAxis(ap=row_u[:, k:k + 1], axis=0)
                                     ).then_inc(S["chunk_in"], 16)
            pool.wait_ge(S["start_ix"], 1)
            for k in range(NG):
                for r, v in ((run_d, runs_dst), (run_s, runs_src)):
                    g.indirect_dma_start(r[:, k, :], None, v,
                                         bass.IndirectOffsetOnAxis(ap=start_u[:, k:k + 1], axis=1)
                                         ).then_inc(S["run_in"], 16)
            with pool.Fori(0, NT) as t:
                pool.wait_ge(S["var_in"], t + 1)
                g.tensor_tensor(stat[:, 8:9], stat[:, 9:10], stat[:, 10:11], ALU.pow).then_inc(S["rstd_in"], 1)
            pool.wait_ge(S["flag_in"], 1)
            g.partition_all_reduce(flag_all[:, :], flag[:, :], P, RMAX).then_inc(S["flag_all"], 1)
            pool.wait_ge(S["agg"], 1)
            g.iota(iota_ei, [[1, NE]], base=0, channel_multiplier=0).then_inc(S["iota"], 1)
            pool.wait_ge(S["tri_in"], 1)
            g.affine_select(out=tri, in_=tri, compare_op=ALU.is_gt, fill=0.0, base=0,
                            pattern=[[1, P]], channel_multiplier=-1).then_inc(S["iota"], 1)

            def root(t):
                pool.wait_ge(S["var_in"], t + NT + 1)
                g.tensor_tensor(stat[:, 8:9], stat[:, 9:10], stat[:, 10:11], ALU.pow).then_inc(S["rstd_in"], 1)

            def scatter(t, s, rows=P):
                pool.wait_ge(S["slots"], t + 1)
                pool.sem_inc(S["pool_held"], 1)
                for k in range(TOPK):
                    g.indirect_dma_start(xs_dram, bass.IndirectOffsetOnAxis(ap=slot_u[s][0:rows, k:k + 1], axis=0),
                                         tok[s][0:rows, :], None).then_inc(S["scattered"], 16)

            root(0)
            with pool.Fori(0, NT // 2) as i:
                for q in range(2):
                    root(i * 2 + (q + 1))
                    scatter(i * 2 + q, q)
            scatter(NT - 1, 0, LAST)
            pool.wait_ge(S["agg"], 2 * NT)
            g.iota(iota_j, [[1, NTAB]], base=0, channel_multiplier=0).then_inc(S["iota"], 1)
            pool.wait_ge(S["table"], 1)
            pool.wait_ge(S["padded"], 16 * (NE + 1))
            pairs = pool.value_load(npair_i[0:1, 0:1], min_val=MIN_PAIRS, max_val=(MAX_TILES + 1) // 2)
            with pool.Fori(0, pairs) as i:
                for h in range(2):
                    pool.wait_ge(S["ye_in"], i * 2 + h + 1)
                    pool.dma_start(ys_dram[bass.ds((i * 2 + h) * P, P), :], ye[h]).then_inc(ye_out[h], 16)
            for h in range(2):
                pool.wait_ge(ye_out[h], pairs * 16)
            def gather(t, s):
                pool.wait_ge(S["gix_in"], t + 1)
                pool.sem_inc(S["pool_held"], 1)
                for k in range(TOPK):
                    g.indirect_dma_start(yg[:, s * TOPK + k, :], None, ys_rows,
                                         bass.IndirectOffsetOnAxis(ap=gix[:, s, k:k + 1], axis=0)
                                         ).then_inc(yg_in[s], 16)

            gather(0, 0)
            with pool.Fori(0, NT // RING) as i:
                for q in range(RING):
                    gather(i * RING + (q + 1), (q + 1) % RING)

        def pair_onehots(dve, pair, slot):
            dve.wait_ge(S["counted"], pair * 2 - 2)
            pair_onehots_now(pair, slot)

        def pair_onehots_now(pair, slot):
            for h in range(2):
                for j in range(2):
                    w = pair * 2 + h
                    nc.vector.tensor_scalar(oh_src[0:JE, slot, 2 * h + j, :], iota_h[0:JE, 0:P],
                                            lo_t[0:JE, j, bass.ds(w, 1)], None, ALU.is_equal)
                    last = nc.vector.tensor_scalar(oh_key[0:JE, slot, 2 * h + j, :], iota_h[0:JE, :],
                                                   key_t[0:JE, j, bass.ds(w, 1)], None, ALU.is_equal)
                last.then_inc(S["onehot"], 1)

        def pair_counts(pe, pair, slot):
            for h in range(2):
                pe.wait_ge(S["onehot"], pair * 2 + h + 1)
                for j in range(2):
                    last = nc.tensor.matmul(counts_ps[:, 2 * slot + h, 0:KEYS], oh_src[0:JE, slot, 2 * h + j, :],
                                            oh_key[0:JE, slot, 2 * h + j, :], start=(j == 0), stop=(j == 1))
                last.then_inc(S["counted"], 1)

        def pair_keep(act, pair, slot):
            act.wait_ge(S["counted"], pair * 2 + 2)
            nc.scalar.activation(
                adj[:, :, bass.ds(pair * 2 * WD, 2 * WD)].rearrange("p b (h d) -> p b h d", h=2),
                counts_ps[:, 2 * slot:2 * slot + 2, 0:KEYS].rearrange("p h (b d) -> p b h d", d=WD),
                ACT.Copy).then_inc(S["adj_in"], 1)

        PER3 = 32
        FIRST_TAIL = NT * PAIRS_PER_TILE
        TAIL = (NPAIR - FIRST_TAIL) // 2
        assert NPAIR == FIRST_TAIL + 2 * TAIL

        @block.vector
        def _(dve):
            v = nc.vector
            count = [0]
            base = [0]

            def link(ins):
                count[0] += 1
                ins.then_inc(chain, 1)
                dve.wait_ge(chain, base[0] + count[0])

            v.memset(ident[:, :], 0.0).then_inc(S["consts"], 1)
            v.memset(ones[:, :], 1.0).then_inc(S["consts"], 1)
            v.memset(stat[:, 10:11], -0.5)
            v.memset(flag[:, :], 0.0)
            dve.wait_ge(S["edges_in"], 32)
            v.tensor_copy(dchunk_f, dchunk)
            link(v.tensor_copy(dnext_f[0:NCH - 1, 0:1], dnext[0:NCH - 1, 0:1]))
            dve.wait_ge(S["iota"], 3)
            v.tensor_scalar(below, wstart, dchunk_f[:, 0:1], None, ALU.is_gt).then_inc(S["first_ge"], 1)
            v.tensor_copy(wlo[:, 0:NG], wlo_i[:, 0:NG])
            v.tensor_tensor(flag[0:NCH - 1, 1:2], dchunk_f[0:NCH - 1, CHUNK - 1:CHUNK], dnext_f[0:NCH - 1, 0:1],
                            ALU.is_gt)
            link(v.tensor_tensor(falls[:, 0:CHUNK - 1], dchunk_f[:, 0:CHUNK - 1], dchunk_f[:, 1:CHUNK], ALU.is_gt))
            v.tensor_reduce(flag[0:NCH, 0:1], falls[:, 0:CHUNK - 1], AX.X, ALU.max)
            dve.wait_ge(S["firsts"], 1)
            link(v.tensor_scalar(row_f, bank[2][0:WPG, 0:NG], -1.0, 0.0, ALU.add, ALU.max))
            v.tensor_copy(row_u, row_f).then_inc(S["chunk_ix"], 1)
            dve.wait_ge(S["w_in"], 96)
            v.tensor_tensor(b1sq, b1b[:, :], b1b[:, :], ALU.mult)
            for q, a in zip(wsq, (w[:, :, :], w2_early)):
                v.tensor_tensor(q, a, a, ALU.mult).then_inc(S["wsq"], 1)
            dve.wait_ge(S["chunk_in"], 16 * NG)
            for k in range(NG):
                ins = v.tensor_scalar(cless[:, k, :], crow[:, k, :], wlo[:, k:k + 1], None, ALU.is_lt)
            link(ins)
            link(v.tensor_reduce(cnt_f, cless, AX.X, ALU.add))
            link(v.scalar_tensor_tensor(start_f, row_f, float(CHUNK), cnt_f, ALU.mult, ALU.add))
            link(v.tensor_scalar(start_f, start_f, float(E - RUN), None, ALU.min))
            v.tensor_copy(start_u, start_f).then_inc(S["start_ix"], 1)
            dve.wait_ge(S["wnorm"], 2)
            v.tensor_reduce(scl[:, 0:1], bank[3][:, 0:D], AX.X, ALU.max)
            v.tensor_reduce(scl[:, 1:3], bank[3][:, :].rearrange("p (s n) -> p s n", s=2), AX.X, ALU.add)
            v.tensor_reduce(scl[:, 3:4], bank[1][:, 0:D], AX.X, ALU.max)
            v.tensor_reduce(scl[:, 4:5], b1sq, AX.X, ALU.add).then_inc(S["wsum"], 1)
            dve.wait_ge(S["wroot"], 1)
            root = scl[:, 8:13]
            link(v.tensor_scalar(scl[:, 5:6], root[:, 1:2], root[:, 2:3], float(D) ** 0.5, ALU.add, ALU.mult))
            link(v.tensor_scalar(scl[:, 5:6], scl[:, 5:6], root[:, 4:5], root[:, 3:4], ALU.add, ALU.mult))
            link(v.tensor_scalar(scl[:, 4:5], root[:, 0:1], float(D) ** 0.5, None, ALU.mult))
            link(v.tensor_scalar(scl[:, 4:6], scl[:, 4:6], 1e-30, None, ALU.max))
            link(v.tensor_scalar(scl_i[:, 0:2], scl[:, 4:6].bitcast(I32), EXPONENT_AT, None, ALU.logical_shift_right))
            link(v.tensor_scalar(scl_i[:, 2:4], scl_i[:, 0:2], -1.0, 268.0, ALU.mult, ALU.add))
            link(v.tensor_scalar(scl_i[:, 4:6], scl_i[:, 2:4], -1.0, 254.0, ALU.mult, ALU.add))
            v.tensor_scalar(scl_i[:, 8:10], scl_i[:, 2:4], EXPONENT_AT, None, ALU.logical_shift_left)
            link(v.tensor_scalar(scl_i[:, 10:12], scl_i[:, 4:6], EXPONENT_AT, None, ALU.logical_shift_left))
            dve.wait_ge(S["run_in"], 32 * NG)
            for k in range(NG):
                v.tensor_scalar(rel[:, k, :], run_d[:, k, :], wlo[:, k:k + 1], None, ALU.subtract)
            v.tensor_scalar(blk_i, run_s, P.bit_length() - 1, None, ALU.logical_shift_right)
            link(v.tensor_scalar(lo_i, run_s, P - 1, None, ALU.bitwise_and))
            v.tensor_scalar(inside, rel, 0.0, None, ALU.is_ge)
            v.tensor_scalar(lo1, lo_i, 1.0, None, ALU.add)
            link(v.scalar_tensor_tensor(key_f, blk_i, float(WD), rel, ALU.mult, ALU.add))
            link(v.scalar_tensor_tensor(valid, rel, float(WD), inside, ALU.is_lt, ALU.mult))
            v.scalar_tensor_tensor(key1, key_f, 1.0, valid, ALU.add, ALU.mult).then_inc(S["keys"], 1)
            link(v.tensor_scalar(not_end, start_f, float(E - RUN), None, ALU.is_lt))
            v.scalar_tensor_tensor(flag[0:WPG, 2:2 + NG], rel[:, :, RUN - 1:RUN].rearrange("p g a -> p (g a)"), float(WD),
                                   not_end, ALU.is_lt, ALU.mult).then_inc(S["flag_in"], 1)
            v.memset(y[:, :, 2 * D:2 * D + 1], 1.0)
            dve.wait_ge(S["keys_tr"], 1)
            v.memset(adj[:, :, NW * WD:AC], 0.0)
            v.tensor_copy(key_t[0:JE, :, :], counts_ps[0:JE, 0:2, 0:NW])
            link(v.tensor_copy(lo_t[0:JE, :, :], counts_ps[0:JE, 2:4, 0:NW]))
            v.memset(stat[:, 11:12], 0.0).then_inc(S["scaled"], 1)

            def stats(t):
                dve.wait_ge(S["x_in"], 16 * (t + 1))
                link(v.bn_stats(stat[:, 0:6], xt[:, :]))
                dve.sem_inc(S["held"], 1)
                link(v.bn_aggr(stat[:, 6:8], stat[:, 0:6]))
                v.tensor_scalar(stat[:, 9:10], stat[:, 7:8], EPS, None, ALU.add).then_inc(S["var_in"], 1)

            def normalise(t, read):
                dve.wait_ge(S["rstd_in"], t + 1)
                if read:
                    dve.wait_ge(S["nrm_tr"], t)
                v.tensor_scalar(nrm[:, :], xt[:, :], stat[:, 6:7], stat[:, 8:9], ALU.subtract, ALU.mult
                                ).then_inc(S["normed"], 1)

            def split_y(t, out_, bias, scale):
                dve.wait_ge(S["hi_in"], t + 1)
                v.scalar_tensor_tensor(out_[0], bank[1][:, 0:D], scale, out_[1], ALU.mult, ALU.subtract)
                v.tensor_tensor(zt[:, :], bank[1][:, D:2 * D], bias, ALU.add).then_inc(S["yz_in"], 1)

            def yrow(t):
                return (y[:, bass.ds(t, 1), 0:D].rearrange("p a n -> p (a n)"),
                        y[:, bass.ds(t, 1), D:2 * D].rearrange("p a n -> p (a n)"))

            s1 = scl_i[:, 8:9].bitcast(F32)
            s2 = scl_i[:, 9:10].bitcast(F32)
            i1 = scl_i[:, 10:11].bitcast(F32)
            i2 = scl_i[:, 11:12].bitcast(F32)

            def phase1(t, first=False, pairs=PAIRS_PER_TILE):
                stats(t)
                for q in range(pairs):
                    pair = t * PAIRS_PER_TILE + q
                    if first and q < 2:
                        pair_onehots_now(pair, q % 2)
                    else:
                        pair_onehots(dve, pair, q % 2)
                    if q == 0:
                        normalise(t, not first)
                if not first:
                    dve.wait_ge(S["z_out"], 16 * t)
                split_y(t, yrow(t), b1b[:, :], s1)

            phase1(0, True)
            per = 2
            with dve.Fori(1, NT - 1) as t:
                start = count[0]
                base[0] = (t - 1) * per
                phase1(t)
                assert count[0] - start == per
            base[0] = 0
            count[0] += per * (NT - 3)
            dve.wait_ge(S["nrm_tr"], NT - 1)
            link(v.memset(xt[:, :], 0.0))
            v.memset(stat[:, 11:12], 0.0).then_inc(S["pad_ok"], 1)
            phase1(NT - 1)
            with dve.Fori(0, TAIL) as i:
                for q in range(2):
                    pair_onehots(dve, i * 2 + (FIRST_TAIL + q), q)

            dve.wait_ge(S["flag_all"], 1)
            link(v.tensor_reduce(flag_all[:, 5:6], flag_all[:, 0:5], AX.X, ALU.max))
            v.tensor_copy(flag_i[:, 0:1], flag_all[:, 5:6]).then_inc(S["flag_out"], 1)
            dve.wait_ge(S["flag_out"], 1)
            with dve.If(dve.value_load(flag_i[0:1, 0:1], min_val=0, max_val=1) == 1):
                n = [0]

                def then(ins, at=0):
                    n[0] += 1
                    ins.then_inc(S["all_keys"], 1)
                    dve.wait_ge(S["all_keys"], at + n[0])

                dve.wait_ge(S["projected"], NT)
                dve.wait_ge(S["z_out"], 16 * NT)
                dve.wait_ge(S["counted"], NW)
                dve.wait_ge(S["all_in"], 16)
                then(v.memset(zero_h, 0.0))
                then(v.memset(window_at, 0.0))
                v.tensor_copy(edge_dst, edge_i).then_inc(S["all_free"], 1)
                dve.wait_ge(S["all_in"], 32)
                then(v.tensor_scalar(edge_rel.bitcast(I32), edge_i, P - 1, None, ALU.bitwise_and))
                then(v.tensor_scalar(edge_key.bitcast(I32), edge_i, P.bit_length() - 1, None, ALU.logical_shift_right))
                then(v.tensor_scalar(edge_lo, edge_rel.bitcast(I32), 1.0, None, ALU.add))
                then(v.tensor_scalar(edge_blk, edge_key.bitcast(I32), float(WD), 1.0, ALU.mult, ALU.add))
                with dve.Fori(0, NW) as wi:
                    at, before = wi * 5, n[0]
                    then(v.tensor_scalar(edge_rel, edge_dst, window_at, None, ALU.subtract), at)
                    dve.wait_ge(S["all_counted"], wi * STEPS + 2)
                    then(v.tensor_tensor(edge_key, edge_blk, edge_rel, ALU.add), at)
                    then(v.scalar_tensor_tensor(edge_key, edge_rel, 0.0, edge_key, ALU.is_ge, ALU.mult), at)
                    then(v.scalar_tensor_tensor(edge_key, edge_rel, float(WD), edge_key, ALU.is_lt, ALU.mult), at)
                    then(v.tensor_scalar(window_at, window_at, float(WD), None, ALU.add), at)
                    assert n[0] - before == 5
                    n[0] = before
                    dve.sem_inc(S["held"], 1)
                    with dve.Fori(0, STEPS // 2) as i:
                        for q in range(2):
                            dve.wait_ge(S["all_counted"], wi * STEPS + i * 2 + (q + 1))
                            for c in range(STEP):
                                col = (i * 2 + q) * STEP + c
                                v.tensor_scalar(oh_src[0:NCH, q, c, :], iota_h[0:NCH, 0:P],
                                                edge_lo[:, bass.ds(col, 1)], None, ALU.is_equal)
                                last = v.tensor_scalar(oh_key[0:NCH, q, c, :], iota_h[0:NCH, :],
                                                       edge_key[:, bass.ds(col, 1)], None, ALU.is_equal)
                            last.then_inc(S["all_onehot"], 1)

            def phase2(t, first=False):
                dve.wait_ge(S["agg"], t + 1)
                link(v.tensor_scalar(stat[:, 9:10], counts_ps[:, 0, D:D + 1], 1.0, None, ALU.max))
                link(v.reciprocal(stat[:, 8:9], stat[:, 9:10]))
                v.tensor_copy(rdeg[:, bass.ds(t, 1)], stat[:, 8:9])
                link(v.tensor_tensor(stat[:, 11:12], stat[:, 8:9], i1, ALU.mult))
                dve.wait_ge(S["z_in"], 16 * (t + 1))
                dve.wait_ge(S["nrm_tr"], t + NT)
                v.scalar_tensor_tensor(nrm[:, :], counts_ps[:, 0, 0:D], stat[:, 11:12], zi[:, :], ALU.mult, ALU.add
                                       ).then_inc(S["h_in"], 1)

            def phase2_split(t, first=False):
                if first:
                    dve.wait_ge(S["z_out"], 16 * NT)
                else:
                    dve.wait_ge(S["y2_out"], 32 * t)
                split_y(t + NT, (yo[:, 0:D], yo[:, D:2 * D]), b2b[:, :], s2)

            phase2(0)
            phase2(1)
            phase2_split(0, True)
            per = 3
            with dve.Fori(2, NT) as t:
                start = count[0]
                base[0] = (t - 2) * per
                phase2(t)
                phase2_split(t - 1)
                assert count[0] - start == per
            base[0] = 0
            count[0] += per * (NT - 3)
            phase2_split(NT - 1)

            dve.wait_ge(S["counted"], NW)
            v.memset(tri, 1.0).then_inc(S["tri_in"], 1)
            dve.wait_ge(S["iota"], 5)
            link(v.tensor_copy(iota_e, iota_ei))
            link(v.tensor_scalar(base_e, iota_e, float(REGION), None, ALU.mult))
            link(v.tensor_scalar(rdeg[:, :], rdeg[:, :], i2, None, ALU.mult))

            def x2_and_norm(t, s, first=False, alone=False):
                dve.wait_ge(S["agg"], t + 1 + NT)
                dve.wait_ge(S["z_in"], 16 * (t + 1 + NT))
                dve.wait_ge(S["x_in"], 16 * (t + 1 + NT))
                link(v.scalar_tensor_tensor(zt[:, :], counts_ps[:, s, 0:D], rdeg[:, bass.ds(t, 1)], zi[:, :],
                                            ALU.mult, ALU.add))
                last = v.tensor_tensor(zt[:, :], zt[:, :], xt[:, :], ALU.add)
                last.then_inc(S["x2_in"], 1)
                dve.wait_ge(S["x2_in"], t + 1)
                link(v.bn_stats(stat[:, 0:6], zt[:, :]))
                dve.sem_inc(S["held"], 1)
                link(v.bn_aggr(stat[:, 6:8], stat[:, 0:6]))
                v.tensor_scalar(stat[:, 9:10], stat[:, 7:8], EPS, None, ALU.add).then_inc(S["var_in"], 1)
                dve.wait_ge(S["rstd_in"], t + 1 + NT)
                if not first:
                    dve.wait_ge(S["scattered"], t * 16 * TOPK - 16 * TOPK)
                v.tensor_scalar(tok[s], zt[:, :], stat[:, 6:7], stat[:, 8:9], ALU.subtract, ALU.mult
                                ).then_inc(S["normed"], 1)
                dve.wait_ge(S["normed"], t + 1 + NT)
                if not alone:
                    dve.wait_ge(S["u_out"], t * 16)
                v.tensor_tensor(uo, zt[:, :], tok[s], ALU.add).then_inc(S["u_ready"], 1)

            def choose(t, first=False, rows=P):
                dve.wait_ge(S["logits"], t + 1)
                link(v.tensor_copy(lg, bank[1][:, 0:NE]))
                dve.sem_inc(S["held"], 1)
                link(v.max(mx, lg))
                v.tensor_scalar(neg, mx[:, 0:1], -1.0, None, ALU.mult).then_inc(S["top"], 1)
                v.max_index(mix, mx, lg)
                link(v.memset(stat[:, 13:14], 0.0))
                link(v.tensor_copy(pick, mix[:, 0:TOPK]))
                for k in range(TOPK):
                    last = v.tensor_scalar(mask[:, k, :], iota_e, pick[:, k:k + 1], None, ALU.is_equal)
                link(last)
                v.tensor_tensor(both, mask[:, 0, :], mask[:, 1, :], ALU.add).then_inc(S["masks"], 1)
                dve.wait_ge(S["expd"], t + 1)
                link(v.reciprocal(esum[:, 1:2], esum[:, 0:1]))
                link(v.tensor_scalar(prob[:, 0:TOPK], ex[:, 0:TOPK], esum[:, 1:2], None, ALU.mult))
                link(v.tensor_tensor(prob[:, TOPK:TOPK + 1], prob[:, 0:1], prob[:, 1:2], ALU.add))
                link(v.tensor_scalar(prob[:, TOPK:TOPK + 1], prob[:, TOPK:TOPK + 1], 1e-12, None, ALU.max))
                link(v.reciprocal(prob[:, TOPK + 1:TOPK + 2], prob[:, TOPK:TOPK + 1]))
                v.tensor_scalar(coef[:, bass.ds(t, 1), :].rearrange("p a k -> p (a k)"), prob[:, 0:TOPK],
                                prob[:, TOPK + 1:TOPK + 2], None, ALU.mult)

            def place(t, s, first=False):
                dve.wait_ge(S["prefix"], t + 1)
                link(v.tensor_tensor(pos, base_e, bank[3][:, 0:NE], ALU.add))
                v.tensor_tensor(base_e, base_e, bank[3][:, NE:2 * NE], ALU.add)
                for k in range(TOPK):
                    last = v.tensor_tensor(posm[:, k, :], mask[:, k, :], pos, ALU.mult)
                link(last)
                link(v.tensor_reduce(slot_f, posm, AX.X, ALU.add))
                v.tensor_copy(slots[:, bass.ds(t, 1), :].rearrange("p a k -> p (a k)"), slot_f)
                if not first:
                    dve.wait_ge(S["scattered"], t * 16 * TOPK - 16 * TOPK)
                v.tensor_copy(slot_u[s], slot_f).then_inc(S["slots"], 1)

            x2_and_norm(0, 0, True, True)
            choose(0)
            x2_and_norm(1, 1, True)
            place(0, 0, True)
            choose(1)
            x2_and_norm(2, 0)
            place(1, 1, True)
            choose(2)
            with dve.Fori(1, NT // 2) as i:
                start = count[0]
                base[0] = (i - 1) * PER3
                for q in range(2):
                    x2_and_norm(i * 2 + (q + 1), (q + 1) % 2)
                    place(i * 2 + q, q % 2)
                    choose(i * 2 + (q + 1))
                assert count[0] - start == PER3, count[0] - start
            base[0] = 0
            count[0] += PER3 * (NT // 2 - 2)
            place(NT - 1, 0)
            dve.wait_ge(S["agg"], 2 * NT)
            v.memset(zero_t, 0.0).then_inc(S["zeros"], 1)
            link(v.tensor_copy(end_i, base_e))
            link(v.scalar_tensor_tensor(cnt, iota_e, -float(REGION), base_e, ALU.mult, ALU.add))
            link(v.tensor_scalar(nt_i, cnt, float(P - 1), None, ALU.add))
            link(v.tensor_scalar(nt_i, nt_i, P.bit_length() - 1, None, ALU.logical_shift_right))
            link(v.tensor_copy(cum[0], nt_i))
            for n, d in enumerate((1, 2, 4)):
                v.tensor_copy(cum[n + 1][:, 0:d], cum[n][:, 0:d])
                link(v.tensor_tensor(cum[n + 1][:, d:NE], cum[n][:, d:NE], cum[n][:, 0:NE - d], ALU.add))
            total = cum[3][:, NE - 1:NE]
            link(v.tensor_scalar(first_row[:, 1:NE], cum[3][:, 0:NE - 1], -float(P), None, ALU.mult))
            link(v.memset(first_row[:, 0:1], 0.0))
            link(v.scalar_tensor_tensor(first_row, iota_e, float(REGION), first_row, ALU.mult, ALU.add))
            link(v.tensor_tensor(jump[:, 0:NE - 1], first_row[:, 1:NE], first_row[:, 0:NE - 1], ALU.subtract))
            dve.wait_ge(S["iota"], 7)
            link(v.tensor_copy(jf, iota_j))
            link(v.tensor_scalar(tab_r, jf, float(P), None, ALU.mult))
            link(v.memset(tab_e, 0.0))
            for e in range(NE - 1):
                v.tensor_scalar(past, jf, cum[3][:, e:e + 1], None, ALU.is_ge)
                link(v.tensor_scalar(stay, jf, cum[3][:, e:e + 1], jump[:, e:e + 1], ALU.is_ge, ALU.mult))
                v.tensor_tensor(tab_e, tab_e, past, ALU.add)
                link(v.tensor_tensor(tab_r, tab_r, stay, ALU.add))
            link(v.tensor_scalar(stay, jf, total, None, ALU.is_lt))
            v.tensor_scalar(past, jf, total, None, ALU.is_ge)
            link(v.tensor_copy(cnt[:, 0:1], tab_e[:, 0:1]))
            link(v.tensor_copy(cnt[:, 1:2], tab_r[:, 0:1]))
            v.tensor_tensor(tab_e, tab_e, stay, ALU.mult)
            link(v.tensor_tensor(tab_r, tab_r, stay, ALU.mult))
            v.scalar_tensor_tensor(tab_ei, past, cnt[:, 0:1], tab_e, ALU.mult, ALU.add)
            link(v.scalar_tensor_tensor(tab_ri, past, cnt[:, 1:2], tab_r, ALU.mult, ALU.add))
            v.tensor_scalar(ends_i[:, 0:1], total, float(P), None, ALU.mult)
            link(v.tensor_scalar(npair_i[:, 1:2], total, 1.0, None, ALU.add))
            v.tensor_scalar(npair_i[:, 0:1], npair_i[:, 1:2], 1, None, ALU.logical_shift_right).then_inc(S["table"], 1)

            link(v.tensor_copy(slots_f, slots.rearrange("p t k -> p (t k)")))
            for e in range(1, NE):
                link(v.tensor_scalar(moved, slots_f, float(e * REGION), jump[:, e - 1:e], ALU.is_ge, ALU.mult))
                if e == 1:
                    kept = slots_f
                link(v.tensor_tensor(place_f[e % 2], kept, moved, ALU.subtract))
                kept = place_f[e % 2]
            v.tensor_copy(slots_y.rearrange("p t k -> p (t k)"), kept)

            dve.wait_ge(S["ew_in"], 16 * (2 * NE + 2))
            dve.wait_ge(S["table"], 1)
            pairs = dve.value_load(npair_i[0:1, 0:1], min_val=MIN_PAIRS, max_val=(MAX_TILES + 1) // 2)

            def pair_of_tiles(i, first=False):
                es = [dve.value_load(tab_ei[0:1, bass.ds(i * 2 + h, 1)], min_val=0, max_val=NE - 1) for h in range(2)]
                for h in range(2):
                    dve.wait_ge(S["hid"], i * 2 + h + 1)
                    v.tensor_tensor(hb[h], counts_ps[:, 2 + h, 0:D],
                                    eb1_sb[:, bass.ds(es[h], 1), :].rearrange("p a n -> p (a n)"), ALU.add
                                    ).then_inc(S["hb_in"], 1)
                for h in range(2):
                    dve.wait_ge(S["ye_ps"], i * 2 + h + 1)
                    if not first:
                        dve.wait_ge(ye_out[h], i * 16)
                    v.tensor_tensor(ye[h], bank[2 + h][:, 0:D],
                                    eb2_sb[:, bass.ds(es[h], 1), :].rearrange("p a n -> p (a n)"), ALU.add
                                    ).then_inc(S["ye_in"], 1)

            pair_of_tiles(0, True)
            with dve.Fori(1, pairs) as i:
                pair_of_tiles(i)

            def indices(t, s):
                link(v.tensor_copy(gix[:, s, :], slots_y[:, bass.ds(t, 1), :].rearrange("p a k -> p (a k)")))
                v.memset(stat[:, 14:15], 0.0).then_inc(S["gix_in"], 1)

            def combine(t, s, turn, more=True, first=False):
                dve.wait_ge(yg_in[s], turn * (16 * TOPK) + 16 * TOPK)
                dve.wait_ge(ug_in[s], turn * 16 + 16)
                if not first:
                    dve.wait_ge(sum_out_of[s], turn * 16)
                for k in range(TOPK):
                    ins = v.scalar_tensor_tensor(og[:, s, :], yg[:, s * TOPK + k, :],
                                                 coef[:, bass.ds(t, 1), k:k + 1].rearrange("p a k -> p (a k)"),
                                                 ug[:, s, :] if k == 0 else og[:, s, :], ALU.mult, ALU.add)
                    if k == 0:
                        link(ins)
                ins.then_inc(S["og_in"], 1)
                if more:
                    indices(t + RING, s)

            for t in range(RING):
                indices(t, t)
            for t in range(RING):
                combine(t, t, 0, True, True)
            combine(RING, 0, 1)
            with dve.Fori(1, NT // RING - 1) as i:
                start = count[0]
                base[0] = (i - 1) * (2 * RING)
                for q in range(RING):
                    combine(i * RING + (q + 1), (q + 1) % RING, i + (q + 1) // RING)
                assert count[0] - start == 2 * RING
            base[0] = 0
            count[0] += 2 * RING * (NT // RING - 3)
            for t in range(NT - RING, NT):
                combine(t, t % RING, t // RING, False)

        @block.tensor
        def _(pe):
            te = nc.tensor
            pe.wait_ge(S["consts"], 2)
            pe.wait_ge(S["first_ge"], 1)
            for k in range(NG):
                last = te.matmul(bank[2][0:WPG, k:k + 1], below[:, k * WPG:(k + 1) * WPG], ones[0:NCH, 0:1],
                                 start=True, stop=True)
            last.then_inc(S["firsts"], 1)
            pe.wait_ge(S["wsq"], 2)
            for q, b in zip(wsq, (bank[3], bank[1])):
                for k in range(KD):
                    last = te.matmul(b[:, :], ones[:, :], q[:, k, :], start=(k == 0), stop=(k == KD - 1))
                last.then_inc(S["wnorm"], 1)
            pe.wait_ge(S["keys"], 1)
            pe.wait_ge(S["iota"], 4)
            for k in range(NG):
                for j in range(2):
                    for n, a in ((j, key1), (2 + j, lo1)):
                        last = te.transpose(counts_ps[0:JE, n, k * WPG:(k + 1) * WPG], a[:, k, j * JE:(j + 1) * JE],
                                            ident[0:WPG, 0:WPG])
            last.then_inc(S["keys_tr"], 1)

            def transposes(t):
                for k in range(KD):
                    last = te.transpose(bank[0][:, k * P:(k + 1) * P], nrm[:, k * P:(k + 1) * P], ident[:, :])
                last.then_inc(S["nrm_tr"], 1)

            def project(t):
                pe.wait_ge(S["nrm_t_in"], t + 1)
                pe.wait_ge(S["yz_in"], t)
                for k in range(KD):
                    last = te.matmul(bank[1][:, :], nrm_t[:, k * P:(k + 1) * P], w[:, k, :],
                                     start=(k == 0), stop=(k == KD - 1))
                last.then_inc(S["projected"], 1)

            def counts(pair, slot, fresh):
                if fresh:
                    pe.wait_ge(S["scaled"], 1)
                else:
                    pe.wait_ge(S["adj_in"], pair - 1)
                pair_counts(pe, pair, slot)

            def phase1(t, first=False):
                for q in range(PAIRS_PER_TILE):
                    counts(t * PAIRS_PER_TILE + q, q % 2, first and q < 2)
                    if q == 1:
                        pe.wait_ge(S["normed"], t + 1)
                        if not first:
                            pe.wait_ge(S["nrm_t_in"], t)
                        transposes(t)
                    if q == 2:
                        if first:
                            pe.wait_ge(S["nrm_t_in"], 1)
                            for k in range(KD):
                                last = te.matmul(bank[1][:, :], nrm_t[:, k * P:(k + 1) * P], w[:, k, :],
                                                 start=(k == 0), stop=(k == KD - 1))
                            last.then_inc(S["projected"], 1)
                        else:
                            project(t)

            phase1(0, True)
            with pe.Fori(1, NT) as t:
                phase1(t)
            with pe.Fori(0, TAIL) as i:
                for q in range(2):
                    counts(i * 2 + (FIRST_TAIL + q), q, False)

            def aggregate(t, mid, cols):
                for b in range(NT):
                    if mid is not None and b == NT // 3:
                        mid()
                    a = adj[:, b, bass.ds(t * P, P)]
                    te.matmul(counts_ps[:, 0, 0:cols], a, y[:, b, D:D + cols], start=(b == 0), stop=False)
                    last = te.matmul(counts_ps[:, 0, 0:D], a, y[:, b, 0:D], start=False, stop=(b == NT - 1))
                last.then_inc(S["agg"], 1)

            def phase2(t, first=False):
                if not first:
                    pe.wait_ge(S["h_in"], t)

                def mid():
                    pe.wait_ge(S["nrm_t_in"], t + NT - 1)
                    transposes(t + NT - 1)
                aggregate(t, None if first else mid, D + 1)
                if not first:
                    project(t + NT - 1)

            pe.wait_ge(S["flag_out"], 1)
            with pe.If(pe.value_load(flag_i[0:1, 0:1], min_val=0, max_val=1) == 1):
                pe.wait_ge(S["adj_in"], NPAIR)
                pe.sem_inc(S["all_counted"], 2)
                with pe.Fori(0, NW) as wi:
                    pe.wait_ge(S["all_kept"], wi + 1)
                    pe.wait_ge(S["all_onehot"], wi * STEPS + 1)
                    te.matmul(counts_ps[:, 0, 0:KEYS], zero_h, iota_h[0:NCH, :], start=True, stop=False)
                    with pe.Fori(0, STEPS // 2) as i:
                        for q in range(2):
                            pe.wait_ge(S["all_onehot"], wi * STEPS + i * 2 + (q + 1))
                            for c in range(STEP):
                                last = te.matmul(counts_ps[:, 0, 0:KEYS], oh_src[0:NCH, q, c, :],
                                                 oh_key[0:NCH, q, c, :], start=False, stop=False)
                            last.then_inc(S["all_counted"], 1)
                    te.matmul(counts_ps[:, 0, 0:KEYS], zero_h, iota_h[0:NCH, :], start=False, stop=True
                              ).then_inc(S["all_window"], 1)
                pe.wait_ge(S["all_kept"], NW + 1)
            pe.wait_ge(S["w_in"], 128)
            pe.wait_ge(S["adj_in"], NPAIR)
            pe.wait_ge(S["yz_in"], NT)
            phase2(0, True)
            with pe.Fori(1, NT) as t:
                phase2(t)
            pe.wait_ge(S["h_in"], NT)
            pe.wait_ge(S["nrm_t_in"], 2 * NT - 1)
            transposes(2 * NT - 1)
            project(2 * NT - 1)

            def route(t, s, step, rows=P):
                if step == 0:
                    pe.wait_ge(S["normed"], t + 1 + NT)
                    pe.wait_ge(S["nrm_t_in"], t + 2 * NT)
                    for k in range(KD):
                        last = te.transpose(bank[0][:, k * P:(k + 1) * P], tok[s][:, k * P:(k + 1) * P], ident[:, :])
                    last.then_inc(S["nrm_tr"], 1)
                if step == 1:
                    pe.wait_ge(S["nrm_t_in"], t + 1 + 2 * NT)
                    for k in range(KD):
                        last = te.matmul(bank[1][:, 0:NE], nrm_t[:, k * P:(k + 1) * P], rw_t[:, k, :],
                                         start=(k == 0), stop=(k == KD - 1))
                    last.then_inc(S["logits"], 1)
                if step == 2:
                    pe.wait_ge(S["masks"], t + 1)
                    te.matmul(bank[3][:, 0:NE], tri[0:rows, :], both[0:rows, :], start=True, stop=True)
                    te.matmul(bank[3][:, NE:2 * NE], ones[0:rows, :], both[0:rows, :], start=True, stop=True
                              ).then_inc(S["prefix"], 1)

            def phase3(t, s, first=False, route_last=True):
                if not first:
                    pe.wait_ge(S["x2_in"], t - 1)
                for b in range(NT):
                    if first and b % (NT // NQ) == 0:
                        pe.wait_ge(y2_in[b // (NT // NQ)], 16)
                    if route_last and b == NT // 2:
                        route(t - 1, 1 - s, 0)
                    if route_last and b == NT // 4 * 3:
                        route(t - 1, 1 - s, 1)
                    a = adj[:, b, bass.ds(t * P, P)]
                    te.matmul(counts_ps[:, s, 0:D], a, y[:, b, D:2 * D], start=(b == 0), stop=False)
                    last = te.matmul(counts_ps[:, s, 0:D], a, y[:, b, 0:D], start=False, stop=(b == NT - 1))
                last.then_inc(S["agg"], 1)
                if route_last:
                    route(t - 1, 1 - s, 2)

            phase3(0, 0, True, False)
            pe.wait_ge(S["rw_in"], 16 * KD)
            pe.wait_ge(S["iota"], 6)
            phase3(1, 1, True)
            phase3(2, 0)
            with pe.Fori(1, NT // 2) as i:
                for q in range(2):
                    phase3(i * 2 + (q + 1), (q + 1) % 2)
            for step in range(3):
                route(NT - 1, 0, step, LAST if step == 2 else P)

            def turn_rows(i):
                for h in range(2):
                    pe.wait_ge(xe_in[h], i * 16 + 16)
                    for k in range(KD):
                        last = te.transpose(counts_ps[:, h, k * P:(k + 1) * P], xe[h][:, k * P:(k + 1) * P], ident[:, :])
                last.then_inc(S["xe_tr"], 1)

            pe.wait_ge(S["table"], 1)
            pairs = pe.value_load(npair_i[0:1, 0:1], min_val=MIN_PAIRS, max_val=(MAX_TILES + 1) // 2)
            turn_rows(0)
            pe.wait_ge(S["ew_in"], 16 * (2 * NE + 2))
            with pe.Fori(0, pairs) as i:
                es = [pe.value_load(tab_ei[0:1, bass.ds(i * 2 + h, 1)], min_val=0, max_val=NE - 1) for h in range(2)]
                for h in range(2):
                    pe.wait_ge(S["xe_t_in"], i * 2 + h + 1)
                    for k in range(KD):
                        last = te.matmul(counts_ps[:, 2 + h, 0:D], xe_t[h][:, k * P:(k + 1) * P],
                                         ew1_sb[:, bass.ds(es[h], 1), k, :].rearrange("p a n -> p (a n)"),
                                         start=(k == 0), stop=(k == KD - 1))
                    last.then_inc(S["hid"], 1)
                turn_rows(i + 1)
                for h in range(2):
                    pe.wait_ge(S["ge_in"], i * 2 + h + 1)
                    for k in range(KD):
                        last = te.transpose(bank[h][:, k * P:(k + 1) * P], ge[h][:, k * P:(k + 1) * P], ident[:, :])
                    last.then_inc(S["ge_tr"], 1)
                for h in range(2):
                    pe.wait_ge(S["ge_t_in"], i * 2 + h + 1)
                    for k in range(KD):
                        last = te.matmul(bank[2 + h][:, 0:D], ge_t[h][:, k * P:(k + 1) * P],
                                         ew2_sb[:, bass.ds(es[h], 1), k, :].rearrange("p a n -> p (a n)"),
                                         start=(k == 0), stop=(k == KD - 1))
                    last.then_inc(S["ye_ps"], 1)

        @block.scalar
        def _(act):
            a = nc.scalar
            act.wait_ge(S["wsum"], 1)
            a.activation(scl[:, 8:13], scl[:, 0:5], ACT.Sqrt).then_inc(S["wroot"], 1)
            act.wait_ge(S["scaled"], 1)

            def turn(t, func):
                act.wait_ge(S["nrm_tr"], t + 1)
                act.wait_ge(S["projected"], t)
                a.activation(nrm_t[:, :], bank[0][:, 0:D], func).then_inc(S["nrm_t_in"], 1)

            def high(t, to, scale):
                act.wait_ge(S["projected"], t + 1)
                a.activation(to, bank[1][:, 0:D], ACT.Copy, scale=scale).then_inc(S["hi_in"], 1)

            def phase1(t, first=False):
                for q in range(PAIRS_PER_TILE):
                    pair_keep(act, t * PAIRS_PER_TILE + q, q % 2)
                    if q == 1:
                        if first:
                            act.wait_ge(S["nrm_tr"], 1)
                            a.activation(nrm_t[:, :], bank[0][:, 0:D], ACT.Copy).then_inc(S["nrm_t_in"], 1)
                        else:
                            turn(t, ACT.Copy)
                    if q == 2:
                        high(t, y[:, bass.ds(t, 1), D:2 * D].rearrange("p a n -> p (a n)"),
                             scl_i[:, 8:9].bitcast(F32))

            phase1(0, True)
            with act.Fori(1, NT) as t:
                phase1(t)
            with act.Fori(0, TAIL) as i:
                for q in range(2):
                    pair_keep(act, i * 2 + (FIRST_TAIL + q), q)

            act.wait_ge(S["flag_out"], 1)
            with act.If(act.value_load(flag_i[0:1, 0:1], min_val=0, max_val=1) == 1):
                act.sem_inc(S["all_kept"], 1)
                with act.Fori(0, NW) as wi:
                    act.wait_ge(S["all_window"], wi + 1)
                    a.activation(adj[:, :, bass.ds(wi * WD, WD)],
                                 counts_ps[:, 0, 0:KEYS].rearrange("p (b d) -> p b d", d=WD), ACT.Copy
                                 ).then_inc(S["all_kept"], 1)
                act.wait_ge(S["all_kept"], NW + 1)
                act.sem_inc(S["all_done"], 1)

            def phase2(t, first=False):
                turn(t + NT, ACT.Relu)
                if not first:
                    act.wait_ge(S["y2_out"], 32 * t)
                high(t + NT, yo[:, D:2 * D], scl_i[:, 9:10].bitcast(F32))

            phase2(0, True)
            with act.Fori(1, NT) as t:
                phase2(t)

            def phase3(t):
                act.wait_ge(S["nrm_tr"], t + 1 + 2 * NT)
                a.activation(nrm_t[:, :], bank[0][:, 0:D], ACT.Copy).then_inc(S["nrm_t_in"], 1)
                act.wait_ge(S["top"], t + 1)
                a.activation(ex, mx, ACT.Exp, bias=neg, accum_out=esum[:, 0:1]).then_inc(S["expd"], 1)

            act.wait_ge(S["counted"], NW)
            with act.Fori(0, NT) as t:
                phase3(t)

            act.wait_ge(S["table"], 1)
            pairs = act.value_load(npair_i[0:1, 0:1], min_val=MIN_PAIRS, max_val=(MAX_TILES + 1) // 2)

            def turn_rows():
                for h in range(2):
                    a.activation(xe_t[h], counts_ps[:, h, 0:D], ACT.Copy).then_inc(S["xe_t_in"], 1)

            act.wait_ge(S["xe_tr"], 1)
            turn_rows()
            with act.Fori(0, pairs) as i:
                for h in range(2):
                    act.wait_ge(S["hb_in"], i * 2 + h + 1)
                    a.activation(ge[h], hb[h], ACT.Gelu).then_inc(S["ge_in"], 1)
                act.wait_ge(S["xe_tr"], i + 2)
                turn_rows()
                for h in range(2):
                    act.wait_ge(S["ge_tr"], i * 2 + h + 1)
                    a.activation(ge_t[h], bank[h][:, 0:D], ACT.Copy).then_inc(S["ge_t_in"], 1)


_INS = ["x", "src", "dst", "L0_gnn_W1_l", "L0_gnn_W1_r", "L0_gnn_b1", "L0_gnn_W2_l", "L0_gnn_W2_r", "L0_gnn_b2",
        "L0_ffn_router_w", "L0_ffn_w1", "L0_ffn_b1", "L0_ffn_w2", "L0_ffn_b2"]


def kernel(**inputs):
    import numpy as _np
    import concourse.bacc as _bacc
    from concourse import mybir as _mybir
    from concourse.bass_utils import run_bass_kernel_spmd as _run

    nc = _bacc.Bacc("TRN2", target_bir_lowering=False, num_devices=1)
    arrays, args = {}, []
    for name in _INS:
        a = _np.ascontiguousarray(inputs[name])
        arrays[f"in_{name}"] = a
        args.append(nc.dram_tensor(f"in_{name}", a.shape, _mybir.dt.from_np(a.dtype), kind="ExternalInput").ap())
    out = nc.dram_tensor("out_0", arrays["in_x"].shape, F32, kind="ExternalOutput").ap()
    with nc.allow_non_contiguous_dma(reason="a few first elements and columns"):
        build(nc, *args, out)
    r = _run(nc, [arrays], core_ids=[0])
    return r.results[0]["out_0"]
```

```python
from contextlib import ExitStack

import concourse.bass as bass
from concourse import mybir

F32 = mybir.dt.float32
F16 = mybir.dt.float16
I32 = mybir.dt.int32
U32 = mybir.dt.uint32
ALU = mybir.AluOpType
ACT = mybir.ActivationFunctionType
AX = mybir.AxisListType
RMAX = bass.bass_isa.ReduceOp.max

P = 128
EPS = 1e-5
EXPONENT_AT = 23


def build(nc, x, src, dst, w1l, w1r, b1, w2l, w2r, b2, router_w, ew1, eb1, ew2, eb2, out):
    N, D = x.shape
    E = src.shape[0]
    KD = D // P
    NT = -(-N // P)
    LAST = N - (NT - 1) * P
    WD = 4
    KEYS = NT * WD
    GW = 8
    HALF = 4
    TILE_GROUPS = P // (GW * WD)
    NW = -(-N // (GW * WD)) * GW
    NGROUP = NW // GW
    WPP = 112
    NG = NW // WPP
    RUN = 125
    FIRSTS = 4
    CHUNK = FIRSTS * RUN
    NCH = E // CHUNK
    ALL_COLS = 400
    ALL_ROWS = E // ALL_COLS
    AC = NT * P
    NE = router_w.shape[0]
    TOPK = 2
    BATCH = 4
    AHEAD = BATCH - 1
    NB = (NT + AHEAD) // BATCH
    RING8 = 2 * BATCH
    REGION = N + P + (-(N + P)) % 16
    MAX_TILES = (TOPK * N) // P + NE
    MIN_TILES = (TOPK * N) // P
    YS_TILES = MAX_TILES + 1
    SPARE = YS_TILES - MIN_TILES
    MIN_PAIRS = (TOPK * N) // P // 2
    NTAB = MAX_TILES + 6
    assert NCH <= P and NCH * CHUNK == E and ALL_ROWS <= P and ALL_ROWS * ALL_COLS == E
    assert NB * BATCH == NT + AHEAD and (NT - 1) % RING8 == 0
    assert NW == NG * WPP and N <= NW * WD <= AC and KEYS <= P and GW == 2 * HALF and HALF * P == 512

    with ExitStack() as ctx:
        def sb(name, shape, dt):
            return ctx.enter_context(nc.sbuf_tensor(name, shape, dt))

        def sem(name):
            return ctx.enter_context(nc.semaphore(name))

        bank = [ctx.enter_context(nc.psum_tensor(f"bank{i}", [P, 512], F32)) for i in range(4, 8)]
        counts_ps = ctx.enter_context(nc.psum_tensor("counts_ps", [P, 4, 512], F32))

        z1_dram = nc.dram_tensor("z1_dram", (NT * P, D), F32, kind="Internal").ap()
        z2_dram = nc.dram_tensor("z2_dram", (NT * P, D), F32, kind="Internal").ap()
        y2_dram = nc.dram_tensor("y2_dram", (NT * P, 2 * D), F16, kind="Internal").ap()
        u_dram = nc.dram_tensor("u_dram", (NT * P, D), F32, kind="Internal").ap()
        xs_dram = nc.dram_tensor("xs_dram", (NE * REGION, D), F32, kind="Internal").ap()
        ys_dram = nc.dram_tensor("ys_dram", ((YS_TILES + SPARE) * P, D), F32, kind="Internal").ap()
        ys_rows = ys_dram[0:YS_TILES * P, :]

        adj = sb("adj", [P, NT, AC], F16)
        y = sb("y", [P, NT, 2 * D], F16)
        w = sb("w", [P, KD, 2 * D], F32)
        b1b = sb("b1b", [P, D], F32)
        b2b = sb("b2b", [P, D], F32)
        ident = sb("ident", [P, P], F32)
        ones = sb("ones", [P, P], F32)
        one_h = sb("one_h", [P, 1], F16)
        iota_4 = sb("iota_4", [P, P, HALF], F16)
        onehots = sb("onehots", [P, 2 * GW * (P + KEYS)], F16)
        oh_src = onehots[:, 0:2 * GW * P].rearrange("p (s c) -> p s c", s=2)
        oh_key = onehots[:, 2 * GW * P:].rearrange("p (s c) -> p s c", s=2)
        key_t = sb("key_t", [P, 2 * ALL_COLS], F16)
        lo_t = sb("lo_t", [P, 2 * ALL_COLS], F16)
        rows = sb("rows", [P, 4 * D], F32)
        xt, nrm, nrm_t, zi = (rows[:, k * D:(k + 1) * D] for k in range(4))
        zt = sb("zt", [P, D], F32)
        yo = sb("yo", [P, 2 * D], F16)
        stat = sb("stat", [P, 16], F32)
        rdeg = sb("rdeg", [P, NT], F32)
        rdeg1 = sb("rdeg1", [P, NT], F32)
        scl = sb("scl", [P, 16], F32)
        scl_i = sb("scl_i", [P, 16], I32)
        flag = sb("flag", [P, 16], F32)
        flag_all = sb("flag_all", [P, 16], F32)
        flag_i = sb("flag_i", [P, 2], I32)

        edge_i = rows[0:ALL_ROWS, 0:ALL_COLS].bitcast(I32)
        edge_lo = rows[0:ALL_ROWS, 2 * D:2 * D + ALL_COLS]
        edge_dst = key_t[0:ALL_ROWS, :].bitcast(F32)
        edge_blk = lo_t[0:ALL_ROWS, :].bitcast(F32)
        w_flat = w[:, :, :].rearrange("p k n -> p (k n)")
        edge_key = w_flat[0:ALL_ROWS, 0:ALL_COLS]
        edge_rel = w_flat[0:ALL_ROWS, ALL_COLS:2 * ALL_COLS]
        zero_h = yo[0:ALL_ROWS, 0:P]
        window_at = stat[0:ALL_ROWS, 15:16]
        STEP = 4
        STEPS = ALL_COLS // STEP
        all_src = oh_src[0:ALL_ROWS, :, 0:STEP * P].rearrange("p s (c k) -> p s c k", c=STEP)
        all_key = oh_key[0:ALL_ROWS, :, 0:STEP * KEYS].rearrange("p s (c k) -> p s c k", c=STEP)
        all_iota = iota_4[0:ALL_ROWS, :, 0:1].rearrange("p k a -> p (k a)")

        used = [0]
        adj_flat = adj[:, :, :].rearrange("p b c -> p (b c)")

        def early(shape, dt, parts=P):
            n = 1
            for d in shape:
                n *= d
            a = adj_flat[0:parts, used[0]:used[0] + 2 * n].bitcast(dt)
            used[0] += 2 * n
            assert used[0] <= NT * AC - AC
            return a.rearrange("p (a b) -> p a b", b=shape[1]) if len(shape) == 2 else a

        dchunk = early([CHUNK], I32, NCH)
        dchunk_f = early([CHUNK], F32, NCH)
        dnext = early([2], I32, NCH)
        dnext_f = early([2], F32, NCH)
        falls = early([CHUNK], F32, NCH)
        wstart = early([NW], I32, NCH)
        below = early([FIRSTS, NW], F32, NCH)
        wlo_i = early([NG], I32, WPP)
        wlo = early([NG], F32, WPP)
        row_f = early([NG], F32, WPP)
        row_u = early([NG], U32, WPP)
        crow = early([NG, RUN], I32, WPP)
        cless = early([NG, RUN], F32, WPP)
        start_f = early([NG], F32, WPP)
        start_u = early([NG], U32, WPP)
        cnt_f = early([NG], F32, WPP)
        run_d = early([NG, RUN], I32, WPP)
        run_s = early([NG, RUN], I32, WPP)
        rel = early([NG, RUN], F32, WPP)
        valid = early([NG, RUN], F32, WPP)
        inside = early([NG, RUN], F32, WPP)
        blk_i = early([NG, RUN], I32, WPP)
        lo_i = early([NG, RUN], I32, WPP)
        key_f = early([NG, RUN], F32, WPP)
        key1 = early([NG, RUN], F32, WPP)
        lo1 = early([NG, RUN], F32, WPP)
        last_in = early([NG], F32, WPP)
        not_end = early([NG], F32, WPP)
        deg_eq = early([NT * P // WD, WD], F16, RUN)
        b1sq = early([D], F32)
        w2_early = early([KD, 2 * D], F32)
        wsq = [early([KD, 2 * D], F32) for _ in range(2)]

        oh_used = [0]

        def later(shape, dt, flat=onehots, used=oh_used):
            n = 1
            for d in shape:
                n *= d
            a = flat[:, used[0]:used[0] + 2 * n].bitcast(dt)
            used[0] += 2 * n
            if len(shape) == 2:
                a = a.rearrange("p (a b) -> p a b", b=shape[1])
            if len(shape) == 3:
                a = a.rearrange("p (a b c) -> p a b c", b=shape[1], c=shape[2])
            return a

        tok = [w_flat[:, k * D:(k + 1) * D] for k in range(2 * KD)] + [later([D], F32) for _ in range(RING8 - 2 * KD)]
        uo = yo[:, :].bitcast(F32)
        tri = later([P], F32)
        rw_t = later([KD, NE], F32)
        iota_e = later([NE], F32)
        iota_ei = later([NE], I32)
        lg = later([BATCH, NE], F32)
        mx = later([BATCH, NE], F32)
        mix = later([BATCH, NE], U32)
        less = later([BATCH, NE], F32)
        ex = later([BATCH, NE], F32)
        pick = later([BATCH, TOPK], F32)
        mask = later([BATCH * TOPK, NE], F32)
        both = later([BATCH, NE], F32)
        pairs_of = later([BATCH, NE], F32)
        before = later([BATCH + 1, NE], F32)
        esum = later([BATCH], F32)
        resum = later([BATCH], F32)
        prob = later([BATCH, TOPK], F32)
        base_e = later([NE], F32)
        pos = later([BATCH, NE], F32)
        posm = later([BATCH * TOPK, NE], F32)
        slot_f = later([BATCH * TOPK], F32)
        slot_u = [later([BATCH * TOPK], U32) for _ in range(2)]
        coef = later([NB * BATCH, TOPK], F32)
        slots = later([NB * BATCH * TOPK], U32)
        node = later([NB * BATCH], F32)
        assert oh_used[0] <= 2 * GW * (P + KEYS)

        FREE_TILES = 2 * KD * D // P
        ew1_sb, ew2_sb, eb_sb = (adj[:, n * NE:(n + 1) * NE, 0:2 * KD * D].bitcast(F32) for n in range(3))
        assert 3 * NE <= NT and KD == 2

        def ew(of, e, k):
            return of[:, bass.ds(e, 1), k * D:(k + 1) * D].rearrange("p a n -> p (a n)")

        moe_used = [2 * KD * D]
        y_flat = y[:, :, :].rearrange("p t n -> p (t n)")
        y_used = [0]

        def expert(shape, dt):
            n = 2
            for d in shape:
                n *= d
            if moe_used[0] % AC == 0:
                moe_used[0] += 2 * KD * D
            if moe_used[0] // AC != (moe_used[0] + n - 1) // AC:
                moe_used[0] = (moe_used[0] // AC + 1) * AC + 2 * KD * D
            assert moe_used[0] % AC + n <= AC
            return later(shape, dt, adj_flat, moe_used)

        def expert_y(shape, dt):
            a = later(shape, dt, y_flat, y_used)
            assert y_used[0] <= NT * 2 * D
            return a

        xe = [expert([D], F32) for _ in range(2)]
        xe_t = [expert([D], F32) for _ in range(2)]
        hb = [expert([D], F32) for _ in range(2)]
        ge = [expert([D], F32) for _ in range(2)]
        ge_t = [expert([D], F32) for _ in range(2)]
        ye = [expert([D], F32) for _ in range(2)]
        zero_t = expert_y([SPARE, D], F32)
        cnt = expert([NE], F32)
        end_i = expert([NE], I32)
        nt_i = expert([NE], I32)
        nt_f = expert([NE], F32)
        cum = [expert([NE], F32) for _ in range(4)]
        jump = expert([NE], F32)
        first_row = expert([NE], F32)
        iota_j = key_t[:, 0:2 * NTAB].bitcast(I32)
        jf = expert([NTAB], F32)
        tab_e = expert([NTAB], F32)
        tab_r = expert([NTAB], F32)
        past = expert([NTAB], F32)
        stay = expert([NTAB], F32)
        tab_ei = expert([NTAB // 2], I32)
        tab_ef = expert([NTAB], F32)
        tab_ri = expert([NTAB], I32)
        npair_i = expert([2], I32)
        ends_i = expert([2], I32)
        slots_f = expert([NB * BATCH * TOPK], F32)
        moved = expert([NB * BATCH * TOPK], F32)
        slots_y = expert([NB * BATCH, TOPK], U32)
        place_f = [expert([NB * BATCH * TOPK], F32) for _ in range(2)]
        RING = 3
        assert (NT - 1) % RING == 0
        yg = expert_y([RING * TOPK, D], F32)
        ug = expert_y([RING, D], F32)
        og = expert_y([RING, D], F32)
        gix = expert([RING, TOPK], U32)

        names = ["edges_in", "x_in", "w_in", "consts", "iota", "first_ge", "firsts", "chunk_ix", "chunk_in", "start_ix",
                 "run_in", "keys", "keys_tr", "keys_in", "onehot", "counted", "adj_in", "wsq", "wnorm", "wsum", "wroot",
                 "scaled", "var_in", "rstd_in", "normed", "nrm_tr", "nrm_t_in", "projected", "hi_in", "yz_in", "z_out",
                 "agg", "z_in", "h_in", "y2_out", "zx_taken", "sums_free", "logits_in", "tok_free", "node_in", "pad_ok", "flag_in", "flag_all",
                 "tri_in", "rw_in", "u_ready", "u_out", "logits", "top", "expd", "masks", "prefix", "slots", 
                 "flag_out", "all_in", "all_free", "all_keys", "all_onehot", "all_counted", "all_open", "all_window", "all_kept",
                 "all_done", "deg_eq", "deg_counted", "all_degrees", "held", "pool_held", "table", "padded", "zeros", "ew_in", "xe_in", "xe_tr", "xe_t_in", "hid", "hb_in", "ge_in", "ge_tr",
                 "ge_t_in", "ye_ps", "ye_in", "ye_out", "gix_in", "yg_in", "ug_in", "og_in", "og_out"]
        S = {n: sem(n) for n in names}
        NQ = 5
        y2_in = [sem(f"y2_in{c}") for c in range(NQ)]
        chain = sem("dve_chain")
        scattered = [sem(f"scattered{q}") for q in range(2)]
        xe_in = [sem(f"xe_in{h}") for h in range(2)]
        ye_out = [sem(f"ye_out{h}") for h in range(2)]
        sum_out_of = [sem(f"sum_out{q}") for q in range(RING)]
        yg_in = [sem(f"yg_in{q}") for q in range(RING)]
        ug_in = [sem(f"ug_in{q}") for q in range(RING)]

        block = ctx.enter_context(nc.Block())
        runs_src = src[0:E].rearrange("(p c) -> p c", c=RUN)
        runs_dst = dst[0:E].rearrange("(p c) -> p c", c=RUN)
        chunks = dst.rearrange("(p c) -> p c", c=CHUNK)
        runs_of_dst = dst.rearrange("(p c) -> p c", c=RUN)

        def tile_rows(ap, t):
            return ap[bass.ds(t * P, P), :]

        @block.sync
        def _(sp):
            sp.dma_start(dchunk, chunks).then_inc(S["edges_in"], 16)
            sp.dma_start(dnext[0:NCH - 1, 0:1], chunks[1:NCH, 0:1]).then_inc(S["edges_in"], 16)
            sp.dma_start(xt[:, :], x[0:P, :]).then_inc(S["x_in"], 16)
            for to, (l, r) in ((w, (w1l, w1r)), (w2_early, (w2l, w2r))):
                sp.dma_start(to[:, :, 0:D], l.rearrange("(k p) n -> p k n", p=P)).then_inc(S["w_in"], 16)
                sp.dma_start(to[:, :, D:2 * D], r.rearrange("(k p) n -> p k n", p=P)).then_inc(S["w_in"], 16)
            for b, v in ((b1b, b1), (b2b, b2)):
                sp.dma_start(b[:, :], v.rearrange("(a n) -> a n", a=1).to_broadcast((P, D))).then_inc(S["w_in"], 16)
            sp.wait_ge(S["normed"], 1)
            sp.dma_start(xt[:, :], x[P:2 * P, :]).then_inc(S["x_in"], 16)
            with sp.Fori(1, NT - 2) as t:
                sp.wait_ge(S["normed"], t + 1)
                sp.dma_start(xt[:, :], tile_rows(x, t + 1)).then_inc(S["x_in"], 16)
                sp.wait_ge(S["yz_in"], t)
                sp.dma_start(tile_rows(z1_dram, t - 1), zt[:, :]).then_inc(S["z_out"], 16)
            sp.wait_ge(S["pad_ok"], 1)
            sp.dma_start(xt[0:LAST, :], x[(NT - 1) * P:N, :]).then_inc(S["x_in"], 16)
            for t in range(NT - 3, NT):
                sp.wait_ge(S["yz_in"], t + 1)
                sp.dma_start(z1_dram[t * P:(t + 1) * P, :], zt[:, :]).then_inc(S["z_out"], 16)
            sp.wait_ge(S["flag_out"], 1)
            with sp.If(sp.value_load(flag_i[0:1, 0:1], min_val=0, max_val=1) == 1):
                sp.wait_ge(S["projected"], NT)
                sp.wait_ge(S["adj_in"], NGROUP)
                sp.dma_start(edge_i, dst.rearrange("(p c) -> p c", c=ALL_COLS)).then_inc(S["all_in"], 16)
                sp.wait_ge(S["all_free"], 1)
                sp.dma_start(edge_i, src.rearrange("(p c) -> p c", c=ALL_COLS)).then_inc(S["all_in"], 16)
                sp.wait_ge(S["all_done"], 1)
            sp.wait_ge(S["projected"], NT)
            sp.dma_start(w[:, :, 0:D], w2l.rearrange("(k p) n -> p k n", p=P)).then_inc(S["w_in"], 16)
            sp.dma_start(w[:, :, D:2 * D], w2r.rearrange("(k p) n -> p k n", p=P)).then_inc(S["w_in"], 16)
            sp.wait_ge(S["z_out"], 16 * NT)
            sp.dma_start(zi[:, :], z1_dram[0:P, :]).then_inc(S["z_in"], 16)
            with sp.Fori(0, NT - 1) as t:
                sp.wait_ge(S["h_in"], t + 1)
                sp.dma_start(zi[:, :], tile_rows(z1_dram, t + 1)).then_inc(S["z_in"], 16)
                sp.wait_ge(S["yz_in"], t + 1 + NT)
                sp.dma_start(tile_rows(z2_dram, t), zt[:, :]).then_inc(S["y2_out"], 16)
                sp.dma_start(tile_rows(y2_dram, t), yo[:, :]).then_inc(S["y2_out"], 16)
            sp.wait_ge(S["yz_in"], 2 * NT)
            sp.dma_start(z2_dram[(NT - 1) * P:, :], zt[:, :]).then_inc(S["y2_out"], 16)
            sp.dma_start(y2_dram[(NT - 1) * P:, :], yo[:, :]).then_inc(S["y2_out"], 16)
            sp.wait_ge(S["y2_out"], 32 * NT)
            y2v = y2_dram.rearrange("(t p) c -> p t c", p=P)
            for c in range(NQ):
                sp.dma_start(y[:, NT // NQ * c:NT // NQ * (c + 1), 0:2 * D], y2v[:, NT // NQ * c:NT // NQ * (c + 1), :]
                             ).then_inc(y2_in[c], 16)
                if c == 0:
                    sp.dma_start(zi[:, :], z2_dram[0:P, :]).then_inc(S["z_in"], 16)
                    sp.dma_start(xt[:, :], x[0:P, :]).then_inc(S["x_in"], 16)
            for k in range(KD):
                sp.dma_start(rw_t[:, k, :], router_w[:, k * P:(k + 1) * P].rearrange("e p -> p e")
                             ).then_inc(S["rw_in"], 16)
            def node_tile(t):
                sp.wait_ge(S["zx_taken"], t + 1)
                sp.dma_start(zi[:, :], tile_rows(z2_dram, t + 1)).then_inc(S["z_in"], 16)
                sp.dma_start(xt[:, :], tile_rows(x, t + 1)).then_inc(S["x_in"], 16)
                sp.wait_ge(S["u_ready"], t + 1)
                sp.dma_start(tile_rows(u_dram, t), uo).then_inc(S["u_out"], 16)

            with sp.Fori(0, FREE_TILES) as t:
                node_tile(t)
            with sp.Fori(0, NE) as e:
                node_tile(e + FREE_TILES)
                sp.wait_ge(S["agg"], NT + FREE_TILES)
                for to, w_e in ((ew1_sb, ew1), (ew2_sb, ew2)):
                    sp.dma_start(to[:, bass.ds(e, 1), :].rearrange("p a (k n) -> p (a k) n", n=D),
                                 w_e[bass.ds(e, 1), :, :].rearrange("a (k p) n -> p (a k) n", p=P)
                                 ).then_inc(S["ew_in"], 16)
                for n, b_e in enumerate((eb1, eb2)):
                    sp.dma_start(ew(eb_sb, e, n), b_e[bass.ds(e, 1), :].to_broadcast((P, D))).then_inc(S["ew_in"], 16)
            with sp.Fori(FREE_TILES + NE, NT - 2) as t:
                node_tile(t)
            sp.wait_ge(S["zx_taken"], NT - 1)
            sp.dma_start(zi[:, :], z2_dram[(NT - 1) * P:, :]).then_inc(S["z_in"], 16)
            sp.dma_start(xt[0:LAST, :], x[(NT - 1) * P:N, :]).then_inc(S["x_in"], 16)
            for t in range(NT - 2, NT):
                sp.wait_ge(S["u_ready"], t + 1)
                sp.dma_start(u_dram[t * P:(t + 1) * P, :], uo).then_inc(S["u_out"], 16)
            sp.wait_ge(S["table"], 1)
            sp.wait_ge(S["zeros"], 1)
            for e in range(NE):
                end = sp.value_load(end_i[0:1, e:e + 1], min_val=e * REGION, max_val=e * REGION + N)
                sp.dma_start(xs_dram[bass.ds(end, P), :], zero_t[:, 0, :]).then_inc(S["padded"], 16)
            end = sp.value_load(ends_i[0:1, 0:1], min_val=MIN_TILES * P, max_val=YS_TILES * P)
            sp.dma_start(ys_dram[bass.ds(end, SPARE * P), :].rearrange("(t p) n -> p t n", p=P), zero_t
                         ).then_inc(S["padded"], 16)
            sp.wait_ge(S["padded"], 16 * (NE + 1))
            for q in range(2):
                sp.wait_ge(scattered[q], 16 * TOPK * len(range(q, NT, 2)))
            pairs = sp.value_load(npair_i[0:1, 0:1], min_val=MIN_PAIRS, max_val=(MAX_TILES + 1) // 2)

            def load_pair(i):
                for h in range(2):
                    row = sp.value_load(tab_ri[0:1, bass.ds(i * 2 + h, 1)], min_val=0, max_val=NE * REGION - P)
                    sp.dma_start(xe[h], xs_dram[bass.ds(row, P), :]).then_inc(xe_in[h], 16)

            load_pair(0)
            sp.wait_ge(S["xe_tr"], 1)
            load_pair(1)
            with sp.Fori(0, pairs) as i:
                sp.wait_ge(S["xe_tr"], i + 2)
                load_pair(i + 2)
            sp.wait_ge(S["u_out"], 16 * NT)
            for t in range(RING):
                sp.dma_start(ug[:, t, :], u_dram[t * P:(t + 1) * P, :]).then_inc(ug_in[t], 16)

            def sum_out(t, s, more=True):
                sp.wait_ge(S["og_in"], t + 1)
                sp.dma_start(tile_rows(out, t), og[:, s, :]).then_inc(sum_out_of[s], 16)
                if more:
                    sp.dma_start(ug[:, s, :], tile_rows(u_dram, t + RING)).then_inc(ug_in[s], 16)

            sum_out(0, 0)
            with sp.Fori(0, NT // RING - 1) as i:
                for q in range(RING):
                    sum_out(i * RING + (q + 1), (q + 1) % RING)
            for t in range(NT - RING, NT - 1):
                sum_out(t, t % RING, False)
            sp.wait_ge(S["og_in"], NT)
            sp.dma_start(out[(NT - 1) * P:N, :], og[0:LAST, (NT - 1) % RING, :]
                         ).then_inc(sum_out_of[(NT - 1) % RING], 16)
            for q in range(RING):
                sp.wait_ge(sum_out_of[q], 16 * len(range(q, NT, RING)))

        @block.gpsimd
        def _(pool):
            g = nc.gpsimd
            g.iota(wstart, [[WD, NW]], base=0, channel_multiplier=0).then_inc(S["iota"], 1)
            g.iota(wlo_i, [[WD * WPP, NG]], base=0, channel_multiplier=WD).then_inc(S["iota"], 1)
            g.iota(iota_4[:, :, :], [[1, P], [0, HALF]], base=1, channel_multiplier=0,
                   allow_small_or_imprecise_dtypes=True).then_inc(S["iota"], 1)
            pool.wait_ge(S["consts"], 1)
            g.affine_select(out=ident[:, :], in_=ident[:, :], compare_op=ALU.not_equal, fill=1.0, base=0,
                            pattern=[[-1, P]], channel_multiplier=1).then_inc(S["iota"], 1)
            pool.wait_ge(S["chunk_ix"], 1)
            for k in range(NG):
                g.indirect_dma_start(crow[:, k, :], None, runs_of_dst,
                                     bass.IndirectOffsetOnAxis(ap=row_u[:, k:k + 1], axis=0)
                                     ).then_inc(S["chunk_in"], 16)
            pool.wait_ge(S["start_ix"], 1)
            for k in range(NG):
                for r, v in ((run_d, runs_dst), (run_s, runs_src)):
                    g.indirect_dma_start(r[:, k, :], None, v,
                                         bass.IndirectOffsetOnAxis(ap=start_u[:, k:k + 1], axis=1)
                                         ).then_inc(S["run_in"], 16)
            with pool.Fori(0, NT) as t:
                pool.wait_ge(S["var_in"], t + 1)
                g.tensor_tensor(stat[:, 8:9], stat[:, 9:10], stat[:, 10:11], ALU.pow).then_inc(S["rstd_in"], 1)
            pool.wait_ge(S["flag_in"], 1)
            g.partition_all_reduce(flag_all[:, :], flag[:, :], P, RMAX).then_inc(S["flag_all"], 1)
            pool.wait_ge(S["agg"], 1)
            g.iota(iota_ei, [[1, NE]], base=0, channel_multiplier=0).then_inc(S["iota"], 1)
            g.iota(iota_j, [[1, NTAB]], base=0, channel_multiplier=0).then_inc(S["iota"], 1)
            pool.wait_ge(S["tri_in"], 1)
            g.affine_select(out=node[:, NB * BATCH - 1:], in_=node[:, NB * BATCH - 1:], compare_op=ALU.is_ge, fill=0.0,
                            base=LAST - 1, pattern=[[0, 1]], channel_multiplier=-1).then_inc(S["iota"], 1)
            g.affine_select(out=tri, in_=tri, compare_op=ALU.is_gt, fill=0.0, base=0,
                            pattern=[[1, P]], channel_multiplier=-1).then_inc(S["iota"], 1)

            def root(t):
                pool.wait_ge(S["var_in"], t + NT + 1)
                g.tensor_tensor(stat[:, 8:9], stat[:, 9:10], stat[:, 10:11], ALU.pow).then_inc(S["rstd_in"], 1)

            def scatter(i, s, rows=P, first=False):
                pool.wait_ge(S["slots"], i * 2 + (s // BATCH + 1))
                pool.sem_inc(S["pool_held"], 1)
                for k in range(TOPK):
                    g.indirect_dma_start(xs_dram, bass.IndirectOffsetOnAxis(
                        ap=slot_u[s // BATCH][0:rows, s % BATCH * TOPK + k:s % BATCH * TOPK + k + 1], axis=0),
                        tok[(s + RING8 - AHEAD) % RING8][0:rows, :], None).then_inc(scattered[(s + 1) % 2], 16)
                if not first:
                    last = s % 2
                    pool.wait_ge(scattered[last], (i * BATCH + ((s - BATCH) // 2 + 1)) * (16 * TOPK))
                    pool.sem_inc(S["tok_free"], 1)

            def turn_of_tiles(i, first=False):
                for r in range(1, RING8 + 1):
                    root(i * RING8 + r)
                    for s in {1: (), RING8: (RING8 - 2, RING8 - 1)}.get(r, (r - 2,)):
                        if s >= AHEAD or not first:
                            scatter(i, s, first=first and s == AHEAD)

            pool.sem_inc(S["tok_free"], RING8)
            root(0)
            turn_of_tiles(0, True)
            with pool.Fori(1, (NT - 1) // RING8) as i:
                turn_of_tiles(i)
            for q in range(BATCH):
                scatter(NB // 2, q, LAST if q == BATCH - 1 else P)
            pool.wait_ge(S["table"], 1)
            pool.wait_ge(S["padded"], 16 * (NE + 1))
            pairs = pool.value_load(npair_i[0:1, 0:1], min_val=MIN_PAIRS, max_val=(MAX_TILES + 1) // 2)
            with pool.Fori(0, pairs) as i:
                for h in range(2):
                    pool.wait_ge(S["ye_in"], i * 2 + h + 3)
                    pool.dma_start(ys_dram[bass.ds((i * 2 + h) * P, P), :], ye[h]).then_inc(ye_out[h], 16)
            for h in range(2):
                pool.wait_ge(ye_out[h], pairs * 16)
            def gather(t, s):
                pool.wait_ge(S["gix_in"], t + 1)
                pool.sem_inc(S["pool_held"], 1)
                for k in range(TOPK):
                    g.indirect_dma_start(yg[:, s * TOPK + k, :], None, ys_rows,
                                         bass.IndirectOffsetOnAxis(ap=gix[:, s, k:k + 1], axis=0)
                                         ).then_inc(yg_in[s], 16)

            gather(0, 0)
            with pool.Fori(0, NT // RING) as i:
                for q in range(RING):
                    gather(i * RING + (q + 1), (q + 1) % RING)

        def group_onehots(dve, group, slot):
            dve.wait_ge(S["counted"], group - 1)
            group_onehots_now(group, slot)

        def group_onehots_now(group, slot):
            for oh, n, of in ((oh_src, P, lo_t), (oh_key, KEYS, key_t)):
                last = nc.vector.tensor_tensor(
                    oh[0:RUN, slot, :].rearrange("p (g k w) -> p g k w", g=2, w=HALF),
                    iota_4[0:RUN, 0:n, :].rearrange("p (g k) w -> p g k w", g=1).to_broadcast((RUN, 2, n, HALF)),
                    of[0:RUN, bass.ds(group * GW, GW)].rearrange("p (g a w) -> p g a w", g=2, a=1
                                                                 ).to_broadcast((RUN, 2, n, HALF)), ALU.is_equal)
            last.then_inc(S["onehot"], 1)

        def group_counts(pe, group, slot):
            pe.wait_ge(S["onehot"], group + 1)
            for g in range(2):
                stat_g = oh_src[0:RUN, slot, g * HALF * P:(g + 1) * HALF * P].rearrange("p (k w) -> p k w", w=HALF)
                mov_g = oh_key[0:RUN, slot, g * HALF * KEYS:(g + 1) * HALF * KEYS].rearrange("p (k w) -> p k w", w=HALF)
                for h in range(HALF):
                    last = nc.tensor.matmul(counts_ps[:, 2 * slot + g, h * P:h * P + KEYS],
                                            stat_g[:, :, h:h + 1].rearrange("p k a -> p (k a)"),
                                            mov_g[:, :, h:h + 1].rearrange("p k a -> p (k a)"), start=True, stop=True)
            last.then_inc(S["counted"], 1)

        def group_keep(act, group, slot):
            act.wait_ge(S["counted"], group + 1)
            nc.scalar.activation(
                adj[:, :, bass.ds(group * GW * WD, GW * WD)].rearrange("p b (h d) -> p b h d", d=WD),
                counts_ps[:, 2 * slot:2 * slot + 2, :].rearrange("p g (w c) -> p (g w) c", w=HALF)[:, :, 0:KEYS]
                .rearrange("p h (b d) -> p b h d", d=WD),
                ACT.Copy).then_inc(S["adj_in"], 1)

        PER3 = 56
        @block.vector
        def _(dve):
            v = nc.vector
            count = [0]
            base = [0]

            def link(ins):
                count[0] += 1
                ins.then_inc(chain, 1)
                dve.wait_ge(chain, base[0] + count[0])

            v.memset(ident[:, :], 0.0).then_inc(S["consts"], 1)
            v.memset(one_h[:, :], 1.0)
            v.memset(ones[:, :], 1.0).then_inc(S["consts"], 1)
            v.memset(stat[:, 10:11], -0.5)
            v.memset(flag[:, :], 0.0)
            dve.wait_ge(S["edges_in"], 32)
            v.tensor_copy(dchunk_f, dchunk)
            link(v.tensor_copy(dnext_f[0:NCH - 1, 0:1], dnext[0:NCH - 1, 0:1]))
            dve.wait_ge(S["iota"], 3)
            for j in range(FIRSTS):
                last = v.tensor_scalar(below[:, j, :], wstart, dchunk_f[:, j * RUN:j * RUN + 1], None, ALU.is_gt)
            last.then_inc(S["first_ge"], 1)
            v.tensor_copy(wlo, wlo_i)
            v.tensor_tensor(flag[0:NCH - 1, 1:2], dchunk_f[0:NCH - 1, CHUNK - 1:CHUNK], dnext_f[0:NCH - 1, 0:1],
                            ALU.is_gt)
            link(v.tensor_tensor(falls[:, 0:CHUNK - 1], dchunk_f[:, 0:CHUNK - 1], dchunk_f[:, 1:CHUNK], ALU.is_gt))
            v.tensor_reduce(flag[0:NCH, 0:1], falls[:, 0:CHUNK - 1], AX.X, ALU.max)
            dve.wait_ge(S["firsts"], 1)
            link(v.tensor_scalar(row_f, bank[2][0:WPP, 0:NG], -1.0, 0.0, ALU.add, ALU.max))
            v.tensor_copy(row_u, row_f).then_inc(S["chunk_ix"], 1)
            dve.wait_ge(S["w_in"], 96)
            v.tensor_tensor(b1sq, b1b[:, :], b1b[:, :], ALU.mult)
            for q, a in zip(wsq, (w[:, :, :], w2_early)):
                v.tensor_tensor(q, a, a, ALU.mult).then_inc(S["wsq"], 1)
            dve.wait_ge(S["chunk_in"], 16 * NG)
            for k in range(NG):
                ins = v.tensor_scalar(cless[:, k, :], crow[:, k, :], wlo[:, k:k + 1], None, ALU.is_lt)
            link(ins)
            link(v.tensor_reduce(cnt_f, cless, AX.X, ALU.add))
            link(v.scalar_tensor_tensor(start_f, row_f, float(RUN), cnt_f, ALU.mult, ALU.add))
            link(v.tensor_scalar(start_f, start_f, float(E - RUN), None, ALU.min))
            v.tensor_copy(start_u, start_f).then_inc(S["start_ix"], 1)
            dve.wait_ge(S["wnorm"], 2)
            v.tensor_reduce(scl[:, 0:1], bank[3][:, 0:D], AX.X, ALU.max)
            v.tensor_reduce(scl[:, 1:3], bank[3][:, :].rearrange("p (s n) -> p s n", s=2), AX.X, ALU.add)
            v.tensor_reduce(scl[:, 3:4], bank[1][:, 0:D], AX.X, ALU.max)
            v.tensor_reduce(scl[:, 4:5], b1sq, AX.X, ALU.add).then_inc(S["wsum"], 1)
            dve.wait_ge(S["wroot"], 1)
            root = scl[:, 8:13]
            link(v.tensor_scalar(scl[:, 5:6], root[:, 1:2], root[:, 2:3], float(D) ** 0.5, ALU.add, ALU.mult))
            link(v.tensor_scalar(scl[:, 5:6], scl[:, 5:6], root[:, 4:5], root[:, 3:4], ALU.add, ALU.mult))
            link(v.tensor_scalar(scl[:, 4:5], root[:, 0:1], float(D) ** 0.5, None, ALU.mult))
            link(v.tensor_scalar(scl[:, 4:6], scl[:, 4:6], 1e-30, None, ALU.max))
            link(v.tensor_scalar(scl_i[:, 0:2], scl[:, 4:6].bitcast(I32), EXPONENT_AT, None, ALU.logical_shift_right))
            link(v.tensor_scalar(scl_i[:, 2:4], scl_i[:, 0:2], -1.0, 268.0, ALU.mult, ALU.add))
            link(v.tensor_scalar(scl_i[:, 4:6], scl_i[:, 2:4], -1.0, 254.0, ALU.mult, ALU.add))
            v.tensor_scalar(scl_i[:, 8:10], scl_i[:, 2:4], EXPONENT_AT, None, ALU.logical_shift_left)
            link(v.tensor_scalar(scl_i[:, 10:12], scl_i[:, 4:6], EXPONENT_AT, None, ALU.logical_shift_left))
            dve.wait_ge(S["run_in"], 32 * NG)
            for k in range(NG):
                v.tensor_scalar(rel[:, k, :], run_d[:, k, :], wlo[:, k:k + 1], None, ALU.subtract)
            v.tensor_scalar(blk_i, run_s, P.bit_length() - 1, None, ALU.logical_shift_right)
            link(v.tensor_scalar(lo_i, run_s, P - 1, None, ALU.bitwise_and))
            v.tensor_scalar(inside, rel, 0.0, None, ALU.is_ge)
            v.tensor_scalar(lo1, lo_i, 1.0, None, ALU.add)
            link(v.scalar_tensor_tensor(key_f, blk_i, float(WD), rel, ALU.mult, ALU.add))
            link(v.scalar_tensor_tensor(valid, rel, float(WD), inside, ALU.is_lt, ALU.mult))
            v.scalar_tensor_tensor(key1, key_f, 1.0, valid, ALU.add, ALU.mult).then_inc(S["keys"], 1)
            link(v.tensor_scalar(not_end, start_f, float(E - RUN), None, ALU.is_lt))
            v.scalar_tensor_tensor(flag[0:WPP, 2:2 + NG], rel[:, :, RUN - 1:RUN].rearrange("p g a -> p (g a)"), float(WD),
                                   not_end, ALU.is_lt, ALU.mult).then_inc(S["flag_in"], 1)
            dve.wait_ge(S["flag_in"], 1)
            dve.wait_ge(S["keys_tr"], 1)
            v.memset(deg_eq[:, NW:, :], 0.0)
            for b in range(2):
                for d in range(WD):
                    last = v.tensor_scalar(deg_eq[:, HALF * WPP * b:min(HALF * WPP * (b + 1), NW), d:d + 1]
                                           .rearrange("p w a -> p (w a)"),
                                           bank[b][0:RUN, 0:min(HALF, NG - HALF * b) * WPP], float(d), None, ALU.is_equal)
            last.then_inc(S["deg_eq"], 1)
            for b in range(2):
                m = min(HALF, NG - HALF * b) * WPP
                v.tensor_copy(key_t[0:RUN, HALF * WPP * b:HALF * WPP * b + m], counts_ps[0:RUN, b, 0:m])
                last = v.tensor_copy(lo_t[0:RUN, HALF * WPP * b:HALF * WPP * b + m], counts_ps[0:RUN, 2 + b, 0:m])
            link(last)
            v.memset(stat[:, 11:12], 0.0).then_inc(S["scaled"], 1)

            def stats(t):
                dve.wait_ge(S["x_in"], 16 * (t + 1))
                link(v.bn_stats(stat[:, 0:6], xt[:, :]))
                dve.sem_inc(S["held"], 1)
                link(v.bn_aggr(stat[:, 6:8], stat[:, 0:6]))
                v.tensor_scalar(stat[:, 9:10], stat[:, 7:8], EPS, None, ALU.add).then_inc(S["var_in"], 1)

            def normalise(t, read):
                dve.wait_ge(S["rstd_in"], t + 1)
                if read:
                    dve.wait_ge(S["nrm_tr"], t)
                v.tensor_scalar(nrm[:, :], xt[:, :], stat[:, 6:7], stat[:, 8:9], ALU.subtract, ALU.mult
                                ).then_inc(S["normed"], 1)

            def split_y(t, out_, bias, scale):
                dve.wait_ge(S["hi_in"], t + 1)
                v.scalar_tensor_tensor(out_[0], bank[1][:, 0:D], scale, out_[1], ALU.mult, ALU.subtract)
                v.tensor_tensor(zt[:, :], bank[1][:, D:2 * D], bias, ALU.add).then_inc(S["yz_in"], 1)

            def yrow(t):
                return (y[:, bass.ds(t, 1), 0:D].rearrange("p a n -> p (a n)"),
                        y[:, bass.ds(t, 1), D:2 * D].rearrange("p a n -> p (a n)"))

            s1 = scl_i[:, 8:9].bitcast(F32)
            s2 = scl_i[:, 9:10].bitcast(F32)
            i1 = scl_i[:, 10:11].bitcast(F32)
            i2 = scl_i[:, 11:12].bitcast(F32)

            def phase1_split(t, first=False):
                if not first:
                    dve.wait_ge(S["z_out"], 16 * t)
                split_y(t, yrow(t), b1b[:, :], s1)

            def phase1(t, first=False, groups=TILE_GROUPS, second=False):
                stats(t)
                for q in range(groups):
                    group = t * TILE_GROUPS + q
                    if first and q < 2:
                        group_onehots_now(group, q % 2)
                    else:
                        group_onehots(dve, group, q % 2)
                    if q == 0:
                        normalise(t, not first)
                    if q == 1 and not first:
                        phase1_split(t - 1, second)

            phase1(0, True)
            dve.wait_ge(S["deg_counted"], 1)
            v.memset(adj[:, :, NW * WD:AC], 0.0)
            phase1(1, second=True)
            per = 2
            with dve.Fori(2, NT - 1) as t:
                start = count[0]
                base[0] = (t - 2) * per
                phase1(t)
                assert count[0] - start == per
            base[0] = 0
            count[0] += per * (NT - 4)
            dve.wait_ge(S["nrm_tr"], NT - 1)
            link(v.memset(xt[:, :], 0.0))
            v.memset(stat[:, 11:12], 0.0).then_inc(S["pad_ok"], 1)
            phase1(NT - 1, groups=NGROUP - (NT - 1) * TILE_GROUPS)
            phase1_split(NT - 1)

            dve.wait_ge(S["flag_all"], 1)
            link(v.tensor_reduce(flag_all[:, 15:16], flag_all[:, 0:2 + NG], AX.X, ALU.max))
            v.tensor_copy(flag_i[:, 0:1], flag_all[:, 15:16]).then_inc(S["flag_out"], 1)
            dve.wait_ge(S["flag_out"], 1)
            with dve.If(dve.value_load(flag_i[0:1, 0:1], min_val=0, max_val=1) == 1):
                n = [0]

                def then(ins, at=0):
                    n[0] += 1
                    ins.then_inc(S["all_keys"], 1)
                    dve.wait_ge(S["all_keys"], at + n[0])

                dve.wait_ge(S["projected"], NT)
                dve.wait_ge(S["z_out"], 16 * NT)
                dve.wait_ge(S["counted"], NGROUP)
                dve.wait_ge(S["all_in"], 16)
                then(v.memset(zero_h, 0.0))
                then(v.memset(window_at, 0.0))
                v.tensor_copy(edge_dst, edge_i).then_inc(S["all_free"], 1)
                dve.wait_ge(S["all_in"], 32)
                then(v.tensor_scalar(edge_rel.bitcast(I32), edge_i, P - 1, None, ALU.bitwise_and))
                then(v.tensor_scalar(edge_key.bitcast(I32), edge_i, P.bit_length() - 1, None, ALU.logical_shift_right))
                then(v.tensor_scalar(edge_lo, edge_rel.bitcast(I32), 1.0, None, ALU.add))
                then(v.tensor_scalar(edge_blk, edge_key.bitcast(I32), float(WD), 1.0, ALU.mult, ALU.add))
                with dve.Fori(0, NW) as wi:
                    at, links = wi * 5, n[0]
                    then(v.tensor_scalar(edge_rel, edge_dst, window_at, None, ALU.subtract), at)
                    dve.wait_ge(S["all_counted"], wi * STEPS + 2)
                    then(v.tensor_tensor(edge_key, edge_blk, edge_rel, ALU.add), at)
                    then(v.scalar_tensor_tensor(edge_key, edge_rel, 0.0, edge_key, ALU.is_ge, ALU.mult), at)
                    then(v.scalar_tensor_tensor(edge_key, edge_rel, float(WD), edge_key, ALU.is_lt, ALU.mult), at)
                    then(v.tensor_scalar(window_at, window_at, float(WD), None, ALU.add), at)
                    assert n[0] - links == 5
                    n[0] = links
                    dve.sem_inc(S["held"], 1)
                    with dve.Fori(0, STEPS // 2) as i:
                        for q in range(2):
                            dve.wait_ge(S["all_counted"], wi * STEPS + i * 2 + (q + 1))
                            for c in range(STEP):
                                col = (i * 2 + q) * STEP + c
                                v.tensor_scalar(all_src[:, q, c, :], all_iota,
                                                edge_lo[:, bass.ds(col, 1)], None, ALU.is_equal)
                                last = v.tensor_scalar(all_key[:, q, c, :], all_iota[:, 0:KEYS],
                                                       edge_key[:, bass.ds(col, 1)], None, ALU.is_equal)
                            last.then_inc(S["all_onehot"], 1)

                dve.wait_ge(S["all_degrees"], NT)
            dve.wait_ge(S["deg_counted"], 1)
            link(v.tensor_scalar(rdeg1[:, :], bank[2][:, 0:NT], 1.0, None, ALU.max))
            link(v.reciprocal(rdeg[:, :], rdeg1[:, :]))
            link(v.tensor_scalar(rdeg1[:, :], rdeg[:, :], i1, None, ALU.mult))

            def phase2(t, s):
                dve.wait_ge(S["agg"], t + 1)
                dve.wait_ge(S["z_in"], 16 * (t + 1))
                d = rdeg1[:, bass.ds(t, 1)]
                link(v.scalar_tensor_tensor(zi[:, :], counts_ps[:, s, 0:D], d, zi[:, :], ALU.mult, ALU.add))
                dve.wait_ge(S["nrm_tr"], t + NT)
                v.scalar_tensor_tensor(nrm[:, :], counts_ps[:, s, D:2 * D], d, zi[:, :], ALU.mult, ALU.add
                                       ).then_inc(S["h_in"], 1)

            def phase2_split(t, first=False):
                if first:
                    dve.wait_ge(S["z_out"], 16 * NT)
                else:
                    dve.wait_ge(S["y2_out"], 32 * t)
                split_y(t + NT, (yo[:, 0:D], yo[:, D:2 * D]), b2b[:, :], s2)

            phase2(0, 0)
            phase2(1, 1)
            phase2_split(0, True)
            phase2(2, 0)
            phase2_split(1)
            per = 2
            with dve.Fori(1, NT // 2) as i:
                start = count[0]
                base[0] = (i - 1) * per
                for q in range(2):
                    phase2(i * 2 + (q + 1), (q + 1) % 2)
                    phase2_split(i * 2 + q)
                assert count[0] - start == per
            base[0] = 0
            count[0] += per * (NT // 2 - 2)
            phase2_split(NT - 1)

            dve.wait_ge(S["counted"], NGROUP)
            dve.wait_ge(S["projected"], 2 * NT)
            v.memset(node[:, 0:AHEAD], 0.0)
            link(v.memset(node[:, AHEAD:], 1.0))
            v.memset(before[:, 0:1, :], 0.0)
            v.memset(tri, 1.0).then_inc(S["tri_in"], 1)
            dve.wait_ge(S["iota"], 8)
            link(v.tensor_copy(iota_e, iota_ei))
            link(v.tensor_scalar(base_e, iota_e, float(REGION), None, ALU.mult))
            link(v.tensor_scalar(rdeg[:, :], rdeg[:, :], i2, None, ALU.mult))

            dve.sem_inc(S["sums_free"], 1)

            def x2_and_norm(t, s, k, alone=False):
                dve.wait_ge(S["z_in"], 16 * (t + 1 + NT))
                dve.wait_ge(S["x_in"], 16 * (t + 1 + NT))
                if not alone:
                    dve.wait_ge(S["u_ready"], t)
                v.tensor_tensor(zt[:, :], zi[:, :], xt[:, :], ALU.add).then_inc(S["zx_taken"], 1)
                dve.wait_ge(S["zx_taken"], t + 1)
                dve.wait_ge(S["agg"], t + 1 + NT)
                d = rdeg[:, bass.ds(t, 1)]
                link(v.scalar_tensor_tensor(zt[:, :], counts_ps[:, s, 0:D], d, zt[:, :], ALU.mult, ALU.add))
                v.scalar_tensor_tensor(zt[:, :], counts_ps[:, s, D:2 * D], d, zt[:, :], ALU.mult, ALU.add
                                       ).then_inc(S["sums_free"], 1)
                dve.wait_ge(S["sums_free"], t + 2)
                link(v.bn_stats(stat[:, 0:6], zt[:, :]))
                dve.sem_inc(S["held"], 1)
                link(v.bn_aggr(stat[:, 6:8], stat[:, 0:6]))
                v.tensor_scalar(stat[:, 9:10], stat[:, 7:8], EPS, None, ALU.add).then_inc(S["var_in"], 1)
                dve.wait_ge(S["tok_free"], t + 1)
                dve.wait_ge(S["rstd_in"], t + 1 + NT)
                v.tensor_scalar(tok[k], zt[:, :], stat[:, 6:7], stat[:, 8:9], ALU.subtract, ALU.mult
                                ).then_inc(S["normed"], 1)
                dve.wait_ge(S["normed"], t + 1 + NT)
                if not alone:
                    dve.wait_ge(S["u_out"], t * 16)
                v.tensor_tensor(uo, zt[:, :], tok[k], ALU.add).then_inc(S["u_ready"], 1)

            def each(a, n):
                return a.rearrange("p (t a) -> p t a", a=1).to_broadcast((P, a.shape[1], n))

            def choose(j):
                dve.wait_ge(S["logits"], j * BATCH + 1)
                v.tensor_copy(lg, bank[1][:, 0:BATCH * NE].rearrange("p (t e) -> p t e", e=NE)
                              ).then_inc(S["logits_in"], 1)
                dve.wait_ge(S["logits_in"], j + 1)
                dve.sem_inc(S["held"], 1)
                for q in range(BATCH):
                    last = v.max(mx[:, q, :], lg[:, q, :])
                link(last)
                v.tensor_tensor(less, mx, mx[:, :, 0:1].to_broadcast((P, BATCH, NE)), ALU.subtract
                                ).then_inc(S["top"], 1)
                for q in range(BATCH):
                    last = v.max_index(mix[:, q, :], mx[:, q, :], lg[:, q, :])
                link(last)
                link(v.tensor_copy(pick, mix[:, :, 0:TOPK]))
                link(v.tensor_tensor(mask, iota_e.rearrange("p (a e) -> p a e", a=1).to_broadcast((P, BATCH * TOPK, NE)),
                                     each(pick.rearrange("p t k -> p (t k)"), NE), ALU.is_equal))
                by_rank = mask.rearrange("p (t k) e -> p t k e", k=TOPK)
                link(v.tensor_tensor(both, by_rank[:, :, 0, :], by_rank[:, :, 1, :], ALU.add))
                link(v.tensor_tensor(both, both, each(node[:, bass.ds(j * BATCH, BATCH)], NE), ALU.mult))
                v.tensor_copy(pairs_of[:, 0:1, :], both[:, 0:1, :])
                link(v.tensor_tensor(pairs_of[:, 1:, :], both[:, 1:, :], both[:, 0:BATCH - 1, :], ALU.add))
                v.tensor_copy(before[:, 1:3, :], pairs_of[:, 0:2, :])
                v.tensor_tensor(before[:, 3:5, :], pairs_of[:, 2:4, :], pairs_of[:, 0:2, :], ALU.add
                                ).then_inc(S["masks"], 1)
                dve.wait_ge(S["expd"], j + 1)
                link(v.tensor_reduce(esum, ex, AX.X, ALU.add))
                link(v.reciprocal(resum, esum))
                link(v.tensor_tensor(prob, ex[:, :, 0:TOPK], each(resum, TOPK), ALU.mult))
                link(v.tensor_reduce(esum, prob, AX.X, ALU.add))
                link(v.tensor_scalar(esum, esum, 1e-12, None, ALU.max))
                link(v.reciprocal(resum, esum))
                v.tensor_tensor(coef[:, bass.ds(j * BATCH, BATCH), :], prob, each(resum, TOPK), ALU.mult)

            def place(j, s):
                dve.wait_ge(S["prefix"], j + 1)
                link(v.tensor_tensor(pos, bank[3][:, 0:BATCH * NE].rearrange("p (t e) -> p t e", e=NE),
                                     base_e.rearrange("p (a e) -> p a e", a=1).to_broadcast((P, BATCH, NE)), ALU.add))
                v.tensor_tensor(base_e, base_e, bank[3][:, BATCH * NE:(BATCH + 1) * NE], ALU.add)
                for k in range(TOPK):
                    last = v.tensor_tensor(posm.rearrange("p (t k) e -> p t k e", k=TOPK)[:, :, k, :],
                                           mask.rearrange("p (t k) e -> p t k e", k=TOPK)[:, :, k, :], pos, ALU.mult)
                link(last)
                link(v.tensor_reduce(slot_f, posm, AX.X, ALU.add))
                v.tensor_copy(slots[:, bass.ds(j * BATCH * TOPK, BATCH * TOPK)], slot_f)
                v.tensor_copy(slot_u[s], slot_f).then_inc(S["slots"], 1)

            x2_and_norm(0, 0, 0, True)
            with dve.Fori(0, (NT - 1) // RING8) as i:
                start = count[0]
                base[0] = i * PER3
                for r in range(1, RING8 + 1):
                    x2_and_norm(i * RING8 + r, r % 2, r % RING8)
                    for half in range(2):
                        if r == half * BATCH + 1:
                            choose(i * 2 + half)
                        if r == half * BATCH + 2:
                            place(i * 2 + half, half)
                assert count[0] - start == PER3, count[0] - start
            base[0] = 0
            count[0] += PER3 * ((NT - 1) // RING8 - 1)
            choose(NB - 1)
            place(NB - 1, 0)
            dve.wait_ge(S["agg"], 2 * NT)
            v.memset(zero_t, 0.0).then_inc(S["zeros"], 1)
            link(v.tensor_copy(end_i, base_e))
            link(v.scalar_tensor_tensor(cnt, iota_e, -float(REGION), base_e, ALU.mult, ALU.add))
            link(v.tensor_scalar(nt_i, cnt, float(P - 1), None, ALU.add))
            link(v.tensor_scalar(nt_i, nt_i, P.bit_length() - 1, None, ALU.logical_shift_right))
            link(v.tensor_copy(cum[0], nt_i))
            for n, d in enumerate((1, 2, 4)):
                v.tensor_copy(cum[n + 1][:, 0:d], cum[n][:, 0:d])
                link(v.tensor_tensor(cum[n + 1][:, d:NE], cum[n][:, d:NE], cum[n][:, 0:NE - d], ALU.add))
            total = cum[3][:, NE - 1:NE]
            link(v.tensor_scalar(first_row[:, 1:NE], cum[3][:, 0:NE - 1], -float(P), None, ALU.mult))
            link(v.memset(first_row[:, 0:1], 0.0))
            link(v.scalar_tensor_tensor(first_row, iota_e, float(REGION), first_row, ALU.mult, ALU.add))
            link(v.tensor_tensor(jump[:, 0:NE - 1], first_row[:, 1:NE], first_row[:, 0:NE - 1], ALU.subtract))
            link(v.tensor_copy(jf, iota_j))
            link(v.tensor_scalar(tab_r, jf, float(P), None, ALU.mult))
            link(v.memset(tab_e, 0.0))
            for e in range(NE - 1):
                v.tensor_scalar(past, jf, cum[3][:, e:e + 1], None, ALU.is_ge)
                link(v.tensor_scalar(stay, jf, cum[3][:, e:e + 1], jump[:, e:e + 1], ALU.is_ge, ALU.mult))
                v.tensor_tensor(tab_e, tab_e, past, ALU.add)
                link(v.tensor_tensor(tab_r, tab_r, stay, ALU.add))
            link(v.tensor_scalar(stay, jf, total, None, ALU.is_lt))
            v.tensor_scalar(past, jf, total, None, ALU.is_ge)
            link(v.tensor_copy(cnt[:, 0:1], tab_e[:, 0:1]))
            link(v.tensor_copy(cnt[:, 1:2], tab_r[:, 0:1]))
            v.tensor_tensor(tab_e, tab_e, stay, ALU.mult)
            link(v.tensor_tensor(tab_r, tab_r, stay, ALU.mult))
            link(v.scalar_tensor_tensor(tab_ef, past, cnt[:, 0:1], tab_e, ALU.mult, ALU.add))
            of_pair = tab_ef.rearrange("p (i h) -> p i h", h=2)
            v.scalar_tensor_tensor(tab_ei, of_pair[:, :, 1:2].rearrange("p i h -> p (i h)"), float(NE),
                                   of_pair[:, :, 0:1].rearrange("p i h -> p (i h)"), ALU.mult, ALU.add)
            link(v.scalar_tensor_tensor(tab_ri, past, cnt[:, 1:2], tab_r, ALU.mult, ALU.add))
            v.tensor_scalar(ends_i[:, 0:1], total, float(P), None, ALU.mult)
            link(v.tensor_scalar(npair_i[:, 1:2], total, 1.0, None, ALU.add))
            v.tensor_scalar(npair_i[:, 0:1], npair_i[:, 1:2], 1, None, ALU.logical_shift_right).then_inc(S["table"], 1)

            link(v.tensor_copy(slots_f, slots))
            for e in range(1, NE):
                link(v.tensor_scalar(moved, slots_f, float(e * REGION), jump[:, e - 1:e], ALU.is_ge, ALU.mult))
                if e == 1:
                    kept = slots_f
                link(v.tensor_tensor(place_f[e % 2], kept, moved, ALU.subtract))
                kept = place_f[e % 2]
            v.tensor_copy(slots_y.rearrange("p t k -> p (t k)"), kept)

            dve.wait_ge(S["ew_in"], 16 * 4 * NE)
            dve.wait_ge(S["table"], 1)
            pairs = dve.value_load(npair_i[0:1, 0:1], min_val=MIN_PAIRS, max_val=(MAX_TILES + 1) // 2)

            def experts_of(i):
                both_of = dve.value_load(tab_ei[0:1, bass.ds(i, 1)], min_val=0, max_val=NE * NE - 1)
                return both_of % NE, both_of // NE

            def hidden(i, es):
                for h in range(2):
                    dve.wait_ge(S["hid"], i * 2 + h + 1)
                    v.tensor_tensor(hb[h], counts_ps[:, 2 + h, 0:D], ew(eb_sb, es[h], 0), ALU.add
                                    ).then_inc(S["hb_in"], 1)

            def result(i, es, first=False):
                for h in range(2):
                    dve.wait_ge(S["ye_ps"], i * 2 + h + 1)
                    if not first:
                        dve.wait_ge(ye_out[h], i * 16)
                    v.tensor_tensor(ye[h], bank[2 + h][:, 0:D], ew(eb_sb, es[h], 1), ALU.add).then_inc(S["ye_in"], 1)

            dve.sem_inc(S["ye_in"], 2)
            hidden(0, experts_of(0))
            hidden(1, experts_of(1))
            result(0, experts_of(0), True)
            with dve.Fori(1, pairs) as i:
                hidden(i + 1, experts_of(i + 1))
                result(i, experts_of(i))

            def indices(t, s):
                link(v.tensor_copy(gix[:, s, :], slots_y[:, bass.ds(t + AHEAD, 1), :].rearrange("p a k -> p (a k)")))
                v.memset(stat[:, 14:15], 0.0).then_inc(S["gix_in"], 1)

            def combine(t, s, turn, more=True, first=False):
                dve.wait_ge(yg_in[s], turn * (16 * TOPK) + 16 * TOPK)
                dve.wait_ge(ug_in[s], turn * 16 + 16)
                if not first:
                    dve.wait_ge(sum_out_of[s], turn * 16)
                for k in range(TOPK):
                    ins = v.scalar_tensor_tensor(og[:, s, :], yg[:, s * TOPK + k, :],
                                                 coef[:, bass.ds(t + AHEAD, 1), k:k + 1].rearrange("p a k -> p (a k)"),
                                                 ug[:, s, :] if k == 0 else og[:, s, :], ALU.mult, ALU.add)
                    if k == 0:
                        link(ins)
                ins.then_inc(S["og_in"], 1)
                if more:
                    indices(t + RING, s)

            for t in range(RING):
                indices(t, t)
            for t in range(RING):
                combine(t, t, 0, True, True)
            combine(RING, 0, 1)
            with dve.Fori(1, NT // RING - 1) as i:
                start = count[0]
                base[0] = (i - 1) * (2 * RING)
                for q in range(RING):
                    combine(i * RING + (q + 1), (q + 1) % RING, i + (q + 1) // RING)
                assert count[0] - start == 2 * RING
            base[0] = 0
            count[0] += 2 * RING * (NT // RING - 3)
            for t in range(NT - RING, NT):
                combine(t, t % RING, t // RING, False)

        @block.tensor
        def _(pe):
            te = nc.tensor
            pe.wait_ge(S["consts"], 2)
            pe.wait_ge(S["first_ge"], 1)
            for k in range(NG):
                for j in range(FIRSTS):
                    last = te.matmul(bank[2][0:WPP, k:k + 1], below[:, j, k * WPP:(k + 1) * WPP], ones[0:NCH, 0:1],
                                     start=(j == 0), stop=(j == FIRSTS - 1))
            last.then_inc(S["firsts"], 1)
            pe.wait_ge(S["wsq"], 2)
            for q, b in zip(wsq, (bank[3], bank[1])):
                for k in range(KD):
                    last = te.matmul(b[:, :], ones[:, :], q[:, k, :], start=(k == 0), stop=(k == KD - 1))
                last.then_inc(S["wnorm"], 1)
            pe.wait_ge(S["keys"], 1)
            pe.wait_ge(S["iota"], 4)
            pe.wait_ge(S["wsum"], 1)
            for to, a in ((bank, rel), ((counts_ps[:, 0], counts_ps[:, 1]), key1),
                          ((counts_ps[:, 2], counts_ps[:, 3]), lo1)):
                for k in range(NG):
                    last = te.transpose(to[k // HALF][0:RUN, k % HALF * WPP:(k % HALF + 1) * WPP], a[:, k, :],
                                        ident[0:WPP, 0:WPP])
            last.then_inc(S["keys_tr"], 1)
            pe.wait_ge(S["deg_eq"], 1)
            for t in range(NT):
                last = te.matmul(bank[2][:, t:t + 1],
                                 deg_eq[:, t * P // WD:(t + 1) * P // WD, :].rearrange("p w d -> p (w d)"),
                                 one_h[0:RUN, :], start=True, stop=True)
            last.then_inc(S["deg_counted"], 1)

            def transposes(t):
                for k in range(KD):
                    last = te.transpose(bank[0][:, k * P:(k + 1) * P], nrm[:, k * P:(k + 1) * P], ident[:, :])
                last.then_inc(S["nrm_tr"], 1)

            def project_half(t, k, first=False):
                if k == 0:
                    pe.wait_ge(S["nrm_t_in"], t + 1)
                    if not first:
                        pe.wait_ge(S["yz_in"], t)
                last = te.matmul(bank[1][:, :], nrm_t[:, k * P:(k + 1) * P], w[:, k, :],
                                 start=(k == 0), stop=(k == KD - 1))
                if k == KD - 1:
                    last.then_inc(S["projected"], 1)

            def project(t):
                for k in range(KD):
                    project_half(t, k)

            def counts(group, slot, fresh):
                if fresh:
                    pe.wait_ge(S["scaled"], 1)
                else:
                    pe.wait_ge(S["adj_in"], group - 1)
                group_counts(pe, group, slot)

            def phase1(t, first=False, groups=TILE_GROUPS):
                for q in range(groups):
                    counts(t * TILE_GROUPS + q, q % 2, first and q < 2)
                    if q == 1:
                        pe.wait_ge(S["normed"], t + 1)
                        if not first:
                            pe.wait_ge(S["nrm_t_in"], t)
                        transposes(t)
                    if q >= 2:
                        project_half(t, q - 2, first)
                if groups == 2:
                    project(t)

            phase1(0, True)
            with pe.Fori(1, NT - 1) as t:
                phase1(t)
            phase1(NT - 1, groups=NGROUP - (NT - 1) * TILE_GROUPS)

            def aggregate(t, s, mid=None, at=NT // 3, mid2=None, ready=None):
                for b in range(NT):
                    if ready is not None:
                        ready(b)
                    if mid is not None and b == at:
                        mid()
                    if mid2 is not None and b == NT // 4 * 3:
                        mid2()
                    last = te.matmul(counts_ps[:, s, :], adj[:, b, bass.ds(t * P, P)], y[:, b, :],
                                     start=(b == 0), stop=(b == NT - 1))
                last.then_inc(S["agg"], 1)

            def phase2(t, s, fresh=False, first=False):
                if not fresh:
                    pe.wait_ge(S["h_in"], t - 1)

                def mid():
                    pe.wait_ge(S["h_in"], t)
                    pe.wait_ge(S["nrm_t_in"], t + NT - 1)
                    transposes(t + NT - 1)
                aggregate(t, s, None if first else mid)
                if not first:
                    project(t + NT - 1)

            pe.wait_ge(S["flag_out"], 1)
            with pe.If(pe.value_load(flag_i[0:1, 0:1], min_val=0, max_val=1) == 1):
                pe.wait_ge(S["adj_in"], NGROUP)
                pe.sem_inc(S["all_counted"], 2)
                with pe.Fori(0, NW) as wi:
                    pe.wait_ge(S["all_kept"], wi + 1)
                    pe.wait_ge(S["all_onehot"], wi * STEPS + 1)
                    te.matmul(counts_ps[:, 0, 0:KEYS], zero_h, all_iota[:, 0:KEYS], start=True, stop=False)
                    with pe.Fori(0, STEPS // 2) as i:
                        for q in range(2):
                            pe.wait_ge(S["all_onehot"], wi * STEPS + i * 2 + (q + 1))
                            for c in range(STEP):
                                last = te.matmul(counts_ps[:, 0, 0:KEYS], all_src[:, q, c, :],
                                                 all_key[:, q, c, :], start=False, stop=False)
                            last.then_inc(S["all_counted"], 1)
                    te.matmul(counts_ps[:, 0, 0:KEYS], zero_h, all_iota[:, 0:KEYS], start=False, stop=True
                              ).then_inc(S["all_window"], 1)
                pe.wait_ge(S["all_kept"], NW + 1)
                with pe.Fori(0, NT) as t:
                    for b in range(NT):
                        last = te.matmul(bank[2][:, bass.ds(t, 1)], adj[:, b, bass.ds(t * P, P)], one_h[:, :],
                                         start=(b == 0), stop=(b == NT - 1))
                    last.then_inc(S["all_degrees"], 1)
            pe.wait_ge(S["w_in"], 128)
            pe.wait_ge(S["adj_in"], NGROUP)
            pe.wait_ge(S["yz_in"], NT)
            phase2(0, 0, True, True)
            phase2(1, 1, True)
            phase2(2, 0)
            with pe.Fori(1, NT // 2) as i:
                for q in range(2):
                    phase2(i * 2 + (q + 1), (q + 1) % 2)
            pe.wait_ge(S["h_in"], NT)
            pe.wait_ge(S["nrm_t_in"], 2 * NT - 1)
            transposes(2 * NT - 1)
            project(2 * NT - 1)

            def route(t, k, step, read=None):
                if step == 0:
                    pe.wait_ge(S["normed"], t + 1 + NT)
                    pe.wait_ge(S["nrm_t_in"], t + 2 * NT)
                    for c in range(KD):
                        last = te.transpose(bank[0][:, c * P:(c + 1) * P], tok[k][:, c * P:(c + 1) * P], ident[:, :])
                    last.then_inc(S["nrm_tr"], 1)
                if step == 1:
                    q = (k + AHEAD) % BATCH
                    pe.wait_ge(S["nrm_t_in"], t + 1 + 2 * NT)
                    if q == 0:
                        pe.wait_ge(S["logits_in"], read)
                    for c in range(KD):
                        last = te.matmul(bank[1][:, q * NE:(q + 1) * NE], nrm_t[:, c * P:(c + 1) * P], rw_t[:, c, :],
                                         start=(c == 0), stop=(c == KD - 1))
                    last.then_inc(S["logits"], 1)

            def prefix(j):
                pe.wait_ge(S["masks"], j + 1)
                te.matmul(bank[3][:, 0:BATCH * NE], tri, both.rearrange("p t e -> p (t e)"), start=True, stop=False)
                te.matmul(bank[3][:, 0:BATCH * NE], ones[:, :], before[:, 0:BATCH, :].rearrange("p t e -> p (t e)"),
                          start=False, stop=True)
                te.matmul(bank[3][:, BATCH * NE:(BATCH + 1) * NE], ones[:, :],
                          before[:, BATCH:, :].rearrange("p t e -> p (t e)"), start=True, stop=True
                          ).then_inc(S["prefix"], 1)

            def first_reads(b):
                if b % (NT // NQ) == 0:
                    pe.wait_ge(y2_in[b // (NT // NQ)], 16)

            aggregate(0, 0, ready=first_reads)
            pe.wait_ge(S["rw_in"], 16 * KD)
            pe.wait_ge(S["iota"], 8)
            with pe.Fori(0, (NT - 1) // RING8) as i:
                for r in range(1, RING8 + 1):
                    pe.wait_ge(S["sums_free"], i * RING8 + r)
                    read = i * 2 + (r + 2) // BATCH
                    aggregate(i * RING8 + r, r % 2,
                              lambda: route(i * RING8 + (r - 1), r - 1, 0), NT // 2,
                              lambda: route(i * RING8 + (r - 1), r - 1, 1, read))
                    if r % BATCH == 2:
                        prefix(i * 2 + r // BATCH)
            for step in range(2):
                route(NT - 1, 0, step)
            prefix(NB - 1)

            def turn_rows(i):
                for h in range(2):
                    pe.wait_ge(xe_in[h], i * 16 + 16)
                    for k in range(KD):
                        last = te.transpose(counts_ps[:, h, k * P:(k + 1) * P], xe[h][:, k * P:(k + 1) * P], ident[:, :])
                last.then_inc(S["xe_tr"], 1)

            pe.wait_ge(S["table"], 1)
            pairs = pe.value_load(npair_i[0:1, 0:1], min_val=MIN_PAIRS, max_val=(MAX_TILES + 1) // 2)
            turn_rows(0)
            pe.wait_ge(S["ew_in"], 16 * 4 * NE)

            def experts_of(i):
                both_of = pe.value_load(tab_ei[0:1, bass.ds(i, 1)], min_val=0, max_val=NE * NE - 1)
                return both_of % NE, both_of // NE

            def hidden(i, es):
                for h in range(2):
                    pe.wait_ge(S["xe_t_in"], i * 2 + h + 1)
                    for k in range(KD):
                        last = te.matmul(counts_ps[:, 2 + h, 0:D], xe_t[h][:, k * P:(k + 1) * P], ew(ew1_sb, es[h], k),
                                         start=(k == 0), stop=(k == KD - 1))
                    last.then_inc(S["hid"], 1)

            def turn_hidden(i):
                for h in range(2):
                    pe.wait_ge(S["ge_in"], i * 2 + h + 1)
                    for k in range(KD):
                        last = te.transpose(bank[h][:, k * P:(k + 1) * P], ge[h][:, k * P:(k + 1) * P], ident[:, :])
                    last.then_inc(S["ge_tr"], 1)

            def result(i, es):
                for h in range(2):
                    pe.wait_ge(S["ge_t_in"], i * 2 + h + 1)
                    pe.wait_ge(S["ye_in"], i * 2 + h + 1)
                    for k in range(KD):
                        last = te.matmul(bank[2 + h][:, 0:D], ge_t[h][:, k * P:(k + 1) * P], ew(ew2_sb, es[h], k),
                                         start=(k == 0), stop=(k == KD - 1))
                    last.then_inc(S["ye_ps"], 1)

            hidden(0, experts_of(0))
            turn_rows(1)
            turn_hidden(0)
            hidden(1, experts_of(1))
            with pe.Fori(0, pairs) as i:
                result(i, experts_of(i))
                turn_rows(i + 2)
                es = experts_of(i + 2)
                turn_hidden(i + 1)
                hidden(i + 2, es)

        @block.scalar
        def _(act):
            a = nc.scalar
            act.wait_ge(S["wsum"], 1)
            a.activation(scl[:, 8:13], scl[:, 0:5], ACT.Sqrt).then_inc(S["wroot"], 1)
            act.wait_ge(S["scaled"], 1)
            act.wait_ge(S["deg_counted"], 1)

            def turn(t, func):
                act.wait_ge(S["nrm_tr"], t + 1)
                act.wait_ge(S["projected"], t)
                a.activation(nrm_t[:, :], bank[0][:, 0:D], func).then_inc(S["nrm_t_in"], 1)

            def high(t, to, scale):
                act.wait_ge(S["projected"], t + 1)
                a.activation(to, bank[1][:, 0:D], ACT.Copy, scale=scale).then_inc(S["hi_in"], 1)

            def phase1(t, first=False, groups=TILE_GROUPS):
                for q in range(groups):
                    group_keep(act, t * TILE_GROUPS + q, q % 2)
                    if q == 1:
                        if first:
                            act.wait_ge(S["nrm_tr"], 1)
                            a.activation(nrm_t[:, :], bank[0][:, 0:D], ACT.Copy).then_inc(S["nrm_t_in"], 1)
                        else:
                            turn(t, ACT.Copy)
                    if q == groups - 1:
                        high(t, y[:, bass.ds(t, 1), D:2 * D].rearrange("p a n -> p (a n)"),
                             scl_i[:, 8:9].bitcast(F32))

            phase1(0, True)
            with act.Fori(1, NT - 1) as t:
                phase1(t)
            phase1(NT - 1, groups=NGROUP - (NT - 1) * TILE_GROUPS)

            act.wait_ge(S["flag_out"], 1)
            with act.If(act.value_load(flag_i[0:1, 0:1], min_val=0, max_val=1) == 1):
                act.sem_inc(S["all_kept"], 1)
                with act.Fori(0, NW) as wi:
                    act.wait_ge(S["all_window"], wi + 1)
                    a.activation(adj[:, :, bass.ds(wi * WD, WD)],
                                 counts_ps[:, 0, 0:KEYS].rearrange("p (b d) -> p b d", d=WD), ACT.Copy
                                 ).then_inc(S["all_kept"], 1)
                act.wait_ge(S["all_kept"], NW + 1)
                act.sem_inc(S["all_done"], 1)

            def phase2(t, first=False):
                turn(t + NT, ACT.Relu)
                if not first:
                    act.wait_ge(S["y2_out"], 32 * t)
                high(t + NT, yo[:, D:2 * D], scl_i[:, 9:10].bitcast(F32))

            phase2(0, True)
            with act.Fori(1, NT) as t:
                phase2(t)

            def phase3(t):
                act.wait_ge(S["nrm_tr"], t + 1 + 2 * NT)
                a.activation(nrm_t[:, :], bank[0][:, 0:D], ACT.Copy).then_inc(S["nrm_t_in"], 1)

            def powers(j):
                act.wait_ge(S["top"], j + 1)
                a.activation(ex, less, ACT.Exp).then_inc(S["expd"], 1)

            act.wait_ge(S["counted"], NGROUP)
            with act.Fori(0, (NT - 1) // RING8) as i:
                for r in range(RING8):
                    phase3(i * RING8 + r)
                    if r % BATCH == 1:
                        powers(i * 2 + r // BATCH)
            phase3(NT - 1)
            powers(NB - 1)

            act.wait_ge(S["table"], 1)
            pairs = act.value_load(npair_i[0:1, 0:1], min_val=MIN_PAIRS, max_val=(MAX_TILES + 1) // 2)

            def turn_rows():
                for h in range(2):
                    a.activation(xe_t[h], counts_ps[:, h, 0:D], ACT.Copy).then_inc(S["xe_t_in"], 1)

            a.activation(scl[:, 14:15], scl[:, 8:9], ACT.Gelu)

            def gelu(i):
                for h in range(2):
                    act.wait_ge(S["hb_in"], i * 2 + h + 1)
                    a.activation(ge[h], hb[h], ACT.Gelu).then_inc(S["ge_in"], 1)

            act.wait_ge(S["xe_tr"], 1)
            turn_rows()
            gelu(0)
            act.wait_ge(S["xe_tr"], 2)
            turn_rows()
            with act.Fori(0, pairs) as i:
                for h in range(2):
                    act.wait_ge(S["ge_tr"], i * 2 + h + 1)
                    a.activation(ge_t[h], bank[h][:, 0:D], ACT.Copy).then_inc(S["ge_t_in"], 1)
                gelu(i + 1)
                act.wait_ge(S["xe_tr"], i + 3)
                turn_rows()


_INS = ["x", "src", "dst", "L0_gnn_W1_l", "L0_gnn_W1_r", "L0_gnn_b1", "L0_gnn_W2_l", "L0_gnn_W2_r", "L0_gnn_b2",
        "L0_ffn_router_w", "L0_ffn_w1", "L0_ffn_b1", "L0_ffn_w2", "L0_ffn_b2"]


def kernel(**inputs):
    import numpy as _np
    import concourse.bacc as _bacc
    from concourse import mybir as _mybir
    from concourse.bass_utils import run_bass_kernel_spmd as _run

    nc = _bacc.Bacc("TRN2", target_bir_lowering=False, num_devices=1)
    arrays, args = {}, []
    for name in _INS:
        a = _np.ascontiguousarray(inputs[name])
        arrays[f"in_{name}"] = a
        args.append(nc.dram_tensor(f"in_{name}", a.shape, _mybir.dt.from_np(a.dtype), kind="ExternalInput").ap())
    out = nc.dram_tensor("out_0", arrays["in_x"].shape, F32, kind="ExternalOutput").ap()
    with nc.allow_non_contiguous_dma(reason="a few first elements and columns"):
        build(nc, *args, out)
    r = _run(nc, [arrays], core_ids=[0])
    return r.results[0]["out_0"]
```

```python
from contextlib import ExitStack

import concourse.bass as bass
from concourse import mybir

F32 = mybir.dt.float32
F16 = mybir.dt.float16
I32 = mybir.dt.int32
U32 = mybir.dt.uint32
ALU = mybir.AluOpType
ACT = mybir.ActivationFunctionType
AX = mybir.AxisListType
RMAX = bass.bass_isa.ReduceOp.max

P = 128
EPS = 1e-5
EXPONENT_AT = 23


def build(nc, x, src, dst, w1l, w1r, b1, w2l, w2r, b2, router_w, ew1, eb1, ew2, eb2, out):
    N, D = x.shape
    E = src.shape[0]
    KD = D // P
    NT = -(-N // P)
    LAST = N - (NT - 1) * P
    WD = 4
    KEYS = NT * WD
    GW = 8
    HALF = 4
    TILE_GROUPS = P // (GW * WD)
    NW = -(-N // (GW * WD)) * GW
    NGROUP = NW // GW
    WPP = 112
    NG = NW // WPP
    PARTS = ((0, 4), (4, NG))
    RUN = 125
    FIRSTS = 4
    CHUNK = FIRSTS * RUN
    NCH = E // CHUNK
    ALL_COLS = 400
    ALL_ROWS = E // ALL_COLS
    AC = NT * P
    NE = router_w.shape[0]
    TOPK = 2
    BATCH = 4
    AHEAD = BATCH - 1
    NB = (NT + AHEAD) // BATCH
    KEPT = 2 * BATCH
    REGION = N + P + (-(N + P)) % 16
    MAX_TILES = (TOPK * N) // P + NE
    MIN_TILES = (TOPK * N) // P
    YS_TILES = MAX_TILES + 1
    SPARE = YS_TILES - MIN_TILES
    MIN_PAIRS = (TOPK * N) // P // 2
    NTAB = MAX_TILES + 6
    assert NCH <= P and NCH * CHUNK == E and ALL_ROWS <= P and ALL_ROWS * ALL_COLS == E
    assert NB * BATCH == NT + AHEAD and (NT - 1) % KEPT == 0
    assert NW == NG * WPP and N <= NW * WD <= AC and KEYS <= P and GW == 2 * HALF and HALF * P == 512

    with ExitStack() as ctx:
        def sb(name, shape, dt):
            return ctx.enter_context(nc.sbuf_tensor(name, shape, dt))

        def sem(name):
            return ctx.enter_context(nc.semaphore(name))

        bank = [ctx.enter_context(nc.psum_tensor(f"bank{i}", [P, 512], F32)) for i in range(4, 8)]
        counts_ps = ctx.enter_context(nc.psum_tensor("counts_ps", [P, 4, 512], F32))

        z1_dram = nc.dram_tensor("z1_dram", (NT * P, D), F32, kind="Internal").ap()
        z2_dram = nc.dram_tensor("z2_dram", (NT * P, D), F32, kind="Internal").ap()
        y2_dram = nc.dram_tensor("y2_dram", (NT * P, 2 * D), F16, kind="Internal").ap()
        u_dram = nc.dram_tensor("u_dram", (NT * P, D), F32, kind="Internal").ap()
        xs_dram = nc.dram_tensor("xs_dram", (NE * REGION, D), F32, kind="Internal").ap()
        ys_dram = nc.dram_tensor("ys_dram", ((YS_TILES + SPARE) * P, D), F32, kind="Internal").ap()
        ys_rows = ys_dram[0:YS_TILES * P, :]

        adj = sb("adj", [P, NT, AC], F16)
        y = sb("y", [P, NT, 2 * D], F16)
        w = sb("w", [P, KD, 2 * D], F32)
        b1b = sb("b1b", [P, D], F32)
        b2b = sb("b2b", [P, D], F32)
        ident = sb("ident", [P, P], F32)
        ones = sb("ones", [P, P], F32)
        one_h = sb("one_h", [P, 1], F16)
        iota_4 = sb("iota_4", [P, P, HALF], F16)
        onehots = sb("onehots", [P, 2 * GW * (P + KEYS)], F16)
        oh_src = onehots[:, 0:2 * GW * P].rearrange("p (s c) -> p s c", s=2)
        oh_key = onehots[:, 2 * GW * P:].rearrange("p (s c) -> p s c", s=2)
        key_t = sb("key_t", [P, 2 * ALL_COLS], F16)
        lo_t = sb("lo_t", [P, 2 * ALL_COLS], F16)
        rows = sb("rows", [P, 4 * D], F32)
        xt, nrm, nrm_t, zi = (rows[:, k * D:(k + 1) * D] for k in range(4))
        zt = sb("zt", [P, D], F32)
        yo = sb("yo", [P, 2 * D], F16)
        stat = sb("stat", [P, 16], F32)
        rdeg = sb("rdeg", [P, NT], F32)
        rdeg1 = sb("rdeg1", [P, NT], F32)
        scl = sb("scl", [P, 16], F32)
        scl_i = sb("scl_i", [P, 16], I32)
        flag = sb("flag", [P, 16], F32)
        flag_all = sb("flag_all", [P, 16], F32)
        flag_i = sb("flag_i", [P, 2], I32)

        edge_i = rows[0:ALL_ROWS, 0:ALL_COLS].bitcast(I32)
        edge_lo = rows[0:ALL_ROWS, 2 * D:2 * D + ALL_COLS]
        edge_dst = key_t[0:ALL_ROWS, :].bitcast(F32)
        edge_blk = lo_t[0:ALL_ROWS, :].bitcast(F32)
        w_flat = w[:, :, :].rearrange("p k n -> p (k n)")
        edge_key = w_flat[0:ALL_ROWS, 0:ALL_COLS]
        edge_rel = w_flat[0:ALL_ROWS, ALL_COLS:2 * ALL_COLS]
        zero_h = yo[0:ALL_ROWS, 0:P]
        window_at = stat[0:ALL_ROWS, 15:16]
        STEP = 4
        STEPS = ALL_COLS // STEP
        all_src = oh_src[0:ALL_ROWS, :, 0:STEP * P].rearrange("p s (c k) -> p s c k", c=STEP)
        all_key = oh_key[0:ALL_ROWS, :, 0:STEP * KEYS].rearrange("p s (c k) -> p s c k", c=STEP)
        all_iota = iota_4[0:ALL_ROWS, :, 0:1].rearrange("p k a -> p (k a)")

        used = [0]
        adj_flat = adj[:, :, :].rearrange("p b c -> p (b c)")

        def early(shape, dt, parts=P):
            n = 1 if dt is F16 else 2
            for d in shape:
                n *= d
            a = adj_flat[0:parts, used[0]:used[0] + n].bitcast(dt)
            used[0] += n + n % 2
            assert used[0] <= NT * AC - AC
            return a.rearrange("p (a b) -> p a b", b=shape[1]) if len(shape) == 2 else a

        dchunk = early([CHUNK], I32, NCH)
        dchunk_f = early([CHUNK], F32, NCH)
        dnext = early([2], I32, NCH)
        dnext_f = early([2], F32, NCH)
        falls = early([CHUNK], F32, NCH)
        wstart = early([NW], I32, NCH)
        below = early([FIRSTS, NW], F16, NCH)
        wlo_i = early([NG], I32, WPP)
        wlo = early([NG], F32, WPP)
        row_f = early([NG], F32, WPP)
        row_u = early([NG], U32, WPP)
        crow = early([NG, RUN], I32, WPP)
        cless = early([NG, RUN], F32, WPP)
        start_f = early([NG], F32, WPP)
        start_u = early([NG], U32, WPP)
        cnt_f = early([NG], F32, WPP)
        run_d = early([NG, RUN], I32, WPP)
        run_s = early([NG, RUN], I32, WPP)
        rel = early([NG, RUN], F32, WPP)
        valid = early([NG, RUN], F32, WPP)
        inside = early([NG, RUN], F32, WPP)
        blk_i = early([NG, RUN], I32, WPP)
        lo_i = early([NG, RUN], I32, WPP)
        key_f = early([NG, RUN], F32, WPP)
        key1 = early([NG, RUN], F32, WPP)
        lo1 = early([NG, RUN], F32, WPP)
        not_end = early([NG], F32, WPP)
        deg_eq = early([NT * P // WD, WD], F16, RUN)
        b1sq = early([D], F32)
        w2_early = early([KD, 2 * D], F32)
        wsq = [early([KD, 2 * D], F32) for _ in range(2)]

        oh_used = [0]

        def later(shape, dt, flat=onehots, used=oh_used):
            n = 1
            for d in shape:
                n *= d
            a = flat[:, used[0]:used[0] + 2 * n].bitcast(dt)
            used[0] += 2 * n
            if len(shape) == 2:
                a = a.rearrange("p (a b) -> p a b", b=shape[1])
            if len(shape) == 3:
                a = a.rearrange("p (a b c) -> p a b c", b=shape[1], c=shape[2])
            return a

        tok = [w_flat[:, k * D:(k + 1) * D] for k in range(2 * KD)] + [later([D], F32) for _ in range(KEPT - 2 * KD)]
        uo = yo[:, :].bitcast(F32)
        tri = later([P], F32)
        rw_t = later([KD, NE], F32)
        iota_e = later([NE], F32)
        iota_ei = later([NE], I32)
        lg = later([BATCH, NE], F32)
        mx = later([BATCH, NE], F32)
        mix = later([BATCH, NE], U32)
        less = later([BATCH, NE], F32)
        ex = later([BATCH, NE], F32)
        pick = later([BATCH, TOPK], F32)
        mask = later([BATCH * TOPK, NE], F32)
        both = later([BATCH, NE], F32)
        pairs_of = later([BATCH, NE], F32)
        before = later([BATCH + 1, NE], F32)
        esum = later([BATCH], F32)
        resum = later([BATCH], F32)
        prob = later([BATCH, TOPK], F32)
        base_e = later([NE], F32)
        pos = later([BATCH, NE], F32)
        posm = later([BATCH * TOPK, NE], F32)
        slot_f = later([BATCH * TOPK], F32)
        slot_u = [later([BATCH * TOPK], U32) for _ in range(2)]
        coef = later([NB * BATCH, TOPK], F32)
        slots = later([NB * BATCH * TOPK], U32)
        node = later([NB * BATCH], F32)
        assert oh_used[0] <= 2 * GW * (P + KEYS)

        FREE_TILES = 2 * KD * D // P
        ew1_sb, ew2_sb, eb_sb = (adj[:, n * NE:(n + 1) * NE, 0:2 * KD * D].bitcast(F32) for n in range(3))
        assert 3 * NE <= NT and KD == 2

        def ew(of, e, k):
            return of[:, bass.ds(e, 1), k * D:(k + 1) * D].rearrange("p a n -> p (a n)")

        moe_used = [2 * KD * D]
        y_flat = y[:, :, :].rearrange("p t n -> p (t n)")
        y_used = [0]

        def expert(shape, dt):
            n = 2
            for d in shape:
                n *= d
            if moe_used[0] % AC == 0:
                moe_used[0] += 2 * KD * D
            if moe_used[0] // AC != (moe_used[0] + n - 1) // AC:
                moe_used[0] = (moe_used[0] // AC + 1) * AC + 2 * KD * D
            assert moe_used[0] % AC + n <= AC
            return later(shape, dt, adj_flat, moe_used)

        def expert_y(shape, dt):
            a = later(shape, dt, y_flat, y_used)
            assert y_used[0] <= NT * 2 * D
            return a

        xe = [expert([D], F32) for _ in range(2)]
        xe_t = [expert([D], F32) for _ in range(2)]
        hb = [expert([D], F32) for _ in range(2)]
        ge = [expert([D], F32) for _ in range(2)]
        ge_t = [expert([D], F32) for _ in range(2)]
        ye = [expert([D], F32) for _ in range(2)]
        zero_t = expert_y([D], F32)
        cnt = expert([NE], F32)
        end_i = expert([NE], I32)
        nt_i = expert([NE], I32)
        cum = [expert([NE], F32) for _ in range(4)]
        jump = expert([NE], F32)
        first_row = expert([NE], F32)
        iota_j = key_t[:, 0:2 * NTAB].bitcast(I32)
        jf = expert([NTAB], F32)
        tab_e = expert([NTAB], F32)
        tab_r = expert([NTAB], F32)
        past = expert([NTAB], F32)
        past_all = expert([NE - 1, NTAB], F32)
        stay_all = expert([NE - 1, NTAB], F32)
        stay = expert([NTAB], F32)
        tab_ei = expert([NTAB // 2], I32)
        tab_ef = expert([NTAB], F32)
        tab_ri = expert([NTAB], I32)
        npair_i = expert([2], I32)
        ends_i = expert([2], I32)
        slots_f = expert([NB * BATCH * TOPK], F32)
        moved = expert([NB * BATCH * TOPK], F32)
        slots_y = expert([NB * BATCH, TOPK], U32)
        place_f = [expert([NB * BATCH * TOPK], F32) for _ in range(2)]
        RING = 3
        assert (NT - 1) % RING == 0
        yg = expert_y([RING * TOPK, D], F32)
        ug = expert_y([RING, D], F32)
        og = expert_y([RING, D], F32)
        gix = expert([RING, TOPK], U32)

        names = ["edges_in", "x_in", "w_in", "consts", "iota", "first_ge", "firsts", "chunk_ix", "start_ix",
                 "keys", "keys_tr", "onehot", "counted", "adj_in", "wsq", "wnorm", "wsum", "wroot", "scaled",
                 "var_in", "rstd_in", "normed", "nrm_tr", "nrm_t_in", "projected", "hi_in", "yz_in", "z_out",
                 "agg", "z_in", "h_in", "y2_out", "zx_taken", "sums_free", "logits_in", "tok_free", "pad_ok",
                 "flag_in", "flag_all", "tri_in", "rw_in", "u_ready", "u_out", "logits", "top", "expd",
                 "masks", "prefix", "slots", "flag_out", "all_in", "all_free", "all_keys", "all_onehot",
                 "all_counted", "all_window", "all_kept", "all_done", "deg_eq", "deg_counted", "all_degrees",
                 "held", "pool_held", "pool_step", "z1_in", "table", "ends", "padded", "ys_padded", "zeros",
                 "ew_in", "xe_tr", "xe_t_in", "hid", "hb_in", "ge_in", "ge_tr", "ge_t_in", "ye_ps", "ye_in",
                 "gix_in", "og_in"]
        S = {n: sem(n) for n in names}
        NQ = 5
        y2_in = [sem(f"y2_in{c}") for c in range(NQ)]
        chain = sem("dve_chain")
        chunk_in = [sem(f"chunk_in{q}") for q in range(2)]
        run_in = [sem(f"run_in{q}") for q in range(2)]
        scattered = [sem(f"scattered{q}") for q in range(2)]
        xe_in = [sem(f"xe_in{h}") for h in range(2)]
        ye_out = [sem(f"ye_out{h}") for h in range(2)]
        sum_out_of = [sem(f"sum_out{q}") for q in range(RING)]
        yg_in = [sem(f"yg_in{q}") for q in range(RING)]
        ug_in = [sem(f"ug_in{q}") for q in range(RING)]

        block = ctx.enter_context(nc.Block())
        runs_src = src[0:E].rearrange("(p c) -> p c", c=RUN)
        runs_dst = dst[0:E].rearrange("(p c) -> p c", c=RUN)
        chunks = dst.rearrange("(p c) -> p c", c=CHUNK)
        runs_of_dst = dst.rearrange("(p c) -> p c", c=RUN)

        def tile_rows(ap, t):
            return ap[bass.ds(t * P, P), :]

        def pad_experts(engine, of):
            engine.wait_ge(S["ends"], 1)
            engine.wait_ge(S["zeros"], 1)
            for e in of:
                end = engine.value_load(end_i[0:1, e:e + 1], min_val=e * REGION, max_val=e * REGION + N)
                engine.dma_start(xs_dram[bass.ds(end, P), :], zero_t).then_inc(S["padded"], 16)

        @block.sync
        def _(sp):
            sp.dma_start(dchunk, chunks).then_inc(S["edges_in"], 16)
            sp.dma_start(dnext[0:NCH - 1, 0:1], chunks[1:NCH, 0:1]).then_inc(S["edges_in"], 16)
            sp.dma_start(xt[:, :], x[0:P, :]).then_inc(S["x_in"], 16)
            for to, (l, r) in ((w, (w1l, w1r)), (w2_early, (w2l, w2r))):
                sp.dma_start(to[:, :, 0:D], l.rearrange("(k p) n -> p k n", p=P)).then_inc(S["w_in"], 16)
                sp.dma_start(to[:, :, D:2 * D], r.rearrange("(k p) n -> p k n", p=P)).then_inc(S["w_in"], 16)
            for b, v in ((b1b, b1), (b2b, b2)):
                sp.dma_start(b[:, :], v.rearrange("(a n) -> a n", a=1).to_broadcast((P, D))).then_inc(S["w_in"], 16)
            sp.wait_ge(S["normed"], 1)
            sp.dma_start(xt[:, :], x[P:2 * P, :]).then_inc(S["x_in"], 16)
            with sp.Fori(1, NT - 2) as t:
                sp.wait_ge(S["normed"], t + 1)
                sp.dma_start(xt[:, :], tile_rows(x, t + 1)).then_inc(S["x_in"], 16)
                sp.wait_ge(S["z1_in"], t)
                sp.dma_start(tile_rows(z1_dram, t - 1), zt[:, :]).then_inc(S["z_out"], 16)
            sp.wait_ge(S["pad_ok"], 1)
            sp.dma_start(xt[0:LAST, :], x[(NT - 1) * P:N, :]).then_inc(S["x_in"], 16)
            for t in range(NT - 3, NT):
                sp.wait_ge(S["z1_in"], t + 1)
                sp.dma_start(z1_dram[t * P:(t + 1) * P, :], zt[:, :]).then_inc(S["z_out"], 16)
            sp.wait_ge(S["flag_out"], 1)
            with sp.If(sp.value_load(flag_i[0:1, 0:1], min_val=0, max_val=1) == 1):
                sp.wait_ge(S["projected"], NT)
                sp.wait_ge(S["adj_in"], NGROUP)
                sp.dma_start(edge_i, dst.rearrange("(p c) -> p c", c=ALL_COLS)).then_inc(S["all_in"], 16)
                sp.wait_ge(S["all_free"], 1)
                sp.dma_start(edge_i, src.rearrange("(p c) -> p c", c=ALL_COLS)).then_inc(S["all_in"], 16)
                sp.wait_ge(S["all_done"], 1)
            sp.wait_ge(S["projected"], NT)
            sp.dma_start(w[:, :, 0:D], w2l.rearrange("(k p) n -> p k n", p=P)).then_inc(S["w_in"], 16)
            sp.dma_start(w[:, :, D:2 * D], w2r.rearrange("(k p) n -> p k n", p=P)).then_inc(S["w_in"], 16)
            sp.wait_ge(S["z_out"], 16 * NT)
            sp.dma_start(zi[:, :], z1_dram[0:P, :]).then_inc(S["z_in"], 16)
            with sp.Fori(0, NT - 1) as t:
                sp.wait_ge(S["h_in"], t + 1)
                sp.dma_start(zi[:, :], tile_rows(z1_dram, t + 1)).then_inc(S["z_in"], 16)
                sp.wait_ge(S["yz_in"], t + 1 + NT)
                sp.dma_start(tile_rows(z2_dram, t), zt[:, :]).then_inc(S["y2_out"], 16)
                sp.dma_start(tile_rows(y2_dram, t), yo[:, :]).then_inc(S["y2_out"], 16)
            sp.wait_ge(S["yz_in"], 2 * NT)
            sp.dma_start(z2_dram[(NT - 1) * P:, :], zt[:, :]).then_inc(S["y2_out"], 16)
            sp.dma_start(y2_dram[(NT - 1) * P:, :], yo[:, :]).then_inc(S["y2_out"], 16)
            sp.wait_ge(S["y2_out"], 32 * NT)
            y2v = y2_dram.rearrange("(t p) c -> p t c", p=P)
            for c in range(NQ):
                sp.dma_start(y[:, NT // NQ * c:NT // NQ * (c + 1), 0:2 * D], y2v[:, NT // NQ * c:NT // NQ * (c + 1), :]
                             ).then_inc(y2_in[c], 16)
                if c == 0:
                    sp.dma_start(zi[:, :], z2_dram[0:P, :]).then_inc(S["z_in"], 16)
                    sp.dma_start(xt[:, :], x[0:P, :]).then_inc(S["x_in"], 16)
            for k in range(KD):
                sp.dma_start(rw_t[:, k, :], router_w[:, k * P:(k + 1) * P].rearrange("e p -> p e")
                             ).then_inc(S["rw_in"], 16)
            def node_tile(t):
                sp.wait_ge(S["zx_taken"], t + 1)
                sp.dma_start(zi[:, :], tile_rows(z2_dram, t + 1)).then_inc(S["z_in"], 16)
                sp.dma_start(xt[:, :], tile_rows(x, t + 1)).then_inc(S["x_in"], 16)
                sp.wait_ge(S["u_ready"], t + 1)
                sp.dma_start(tile_rows(u_dram, t), uo).then_inc(S["u_out"], 16)

            with sp.Fori(0, FREE_TILES) as t:
                node_tile(t)
            with sp.Fori(0, NE) as e:
                node_tile(e + FREE_TILES)
                sp.wait_ge(S["agg"], NT + FREE_TILES)
                for to, w_e in ((ew1_sb, ew1), (ew2_sb, ew2)):
                    sp.dma_start(to[:, bass.ds(e, 1), :].rearrange("p a (k n) -> p (a k) n", n=D),
                                 w_e[bass.ds(e, 1), :, :].rearrange("a (k p) n -> p (a k) n", p=P)
                                 ).then_inc(S["ew_in"], 16)
                for n, b_e in enumerate((eb1, eb2)):
                    sp.dma_start(ew(eb_sb, e, n), b_e[bass.ds(e, 1), :].to_broadcast((P, D))).then_inc(S["ew_in"], 16)
            with sp.Fori(FREE_TILES + NE, NT - 2) as t:
                node_tile(t)
            sp.wait_ge(S["zx_taken"], NT - 1)
            sp.dma_start(zi[:, :], z2_dram[(NT - 1) * P:, :]).then_inc(S["z_in"], 16)
            sp.dma_start(xt[0:LAST, :], x[(NT - 1) * P:N, :]).then_inc(S["x_in"], 16)
            for t in range(NT - 2, NT):
                sp.wait_ge(S["u_ready"], t + 1)
                sp.dma_start(u_dram[t * P:(t + 1) * P, :], uo).then_inc(S["u_out"], 16)
            pad_experts(sp, range(0, NE // 2))
            sp.wait_ge(S["table"], 1)
            pairs = sp.value_load(npair_i[0:1, 0:1], min_val=MIN_PAIRS, max_val=(MAX_TILES + 1) // 2)

            def rows_of_pair(i):
                return [sp.value_load(tab_ri[0:1, bass.ds(i * 2 + h, 1)], min_val=0, max_val=NE * REGION - P)
                        for h in range(2)]

            def load_pair(i, rows_at=None):
                for h, row in enumerate(rows_at or rows_of_pair(i)):
                    sp.dma_start(xe[h], xs_dram[bass.ds(row, P), :]).then_inc(xe_in[h], 16)

            first_rows = rows_of_pair(0)
            sp.wait_ge(S["padded"], 16 * NE)
            for q in range(2):
                sp.wait_ge(scattered[q], 16 * TOPK * len(range(q, NT, 2)))
            load_pair(0, first_rows)
            end = sp.value_load(ends_i[0:1, 0:1], min_val=MIN_TILES * P, max_val=YS_TILES * P)
            sp.dma_start(ys_dram[bass.ds(end, SPARE * P), :].rearrange("(t p) n -> p t n", p=P),
                         zero_t.rearrange("p (a n) -> p a n", a=1).to_broadcast((P, SPARE, D))
                         ).then_inc(S["ys_padded"], 16)
            sp.wait_ge(S["xe_tr"], 1)
            load_pair(1)
            with sp.Fori(0, pairs) as i:
                sp.wait_ge(S["xe_tr"], i + 2)
                load_pair(i + 2)
            sp.wait_ge(S["u_out"], 16 * NT)
            for t in range(RING):
                sp.dma_start(ug[:, t, :], u_dram[t * P:(t + 1) * P, :]).then_inc(ug_in[t], 16)

            def sum_out(t, s, more=True):
                sp.wait_ge(S["og_in"], t + 1)
                sp.dma_start(tile_rows(out, t), og[:, s, :]).then_inc(sum_out_of[s], 16)
                if more:
                    sp.dma_start(ug[:, s, :], tile_rows(u_dram, t + RING)).then_inc(ug_in[s], 16)

            sum_out(0, 0)
            with sp.Fori(0, NT // RING - 1) as i:
                for q in range(RING):
                    sum_out(i * RING + (q + 1), (q + 1) % RING)
            for t in range(NT - RING, NT - 1):
                sum_out(t, t % RING, False)
            sp.wait_ge(S["og_in"], NT)
            sp.dma_start(out[(NT - 1) * P:N, :], og[0:LAST, (NT - 1) % RING, :]
                         ).then_inc(sum_out_of[(NT - 1) % RING], 16)
            for q in range(RING):
                sp.wait_ge(sum_out_of[q], 16 * len(range(q, NT, RING)))

        @block.gpsimd
        def _(pool):
            g = nc.gpsimd
            g.iota(wstart, [[WD, NW]], base=0, channel_multiplier=0).then_inc(S["iota"], 1)
            g.iota(wlo_i, [[WD * WPP, NG]], base=0, channel_multiplier=WD).then_inc(S["iota"], 1)
            g.iota(iota_4[:, :, :], [[1, P], [0, HALF]], base=1, channel_multiplier=0,
                   allow_small_or_imprecise_dtypes=True).then_inc(S["iota"], 1)
            pool.wait_ge(S["consts"], 1)
            g.affine_select(out=ident[:, :], in_=ident[:, :], compare_op=ALU.not_equal, fill=1.0, base=0,
                            pattern=[[-1, P]], channel_multiplier=1).then_inc(S["iota"], 1)
            pool.wait_ge(S["chunk_ix"], 1)
            for part, (lo, hi) in enumerate(PARTS):
                for k in range(lo, hi):
                    g.indirect_dma_start(crow[:, k, :], None, runs_of_dst,
                                         bass.IndirectOffsetOnAxis(ap=row_u[:, k:k + 1], axis=0)
                                         ).then_inc(chunk_in[part], 16)
            for part, (lo, hi) in enumerate(PARTS):
                pool.wait_ge(S["start_ix"], part + 1)
                for k in range(lo, hi):
                    for r, v in ((run_d, runs_dst), (run_s, runs_src)):
                        g.indirect_dma_start(r[:, k, :], None, v,
                                             bass.IndirectOffsetOnAxis(ap=start_u[:, k:k + 1], axis=1)
                                             ).then_inc(run_in[part], 16)
            pool.wait_ge(S["flag_in"], len(PARTS))
            g.partition_all_reduce(flag_all[:, :], flag[:, :], P, RMAX).then_inc(S["flag_all"], 1)
            with pool.Fori(0, NT) as t:
                pool.wait_ge(S["var_in"], t + 1)
                g.tensor_tensor(stat[:, 8:9], stat[:, 9:10], stat[:, 10:11], ALU.pow).then_inc(S["pool_step"], 1)
                pool.wait_ge(S["pool_step"], t + 1)
                g.tensor_tensor(stat[:, 13:14], stat[:, 8:9], stat[:, 12:13], ALU.mult).then_inc(S["rstd_in"], 1)
            pool.wait_ge(S["agg"], 1)
            g.iota(iota_ei, [[1, NE]], base=0, channel_multiplier=0).then_inc(S["iota"], 1)
            g.iota(iota_j, [[1, NTAB]], base=0, channel_multiplier=0).then_inc(S["iota"], 1)
            pool.wait_ge(S["tri_in"], 1)
            g.affine_select(out=node[:, NB * BATCH - 1:], in_=node[:, NB * BATCH - 1:], compare_op=ALU.is_ge, fill=0.0,
                            base=LAST - 1, pattern=[[0, 1]], channel_multiplier=-1).then_inc(S["iota"], 1)
            g.affine_select(out=tri, in_=tri, compare_op=ALU.is_gt, fill=0.0, base=0,
                            pattern=[[1, P]], channel_multiplier=-1).then_inc(S["iota"], 1)

            def root(t):
                pool.wait_ge(S["var_in"], t + NT + 1)
                g.tensor_tensor(stat[:, 8:9], stat[:, 9:10], stat[:, 10:11], ALU.pow).then_inc(S["rstd_in"], 1)

            def scatter(i, s, rows=P, first=False):
                pool.wait_ge(S["slots"], i * 2 + (s // BATCH + 1))
                pool.sem_inc(S["pool_held"], 1)
                for k in range(TOPK):
                    g.indirect_dma_start(xs_dram, bass.IndirectOffsetOnAxis(
                        ap=slot_u[s // BATCH][0:rows, s % BATCH * TOPK + k:s % BATCH * TOPK + k + 1], axis=0),
                        tok[(s + KEPT - AHEAD) % KEPT][0:rows, :], None).then_inc(scattered[(s + 1) % 2], 16)
                if not first:
                    last = s % 2
                    pool.wait_ge(scattered[last], (i * BATCH + ((s - BATCH) // 2 + 1)) * (16 * TOPK))
                    pool.sem_inc(S["tok_free"], 1)

            def turn_of_tiles(i, first=False):
                for r in range(1, KEPT + 1):
                    root(i * KEPT + r)
                    for s in {1: (), KEPT: (KEPT - 2, KEPT - 1)}.get(r, (r - 2,)):
                        if s >= AHEAD or not first:
                            scatter(i, s, first=first and s == AHEAD)

            pool.sem_inc(S["tok_free"], KEPT)
            root(0)
            turn_of_tiles(0, True)
            with pool.Fori(1, (NT - 1) // KEPT) as i:
                turn_of_tiles(i)
            for q in range(BATCH):
                scatter(NB // 2, q, LAST if q == BATCH - 1 else P)
            pool.wait_ge(S["table"], 1)
            pool.wait_ge(S["ys_padded"], 16)
            pairs = pool.value_load(npair_i[0:1, 0:1], min_val=MIN_PAIRS, max_val=(MAX_TILES + 1) // 2)
            with pool.Fori(0, pairs) as i:
                for h in range(2):
                    pool.wait_ge(S["ye_in"], i * 2 + h + 3)
                    pool.dma_start(ys_dram[bass.ds((i * 2 + h) * P, P), :], ye[h]).then_inc(ye_out[h], 16)
            for h in range(2):
                pool.wait_ge(ye_out[h], pairs * 16)
            def gather(t, s):
                pool.wait_ge(S["gix_in"], t + 1)
                pool.sem_inc(S["pool_held"], 1)
                for k in range(TOPK):
                    g.indirect_dma_start(yg[:, s * TOPK + k, :], None, ys_rows,
                                         bass.IndirectOffsetOnAxis(ap=gix[:, s, k:k + 1], axis=0)
                                         ).then_inc(yg_in[s], 16)

            gather(0, 0)
            with pool.Fori(0, NT // RING) as i:
                for q in range(RING):
                    gather(i * RING + (q + 1), (q + 1) % RING)

        def group_onehots(dve, group, slot):
            dve.wait_ge(S["counted"], group - 1)
            group_onehots_now(group, slot)

        def group_onehots_now(group, slot):
            for oh, n, of in ((oh_src, P, lo_t), (oh_key, KEYS, key_t)):
                last = nc.vector.tensor_tensor(
                    oh[0:RUN, slot, :].rearrange("p (g k w) -> p g k w", g=2, w=HALF),
                    iota_4[0:RUN, 0:n, :].rearrange("p (g k) w -> p g k w", g=1).to_broadcast((RUN, 2, n, HALF)),
                    of[0:RUN, bass.ds(group * GW, GW)].rearrange("p (g a w) -> p g a w", g=2, a=1
                                                                 ).to_broadcast((RUN, 2, n, HALF)), ALU.is_equal)
            last.then_inc(S["onehot"], 1)

        def group_counts(pe, group, slot):
            pe.wait_ge(S["onehot"], group + 1)
            for g in range(2):
                stat_g = oh_src[0:RUN, slot, g * HALF * P:(g + 1) * HALF * P].rearrange("p (k w) -> p k w", w=HALF)
                mov_g = oh_key[0:RUN, slot, g * HALF * KEYS:(g + 1) * HALF * KEYS].rearrange("p (k w) -> p k w", w=HALF)
                for h in range(HALF):
                    last = nc.tensor.matmul(counts_ps[:, 2 * slot + g, h * P:h * P + KEYS],
                                            stat_g[:, :, h:h + 1].rearrange("p k a -> p (k a)"),
                                            mov_g[:, :, h:h + 1].rearrange("p k a -> p (k a)"), start=True, stop=True)
            last.then_inc(S["counted"], 1)

        def group_keep(act, group, slot):
            act.wait_ge(S["counted"], group + 1)
            nc.scalar.activation(
                adj[:, :, bass.ds(group * GW * WD, GW * WD)].rearrange("p b (h d) -> p b h d", d=WD),
                counts_ps[:, 2 * slot:2 * slot + 2, :].rearrange("p g (w c) -> p (g w) c", w=HALF)[:, :, 0:KEYS]
                .rearrange("p h (b d) -> p b h d", d=WD),
                ACT.Copy).then_inc(S["adj_in"], 1)

        PER3 = 56
        @block.vector
        def _(dve):
            v = nc.vector
            count = [0]
            base = [0]

            def link(ins):
                count[0] += 1
                ins.then_inc(chain, 1)
                dve.wait_ge(chain, base[0] + count[0])

            v.memset(ident[:, :], 0.0).then_inc(S["consts"], 1)
            v.memset(one_h[:, :], 1.0)
            v.memset(ones[:, :], 1.0).then_inc(S["consts"], 1)
            v.memset(stat[:, 10:11], -0.5)
            v.memset(flag[:, :], 0.0)
            dve.wait_ge(S["edges_in"], 32)
            v.tensor_copy(dchunk_f, dchunk)
            link(v.tensor_copy(dnext_f[0:NCH - 1, 0:1], dnext[0:NCH - 1, 0:1]))
            dve.wait_ge(S["iota"], 3)
            for j in range(FIRSTS):
                last = v.tensor_scalar(below[:, j, :], wstart, dchunk_f[:, j * RUN:j * RUN + 1], None, ALU.is_gt)
            last.then_inc(S["first_ge"], 1)
            v.tensor_copy(wlo, wlo_i)
            v.tensor_tensor(flag[0:NCH - 1, 1:2], dchunk_f[0:NCH - 1, CHUNK - 1:CHUNK], dnext_f[0:NCH - 1, 0:1],
                            ALU.is_gt)
            link(v.tensor_tensor(falls[:, 0:CHUNK - 1], dchunk_f[:, 0:CHUNK - 1], dchunk_f[:, 1:CHUNK], ALU.is_gt))
            v.tensor_reduce(flag[0:NCH, 0:1], falls[:, 0:CHUNK - 1], AX.X, ALU.max)
            dve.wait_ge(S["firsts"], 1)
            link(v.tensor_scalar(row_f, bank[2][0:WPP, 0:NG], -1.0, 0.0, ALU.add, ALU.max))
            v.tensor_copy(row_u, row_f).then_inc(S["chunk_ix"], 1)
            for part, (lo, hi) in enumerate(PARTS):
                dve.wait_ge(chunk_in[part], 16 * (hi - lo))
                for k in range(lo, hi):
                    ins = v.tensor_scalar(cless[:, k, :], crow[:, k, :], wlo[:, k:k + 1], None, ALU.is_lt)
                link(ins)
                link(v.tensor_reduce(cnt_f[:, lo:hi], cless[:, lo:hi, :], AX.X, ALU.add))
                link(v.scalar_tensor_tensor(start_f[:, lo:hi], row_f[:, lo:hi], float(RUN), cnt_f[:, lo:hi],
                                            ALU.mult, ALU.add))
                link(v.tensor_scalar(start_f[:, lo:hi], start_f[:, lo:hi], float(E - RUN), None, ALU.min))
                v.tensor_copy(start_u[:, lo:hi], start_f[:, lo:hi]).then_inc(S["start_ix"], 1)
            dve.wait_ge(S["w_in"], 96)
            v.tensor_tensor(b1sq, b1b[:, :], b1b[:, :], ALU.mult)
            for q, a in zip(wsq, (w[:, :, :], w2_early)):
                v.tensor_tensor(q, a, a, ALU.mult).then_inc(S["wsq"], 1)
            dve.wait_ge(S["wnorm"], 2)
            v.tensor_reduce(scl[:, 0:1], bank[3][:, 0:D], AX.X, ALU.max)
            v.tensor_reduce(scl[:, 1:3], bank[3][:, :].rearrange("p (s n) -> p s n", s=2), AX.X, ALU.add)
            v.tensor_reduce(scl[:, 3:4], bank[1][:, 0:D], AX.X, ALU.max)
            v.tensor_reduce(scl[:, 4:5], b1sq, AX.X, ALU.add).then_inc(S["wsum"], 1)
            dve.wait_ge(S["wroot"], 1)
            root = scl[:, 8:13]
            link(v.tensor_scalar(scl[:, 5:6], root[:, 1:2], root[:, 2:3], float(D) ** 0.5, ALU.add, ALU.mult))
            link(v.tensor_scalar(scl[:, 5:6], scl[:, 5:6], root[:, 4:5], root[:, 3:4], ALU.add, ALU.mult))
            link(v.tensor_scalar(scl[:, 4:5], root[:, 0:1], float(D) ** 0.5, None, ALU.mult))
            link(v.tensor_scalar(scl[:, 4:6], scl[:, 4:6], 1e-30, None, ALU.max))
            link(v.tensor_scalar(scl_i[:, 0:2], scl[:, 4:6].bitcast(I32), EXPONENT_AT, None, ALU.logical_shift_right))
            link(v.tensor_scalar(scl_i[:, 2:4], scl_i[:, 0:2], -1.0, 268.0, ALU.mult, ALU.add))
            link(v.tensor_scalar(scl_i[:, 4:6], scl_i[:, 2:4], -1.0, 254.0, ALU.mult, ALU.add))
            v.tensor_scalar(scl_i[:, 8:10], scl_i[:, 2:4], EXPONENT_AT, None, ALU.logical_shift_left)
            link(v.tensor_scalar(scl_i[:, 10:12], scl_i[:, 4:6], EXPONENT_AT, None, ALU.logical_shift_left))
            v.memset(deg_eq[:, NW:, :], 0.0)
            link(v.tensor_scalar(not_end, start_f, float(E - RUN), None, ALU.is_lt))
            for part, (lo, hi) in enumerate(PARTS):
                dve.wait_ge(run_in[part], 32 * (hi - lo))
                for k in range(lo, hi):
                    v.tensor_scalar(rel[:, k, :], run_d[:, k, :], wlo[:, k:k + 1], None, ALU.subtract)
                g_ = slice(lo, hi)
                v.tensor_scalar(blk_i[:, g_], run_s[:, g_], P.bit_length() - 1, None, ALU.logical_shift_right)
                link(v.tensor_scalar(lo_i[:, g_], run_s[:, g_], P - 1, None, ALU.bitwise_and))
                v.tensor_scalar(inside[:, g_], rel[:, g_], 0.0, None, ALU.is_ge)
                v.tensor_scalar(lo1[:, g_], lo_i[:, g_], 1.0, None, ALU.add)
                link(v.scalar_tensor_tensor(key_f[:, g_], blk_i[:, g_], float(WD), rel[:, g_], ALU.mult, ALU.add))
                link(v.scalar_tensor_tensor(valid[:, g_], rel[:, g_], float(WD), inside[:, g_], ALU.is_lt, ALU.mult))
                v.scalar_tensor_tensor(key1[:, g_], key_f[:, g_], 1.0, valid[:, g_], ALU.add, ALU.mult
                                       ).then_inc(S["keys"], 1)
                v.scalar_tensor_tensor(flag[0:WPP, 2 + lo:2 + hi], rel[:, g_, RUN - 1:RUN].rearrange("p g a -> p (g a)"),
                                       float(WD), not_end[:, g_], ALU.is_lt, ALU.mult).then_inc(S["flag_in"], 1)
            for part, (lo, hi) in enumerate(PARTS):
                m, at = (hi - lo) * WPP, lo * WPP
                dve.wait_ge(S["keys_tr"], part + 1)
                v.tensor_copy(key_t[0:RUN, at:at + m], counts_ps[0:RUN, part, 0:m])
                v.tensor_copy(lo_t[0:RUN, at:at + m], counts_ps[0:RUN, 2 + part, 0:m])
                for d in range(WD):
                    last = v.tensor_scalar(deg_eq[:, at:at + m, d:d + 1].rearrange("p w a -> p (w a)"),
                                           bank[part][0:RUN, 0:m], float(d), None, ALU.is_equal)
            last.then_inc(S["deg_eq"], 1)
            dve.wait_ge(S["deg_eq"], 1)
            v.memset(stat[:, 11:12], 0.0).then_inc(S["scaled"], 1)

            def stats(t):
                dve.wait_ge(S["x_in"], 16 * (t + 1))
                link(v.bn_stats(stat[:, 0:6], xt[:, :]))
                dve.sem_inc(S["held"], 1)
                link(v.bn_aggr(stat[:, 6:8], stat[:, 0:6]))
                v.tensor_scalar(stat[:, 12:13], stat[:, 6:7], -1.0, None, ALU.mult)
                v.tensor_scalar(stat[:, 9:10], stat[:, 7:8], EPS, None, ALU.add).then_inc(S["var_in"], 1)

            def split_y(t, out_, scale, bias=None):
                dve.wait_ge(S["hi_in"], t + 1)
                last = v.scalar_tensor_tensor(out_[0], bank[1][:, 0:D], scale, out_[1], ALU.mult, ALU.subtract)
                if bias is not None:
                    last = v.tensor_tensor(zt[:, :], bank[1][:, D:2 * D], bias, ALU.add)
                last.then_inc(S["yz_in"], 1)

            def yrow(t):
                return (y[:, bass.ds(t, 1), 0:D].rearrange("p a n -> p (a n)"),
                        y[:, bass.ds(t, 1), D:2 * D].rearrange("p a n -> p (a n)"))

            s1 = scl_i[:, 8:9].bitcast(F32)
            s2 = scl_i[:, 9:10].bitcast(F32)
            i1 = scl_i[:, 10:11].bitcast(F32)
            i2 = scl_i[:, 11:12].bitcast(F32)

            def phase1(t, first=False, groups=TILE_GROUPS):
                stats(t)
                for q in range(groups):
                    group = t * TILE_GROUPS + q
                    if first and q < 2:
                        group_onehots_now(group, q % 2)
                    else:
                        group_onehots(dve, group, q % 2)
                    if q == min(2, groups - 1) and not first:
                        split_y(t - 1, yrow(t - 1), s1)

            phase1(0, True)
            dve.wait_ge(S["deg_counted"], 1)
            v.memset(adj[:, :, NW * WD:AC], 0.0)
            dve.wait_ge(S["flag_all"], 1)
            link(v.tensor_reduce(flag_all[:, 15:16], flag_all[:, 0:2 + NG], AX.X, ALU.max))
            v.tensor_copy(flag_i[:, 0:1], flag_all[:, 15:16]).then_inc(S["flag_out"], 1)
            phase1(1)
            per = 2
            with dve.Fori(2, NT - 1) as t:
                start = count[0]
                base[0] = (t - 2) * per
                phase1(t)
                assert count[0] - start == per
            base[0] = 0
            count[0] += per * (NT - 4)
            dve.wait_ge(S["nrm_tr"], NT - 1)
            link(v.memset(xt[:, :], 0.0))
            v.memset(stat[:, 11:12], 0.0).then_inc(S["pad_ok"], 1)
            phase1(NT - 1, groups=NGROUP - (NT - 1) * TILE_GROUPS)
            split_y(NT - 1, yrow(NT - 1), s1)

            dve.wait_ge(S["flag_out"], 1)
            with dve.If(dve.value_load(flag_i[0:1, 0:1], min_val=0, max_val=1) == 1):
                n = [0]

                def then(ins, at=0):
                    n[0] += 1
                    ins.then_inc(S["all_keys"], 1)
                    dve.wait_ge(S["all_keys"], at + n[0])

                dve.wait_ge(S["projected"], NT)
                dve.wait_ge(S["z_out"], 16 * NT)
                dve.wait_ge(S["counted"], NGROUP)
                dve.wait_ge(S["all_in"], 16)
                then(v.memset(zero_h, 0.0))
                then(v.memset(window_at, 0.0))
                v.tensor_copy(edge_dst, edge_i).then_inc(S["all_free"], 1)
                dve.wait_ge(S["all_in"], 32)
                then(v.tensor_scalar(edge_rel.bitcast(I32), edge_i, P - 1, None, ALU.bitwise_and))
                then(v.tensor_scalar(edge_key.bitcast(I32), edge_i, P.bit_length() - 1, None, ALU.logical_shift_right))
                then(v.tensor_scalar(edge_lo, edge_rel.bitcast(I32), 1.0, None, ALU.add))
                then(v.tensor_scalar(edge_blk, edge_key.bitcast(I32), float(WD), 1.0, ALU.mult, ALU.add))
                with dve.Fori(0, NW) as wi:
                    at, links = wi * 5, n[0]
                    then(v.tensor_scalar(edge_rel, edge_dst, window_at, None, ALU.subtract), at)
                    dve.wait_ge(S["all_counted"], wi * STEPS + 2)
                    then(v.tensor_tensor(edge_key, edge_blk, edge_rel, ALU.add), at)
                    then(v.scalar_tensor_tensor(edge_key, edge_rel, 0.0, edge_key, ALU.is_ge, ALU.mult), at)
                    then(v.scalar_tensor_tensor(edge_key, edge_rel, float(WD), edge_key, ALU.is_lt, ALU.mult), at)
                    then(v.tensor_scalar(window_at, window_at, float(WD), None, ALU.add), at)
                    assert n[0] - links == 5
                    n[0] = links
                    dve.sem_inc(S["held"], 1)
                    with dve.Fori(0, STEPS // 2) as i:
                        for q in range(2):
                            dve.wait_ge(S["all_counted"], wi * STEPS + i * 2 + (q + 1))
                            for c in range(STEP):
                                col = (i * 2 + q) * STEP + c
                                v.tensor_scalar(all_src[:, q, c, :], all_iota,
                                                edge_lo[:, bass.ds(col, 1)], None, ALU.is_equal)
                                last = v.tensor_scalar(all_key[:, q, c, :], all_iota[:, 0:KEYS],
                                                       edge_key[:, bass.ds(col, 1)], None, ALU.is_equal)
                            last.then_inc(S["all_onehot"], 1)

                dve.wait_ge(S["all_degrees"], NT)
            dve.wait_ge(S["deg_counted"], 1)
            link(v.tensor_scalar(rdeg1[:, :], bank[2][:, 0:NT], 1.0, None, ALU.max))
            link(v.reciprocal(rdeg[:, :], rdeg1[:, :]))
            link(v.tensor_scalar(rdeg1[:, :], rdeg[:, :], i1, None, ALU.mult))

            def phase2(t, s):
                dve.wait_ge(S["z_in"], 16 * (t + 1))
                link(v.tensor_tensor(zi[:, :], zi[:, :], b1b[:, :], ALU.add))
                dve.wait_ge(S["agg"], t + 1)
                d = rdeg1[:, bass.ds(t, 1)]
                link(v.scalar_tensor_tensor(zi[:, :], counts_ps[:, s, 0:D], d, zi[:, :], ALU.mult, ALU.add))
                dve.wait_ge(S["nrm_tr"], t + NT)
                v.scalar_tensor_tensor(nrm[:, :], counts_ps[:, s, D:2 * D], d, zi[:, :], ALU.mult, ALU.add
                                       ).then_inc(S["h_in"], 1)

            def phase2_split(t, first=False):
                if first:
                    dve.wait_ge(S["z_out"], 16 * NT)
                else:
                    dve.wait_ge(S["y2_out"], 32 * t)
                split_y(t + NT, (yo[:, 0:D], yo[:, D:2 * D]), s2, b2b[:, :])

            phase2(0, 0)
            phase2(1, 1)
            phase2_split(0, True)
            phase2(2, 0)
            phase2_split(1)
            per = 4
            with dve.Fori(1, NT // 2) as i:
                start = count[0]
                base[0] = (i - 1) * per
                for q in range(2):
                    phase2(i * 2 + (q + 1), (q + 1) % 2)
                    phase2_split(i * 2 + q)
                assert count[0] - start == per
            base[0] = 0
            count[0] += per * (NT // 2 - 2)
            phase2_split(NT - 1)

            dve.wait_ge(S["counted"], NGROUP)
            dve.wait_ge(S["projected"], 2 * NT)
            v.memset(node[:, 0:AHEAD], 0.0)
            link(v.memset(node[:, AHEAD:], 1.0))
            v.memset(before[:, 0:1, :], 0.0)
            v.memset(tri, 1.0).then_inc(S["tri_in"], 1)
            dve.wait_ge(S["iota"], 8)
            link(v.tensor_copy(iota_e, iota_ei))
            link(v.tensor_scalar(base_e, iota_e, float(REGION), None, ALU.mult))
            link(v.tensor_scalar(rdeg[:, :], rdeg[:, :], i2, None, ALU.mult))

            dve.sem_inc(S["sums_free"], 1)

            def x2_and_norm(t, s, k, alone=False):
                dve.wait_ge(S["z_in"], 16 * (t + 1 + NT))
                dve.wait_ge(S["x_in"], 16 * (t + 1 + NT))
                if not alone:
                    dve.wait_ge(S["u_ready"], t)
                v.tensor_tensor(zt[:, :], zi[:, :], xt[:, :], ALU.add).then_inc(S["zx_taken"], 1)
                dve.wait_ge(S["zx_taken"], t + 1)
                dve.wait_ge(S["agg"], t + 1 + NT)
                d = rdeg[:, bass.ds(t, 1)]
                link(v.scalar_tensor_tensor(zt[:, :], counts_ps[:, s, 0:D], d, zt[:, :], ALU.mult, ALU.add))
                v.scalar_tensor_tensor(zt[:, :], counts_ps[:, s, D:2 * D], d, zt[:, :], ALU.mult, ALU.add
                                       ).then_inc(S["sums_free"], 1)
                dve.wait_ge(S["sums_free"], t + 2)
                link(v.bn_stats(stat[:, 0:6], zt[:, :]))
                dve.sem_inc(S["held"], 1)
                link(v.bn_aggr(stat[:, 6:8], stat[:, 0:6]))
                v.tensor_scalar(stat[:, 9:10], stat[:, 7:8], EPS, None, ALU.add).then_inc(S["var_in"], 1)
                dve.wait_ge(S["tok_free"], t + 1)
                dve.wait_ge(S["rstd_in"], t + 1 + NT)
                v.tensor_scalar(tok[k], zt[:, :], stat[:, 6:7], stat[:, 8:9], ALU.subtract, ALU.mult
                                ).then_inc(S["normed"], 1)
                dve.wait_ge(S["normed"], t + 1 + NT)
                if not alone:
                    dve.wait_ge(S["u_out"], t * 16)
                v.tensor_tensor(uo, zt[:, :], tok[k], ALU.add).then_inc(S["u_ready"], 1)

            def each(a, n):
                return a.rearrange("p (t a) -> p t a", a=1).to_broadcast((P, a.shape[1], n))

            def choose(j):
                dve.wait_ge(S["logits"], j * BATCH + 1)
                v.tensor_copy(lg, bank[1][:, 0:BATCH * NE].rearrange("p (t e) -> p t e", e=NE)
                              ).then_inc(S["logits_in"], 1)
                dve.wait_ge(S["logits_in"], j + 1)
                dve.sem_inc(S["held"], 1)
                for q in range(BATCH):
                    last = v.max(mx[:, q, :], lg[:, q, :])
                link(last)
                v.tensor_tensor(less, mx, mx[:, :, 0:1].to_broadcast((P, BATCH, NE)), ALU.subtract
                                ).then_inc(S["top"], 1)
                for q in range(BATCH):
                    last = v.max_index(mix[:, q, :], mx[:, q, :], lg[:, q, :])
                link(last)
                link(v.tensor_copy(pick, mix[:, :, 0:TOPK]))
                link(v.tensor_tensor(mask, iota_e.rearrange("p (a e) -> p a e", a=1).to_broadcast((P, BATCH * TOPK, NE)),
                                     each(pick.rearrange("p t k -> p (t k)"), NE), ALU.is_equal))
                by_rank = mask.rearrange("p (t k) e -> p t k e", k=TOPK)
                link(v.tensor_tensor(both, by_rank[:, :, 0, :], by_rank[:, :, 1, :], ALU.add))
                link(v.tensor_tensor(both, both, each(node[:, bass.ds(j * BATCH, BATCH)], NE), ALU.mult))
                v.tensor_copy(pairs_of[:, 0:1, :], both[:, 0:1, :])
                link(v.tensor_tensor(pairs_of[:, 1:, :], both[:, 1:, :], both[:, 0:BATCH - 1, :], ALU.add))
                v.tensor_copy(before[:, 1:3, :], pairs_of[:, 0:2, :])
                v.tensor_tensor(before[:, 3:5, :], pairs_of[:, 2:4, :], pairs_of[:, 0:2, :], ALU.add
                                ).then_inc(S["masks"], 1)
                dve.wait_ge(S["expd"], j + 1)
                link(v.tensor_reduce(esum, ex, AX.X, ALU.add))
                link(v.reciprocal(resum, esum))
                link(v.tensor_tensor(prob, ex[:, :, 0:TOPK], each(resum, TOPK), ALU.mult))
                link(v.tensor_reduce(esum, prob, AX.X, ALU.add))
                link(v.tensor_scalar(esum, esum, 1e-12, None, ALU.max))
                link(v.reciprocal(resum, esum))
                v.tensor_tensor(coef[:, bass.ds(j * BATCH, BATCH), :], prob, each(resum, TOPK), ALU.mult)

            def place(j, s):
                dve.wait_ge(S["prefix"], j + 1)
                link(v.tensor_tensor(pos, bank[3][:, 0:BATCH * NE].rearrange("p (t e) -> p t e", e=NE),
                                     base_e.rearrange("p (a e) -> p a e", a=1).to_broadcast((P, BATCH, NE)), ALU.add))
                v.tensor_tensor(base_e, base_e, bank[3][:, BATCH * NE:(BATCH + 1) * NE], ALU.add)
                for k in range(TOPK):
                    last = v.tensor_tensor(posm.rearrange("p (t k) e -> p t k e", k=TOPK)[:, :, k, :],
                                           mask.rearrange("p (t k) e -> p t k e", k=TOPK)[:, :, k, :], pos, ALU.mult)
                link(last)
                link(v.tensor_reduce(slot_f, posm, AX.X, ALU.add))
                v.tensor_copy(slots[:, bass.ds(j * BATCH * TOPK, BATCH * TOPK)], slot_f)
                v.tensor_copy(slot_u[s], slot_f).then_inc(S["slots"], 1)

            x2_and_norm(0, 0, 0, True)
            with dve.Fori(0, (NT - 1) // KEPT) as i:
                start = count[0]
                base[0] = i * PER3
                for r in range(1, KEPT + 1):
                    x2_and_norm(i * KEPT + r, r % 2, r % KEPT)
                    for half in range(2):
                        if r == half * BATCH + 1:
                            choose(i * 2 + half)
                        if r == half * BATCH + 2:
                            place(i * 2 + half, half)
                assert count[0] - start == PER3, count[0] - start
            base[0] = 0
            count[0] += PER3 * ((NT - 1) // KEPT - 1)
            choose(NB - 1)
            place(NB - 1, 0)
            dve.wait_ge(S["agg"], 2 * NT)
            v.memset(zero_t, 0.0).then_inc(S["zeros"], 1)
            v.tensor_copy(end_i, base_e).then_inc(S["ends"], 1)
            link(v.scalar_tensor_tensor(cnt, iota_e, -float(REGION), base_e, ALU.mult, ALU.add))
            link(v.tensor_scalar(nt_i, cnt, float(P - 1), None, ALU.add))
            link(v.tensor_scalar(nt_i, nt_i, P.bit_length() - 1, None, ALU.logical_shift_right))
            link(v.tensor_copy(cum[0], nt_i))
            for n, d in enumerate((1, 2, 4)):
                v.tensor_copy(cum[n + 1][:, 0:d], cum[n][:, 0:d])
                link(v.tensor_tensor(cum[n + 1][:, d:NE], cum[n][:, d:NE], cum[n][:, 0:NE - d], ALU.add))
            total = cum[3][:, NE - 1:NE]
            link(v.tensor_scalar(first_row[:, 1:NE], cum[3][:, 0:NE - 1], -float(P), None, ALU.mult))
            link(v.memset(first_row[:, 0:1], 0.0))
            link(v.scalar_tensor_tensor(first_row, iota_e, float(REGION), first_row, ALU.mult, ALU.add))
            link(v.tensor_tensor(jump[:, 0:NE - 1], first_row[:, 1:NE], first_row[:, 0:NE - 1], ALU.subtract))
            link(v.tensor_copy(jf, iota_j))
            shape = (P, NE - 1, NTAB)
            link(v.tensor_tensor(past_all, jf.rearrange("p (a j) -> p a j", a=1).to_broadcast(shape),
                                 cum[3][:, 0:NE - 1].rearrange("p (e a) -> p e a", a=1).to_broadcast(shape), ALU.is_ge))
            v.tensor_reduce(tab_e, past_all.rearrange("p e j -> p j e"), AX.X, ALU.add)
            link(v.tensor_tensor(stay_all, past_all,
                                 jump[:, 0:NE - 1].rearrange("p (e a) -> p e a", a=1).to_broadcast(shape), ALU.mult))
            link(v.tensor_reduce(stay, stay_all.rearrange("p e j -> p j e"), AX.X, ALU.add))
            link(v.scalar_tensor_tensor(tab_r, jf, float(P), stay, ALU.mult, ALU.add))
            link(v.tensor_scalar(stay, jf, total, None, ALU.is_lt))
            v.tensor_scalar(past, jf, total, None, ALU.is_ge)
            link(v.tensor_copy(cnt[:, 0:1], tab_e[:, 0:1]))
            link(v.tensor_copy(cnt[:, 1:2], tab_r[:, 0:1]))
            v.tensor_tensor(tab_e, tab_e, stay, ALU.mult)
            link(v.tensor_tensor(tab_r, tab_r, stay, ALU.mult))
            link(v.scalar_tensor_tensor(tab_ef, past, cnt[:, 0:1], tab_e, ALU.mult, ALU.add))
            of_pair = tab_ef.rearrange("p (i h) -> p i h", h=2)
            v.scalar_tensor_tensor(tab_ei, of_pair[:, :, 1:2].rearrange("p i h -> p (i h)"), float(NE),
                                   of_pair[:, :, 0:1].rearrange("p i h -> p (i h)"), ALU.mult, ALU.add)
            link(v.scalar_tensor_tensor(tab_ri, past, cnt[:, 1:2], tab_r, ALU.mult, ALU.add))
            v.tensor_scalar(ends_i[:, 0:1], total, float(P), None, ALU.mult)
            link(v.tensor_scalar(npair_i[:, 1:2], total, 1.0, None, ALU.add))
            v.tensor_scalar(npair_i[:, 0:1], npair_i[:, 1:2], 1, None, ALU.logical_shift_right).then_inc(S["table"], 1)

            link(v.tensor_copy(slots_f, slots))
            for e in range(1, NE):
                link(v.tensor_scalar(moved, slots_f, float(e * REGION), jump[:, e - 1:e], ALU.is_ge, ALU.mult))
                if e == 1:
                    kept = slots_f
                link(v.tensor_tensor(place_f[e % 2], kept, moved, ALU.subtract))
                kept = place_f[e % 2]
            v.tensor_copy(slots_y.rearrange("p t k -> p (t k)"), kept)

            dve.wait_ge(S["ew_in"], 16 * 4 * NE)
            dve.wait_ge(S["table"], 1)
            pairs = dve.value_load(npair_i[0:1, 0:1], min_val=MIN_PAIRS, max_val=(MAX_TILES + 1) // 2)

            def experts_of(i):
                both_of = dve.value_load(tab_ei[0:1, bass.ds(i, 1)], min_val=0, max_val=NE * NE - 1)
                return both_of % NE, both_of // NE

            def hidden(i, es):
                for h in range(2):
                    dve.wait_ge(S["hid"], i * 2 + h + 1)
                    v.tensor_tensor(hb[h], counts_ps[:, 2 + h, 0:D], ew(eb_sb, es[h], 0), ALU.add
                                    ).then_inc(S["hb_in"], 1)

            def result(i, es, first=False):
                for h in range(2):
                    dve.wait_ge(S["ye_ps"], i * 2 + h + 1)
                    if not first:
                        dve.wait_ge(ye_out[h], i * 16)
                    v.tensor_tensor(ye[h], bank[2 + h][:, 0:D], ew(eb_sb, es[h], 1), ALU.add).then_inc(S["ye_in"], 1)

            dve.sem_inc(S["ye_in"], 2)
            hidden(0, experts_of(0))
            hidden(1, experts_of(1))
            result(0, experts_of(0), True)
            with dve.Fori(1, pairs) as i:
                hidden(i + 1, experts_of(i + 1))
                result(i, experts_of(i))

            def indices(t, s):
                link(v.tensor_copy(gix[:, s, :], slots_y[:, bass.ds(t + AHEAD, 1), :].rearrange("p a k -> p (a k)")))
                v.memset(stat[:, 14:15], 0.0).then_inc(S["gix_in"], 1)

            def combine(t, s, turn, more=True, first=False):
                dve.wait_ge(yg_in[s], turn * (16 * TOPK) + 16 * TOPK)
                dve.wait_ge(ug_in[s], turn * 16 + 16)
                if not first:
                    dve.wait_ge(sum_out_of[s], turn * 16)
                for k in range(TOPK):
                    ins = v.scalar_tensor_tensor(og[:, s, :], yg[:, s * TOPK + k, :],
                                                 coef[:, bass.ds(t + AHEAD, 1), k:k + 1].rearrange("p a k -> p (a k)"),
                                                 ug[:, s, :] if k == 0 else og[:, s, :], ALU.mult, ALU.add)
                    if k == 0:
                        link(ins)
                ins.then_inc(S["og_in"], 1)
                if more:
                    indices(t + RING, s)

            for t in range(RING):
                indices(t, t)
            for t in range(RING):
                combine(t, t, 0, True, True)
            combine(RING, 0, 1)
            with dve.Fori(1, NT // RING - 1) as i:
                start = count[0]
                base[0] = (i - 1) * (2 * RING)
                for q in range(RING):
                    combine(i * RING + (q + 1), (q + 1) % RING, i + (q + 1) // RING)
                assert count[0] - start == 2 * RING
            base[0] = 0
            count[0] += 2 * RING * (NT // RING - 3)
            for t in range(NT - RING, NT):
                combine(t, t % RING, t // RING, False)

        @block.tensor
        def _(pe):
            te = nc.tensor
            pe.wait_ge(S["consts"], 2)
            pe.wait_ge(S["first_ge"], 1)
            for k in range(NG):
                for j in range(FIRSTS):
                    last = te.matmul(bank[2][0:WPP, k:k + 1], below[:, j, k * WPP:(k + 1) * WPP], one_h[0:NCH, :],
                                     start=(j == 0), stop=(j == FIRSTS - 1))
            last.then_inc(S["firsts"], 1)
            pe.wait_ge(S["wsq"], 2)
            for q, b in zip(wsq, (bank[3], bank[1])):
                for k in range(KD):
                    last = te.matmul(b[:, :], ones[:, :], q[:, k, :], start=(k == 0), stop=(k == KD - 1))
                last.then_inc(S["wnorm"], 1)
            pe.wait_ge(S["iota"], 4)
            pe.wait_ge(S["wsum"], 1)
            for part, (lo, hi) in enumerate(PARTS):
                pe.wait_ge(S["keys"], part + 1)
                for to, a in ((bank[part], rel), (counts_ps[:, part], key1), (counts_ps[:, 2 + part], lo1)):
                    for k in range(lo, hi):
                        last = te.transpose(to[0:RUN, (k - lo) * WPP:(k - lo + 1) * WPP], a[:, k, :],
                                            ident[0:WPP, 0:WPP])
                last.then_inc(S["keys_tr"], 1)
            pe.wait_ge(S["deg_eq"], 1)
            for t in range(NT):
                last = te.matmul(bank[2][:, t:t + 1],
                                 deg_eq[:, t * P // WD:(t + 1) * P // WD, :].rearrange("p w d -> p (w d)"),
                                 one_h[0:RUN, :], start=True, stop=True)
            last.then_inc(S["deg_counted"], 1)

            def transposes(t):
                for k in range(KD):
                    last = te.transpose(bank[0][:, k * P:(k + 1) * P], nrm[:, k * P:(k + 1) * P], ident[:, :])
                last.then_inc(S["nrm_tr"], 1)

            def project_half(t, k, first=False, layer1=False):
                if k == 0:
                    pe.wait_ge(S["nrm_t_in"], t + 1)
                    if not first:
                        pe.wait_ge(S["yz_in"], t)
                        if layer1:
                            pe.wait_ge(S["z1_in"], t)
                last = te.matmul(bank[1][:, :], nrm_t[:, k * P:(k + 1) * P], w[:, k, :],
                                 start=(k == 0), stop=(k == KD - 1))
                if k == KD - 1:
                    last.then_inc(S["projected"], 1)

            def project(t, layer1=False):
                for k in range(KD):
                    project_half(t, k, False, layer1)

            def counts(group, slot, fresh):
                if fresh:
                    pe.wait_ge(S["scaled"], 1)
                else:
                    pe.wait_ge(S["adj_in"], group - 1)
                group_counts(pe, group, slot)

            def phase1(t, first=False, groups=TILE_GROUPS):
                for q in range(groups):
                    counts(t * TILE_GROUPS + q, q % 2, first and q < 2)
                    if q == 1:
                        pe.wait_ge(S["normed"], t + 1)
                        if not first:
                            pe.wait_ge(S["nrm_t_in"], t)
                        transposes(t)
                    if q >= 2:
                        project_half(t, q - 2, first, True)
                if groups == 2:
                    project(t, True)

            phase1(0, True)
            with pe.Fori(1, NT - 1) as t:
                phase1(t)
            phase1(NT - 1, groups=NGROUP - (NT - 1) * TILE_GROUPS)

            def aggregate(t, s, mid=None, at=NT // 3, mid2=None, ready=None):
                for b in range(NT):
                    if ready is not None:
                        ready(b)
                    if mid is not None and b == at:
                        mid()
                    if mid2 is not None and b == NT - 2:
                        mid2()
                    last = te.matmul(counts_ps[:, s, :], adj[:, b, bass.ds(t * P, P)], y[:, b, :],
                                     start=(b == 0), stop=(b == NT - 1))
                last.then_inc(S["agg"], 1)

            def last_tile_in(b):
                if b == NT - 1:
                    pe.wait_ge(S["yz_in"], NT)
                    pe.wait_ge(S["z1_in"], NT)

            def phase2(t, s, fresh=False, first=False):
                if not fresh:
                    pe.wait_ge(S["h_in"], t - 1)

                def mid():
                    pe.wait_ge(S["h_in"], t)
                    pe.wait_ge(S["nrm_t_in"], t + NT - 1)
                    transposes(t + NT - 1)
                aggregate(t, s, None if first else mid, ready=last_tile_in if fresh and first else None)
                if not first:
                    project(t + NT - 1)

            pe.wait_ge(S["flag_out"], 1)
            with pe.If(pe.value_load(flag_i[0:1, 0:1], min_val=0, max_val=1) == 1):
                pe.wait_ge(S["adj_in"], NGROUP)
                pe.sem_inc(S["all_counted"], 2)
                with pe.Fori(0, NW) as wi:
                    pe.wait_ge(S["all_kept"], wi + 1)
                    pe.wait_ge(S["all_onehot"], wi * STEPS + 1)
                    te.matmul(counts_ps[:, 0, 0:KEYS], zero_h, all_iota[:, 0:KEYS], start=True, stop=False)
                    with pe.Fori(0, STEPS // 2) as i:
                        for q in range(2):
                            pe.wait_ge(S["all_onehot"], wi * STEPS + i * 2 + (q + 1))
                            for c in range(STEP):
                                last = te.matmul(counts_ps[:, 0, 0:KEYS], all_src[:, q, c, :],
                                                 all_key[:, q, c, :], start=False, stop=False)
                            last.then_inc(S["all_counted"], 1)
                    te.matmul(counts_ps[:, 0, 0:KEYS], zero_h, all_iota[:, 0:KEYS], start=False, stop=True
                              ).then_inc(S["all_window"], 1)
                pe.wait_ge(S["all_kept"], NW + 1)
                with pe.Fori(0, NT) as t:
                    for b in range(NT):
                        last = te.matmul(bank[2][:, bass.ds(t, 1)], adj[:, b, bass.ds(t * P, P)], one_h[:, :],
                                         start=(b == 0), stop=(b == NT - 1))
                    last.then_inc(S["all_degrees"], 1)
            pe.wait_ge(S["adj_in"], NGROUP)
            phase2(0, 0, True, True)
            pe.wait_ge(S["w_in"], 128)
            phase2(1, 1, True)
            phase2(2, 0)
            with pe.Fori(1, NT // 2) as i:
                for q in range(2):
                    phase2(i * 2 + (q + 1), (q + 1) % 2)
            pe.wait_ge(S["h_in"], NT)
            pe.wait_ge(S["nrm_t_in"], 2 * NT - 1)
            transposes(2 * NT - 1)
            project(2 * NT - 1)

            def route(t, k, step, read=None):
                if step == 0:
                    pe.wait_ge(S["normed"], t + 1 + NT)
                    pe.wait_ge(S["nrm_t_in"], t + 2 * NT)
                    for c in range(KD):
                        last = te.transpose(bank[0][:, c * P:(c + 1) * P], tok[k][:, c * P:(c + 1) * P], ident[:, :])
                    last.then_inc(S["nrm_tr"], 1)
                if step == 1:
                    q = (k + AHEAD) % BATCH
                    pe.wait_ge(S["nrm_t_in"], t + 1 + 2 * NT)
                    if q == 0:
                        pe.wait_ge(S["logits_in"], read)
                    for c in range(KD):
                        last = te.matmul(bank[1][:, q * NE:(q + 1) * NE], nrm_t[:, c * P:(c + 1) * P], rw_t[:, c, :],
                                         start=(c == 0), stop=(c == KD - 1))
                    last.then_inc(S["logits"], 1)

            def prefix(j):
                pe.wait_ge(S["masks"], j + 1)
                te.matmul(bank[3][:, 0:BATCH * NE], tri, both.rearrange("p t e -> p (t e)"), start=True, stop=False)
                te.matmul(bank[3][:, 0:BATCH * NE], ones[:, :], before[:, 0:BATCH, :].rearrange("p t e -> p (t e)"),
                          start=False, stop=True)
                te.matmul(bank[3][:, BATCH * NE:(BATCH + 1) * NE], ones[:, :],
                          before[:, BATCH:, :].rearrange("p t e -> p (t e)"), start=True, stop=True
                          ).then_inc(S["prefix"], 1)

            def first_reads(b):
                if b % (NT // NQ) == 0:
                    pe.wait_ge(y2_in[b // (NT // NQ)], 16)

            aggregate(0, 0, ready=first_reads)
            pe.wait_ge(S["rw_in"], 16 * KD)
            pe.wait_ge(S["iota"], 8)
            with pe.Fori(0, (NT - 1) // KEPT) as i:
                for r in range(1, KEPT + 1):
                    pe.wait_ge(S["sums_free"], i * KEPT + r)
                    read = i * 2 + (r + 2) // BATCH
                    aggregate(i * KEPT + r, r % 2,
                              lambda: route(i * KEPT + (r - 1), r - 1, 0), NT - 7,
                              lambda: route(i * KEPT + (r - 1), r - 1, 1, read))
                    if r % BATCH == 2:
                        prefix(i * 2 + r // BATCH)
            for step in range(2):
                route(NT - 1, 0, step)
            prefix(NB - 1)

            def turn_rows(i):
                for h in range(2):
                    pe.wait_ge(xe_in[h], i * 16 + 16)
                    for k in range(KD):
                        last = te.transpose(counts_ps[:, h, k * P:(k + 1) * P], xe[h][:, k * P:(k + 1) * P], ident[:, :])
                last.then_inc(S["xe_tr"], 1)

            pe.wait_ge(S["table"], 1)
            pairs = pe.value_load(npair_i[0:1, 0:1], min_val=MIN_PAIRS, max_val=(MAX_TILES + 1) // 2)
            turn_rows(0)
            pe.wait_ge(S["ew_in"], 16 * 4 * NE)

            def experts_of(i):
                both_of = pe.value_load(tab_ei[0:1, bass.ds(i, 1)], min_val=0, max_val=NE * NE - 1)
                return both_of % NE, both_of // NE

            def hidden(i, es):
                for h in range(2):
                    pe.wait_ge(S["xe_t_in"], i * 2 + h + 1)
                    for k in range(KD):
                        last = te.matmul(counts_ps[:, 2 + h, 0:D], xe_t[h][:, k * P:(k + 1) * P], ew(ew1_sb, es[h], k),
                                         start=(k == 0), stop=(k == KD - 1))
                    last.then_inc(S["hid"], 1)

            def turn_hidden(i):
                for h in range(2):
                    pe.wait_ge(S["ge_in"], i * 2 + h + 1)
                    for k in range(KD):
                        last = te.transpose(bank[h][:, k * P:(k + 1) * P], ge[h][:, k * P:(k + 1) * P], ident[:, :])
                    last.then_inc(S["ge_tr"], 1)

            def result(i, es):
                for h in range(2):
                    pe.wait_ge(S["ge_t_in"], i * 2 + h + 1)
                    pe.wait_ge(S["ye_in"], i * 2 + h + 1)
                    for k in range(KD):
                        last = te.matmul(bank[2 + h][:, 0:D], ge_t[h][:, k * P:(k + 1) * P], ew(ew2_sb, es[h], k),
                                         start=(k == 0), stop=(k == KD - 1))
                    last.then_inc(S["ye_ps"], 1)

            hidden(0, experts_of(0))
            turn_rows(1)
            turn_hidden(0)
            hidden(1, experts_of(1))
            with pe.Fori(0, pairs) as i:
                result(i, experts_of(i))
                turn_rows(i + 2)
                es = experts_of(i + 2)
                turn_hidden(i + 1)
                hidden(i + 2, es)

        @block.scalar
        def _(act):
            a = nc.scalar
            act.wait_ge(S["wsum"], 1)
            a.activation(scl[:, 8:13], scl[:, 0:5], ACT.Sqrt).then_inc(S["wroot"], 1)
            act.wait_ge(S["scaled"], 1)
            act.wait_ge(S["deg_counted"], 1)

            def turn(t, func):
                act.wait_ge(S["nrm_tr"], t + 1)
                act.wait_ge(S["projected"], t)
                a.activation(nrm_t[:, :], bank[0][:, 0:D], func).then_inc(S["nrm_t_in"], 1)

            def high(t, to, scale):
                act.wait_ge(S["projected"], t + 1)
                a.activation(to, bank[1][:, 0:D], ACT.Copy, scale=scale).then_inc(S["hi_in"], 1)

            def phase1(t, first=False, groups=TILE_GROUPS):
                for q in range(groups):
                    if q == 0:
                        act.wait_ge(S["rstd_in"], t + 1)
                        if not first:
                            act.wait_ge(S["nrm_tr"], t)
                        a.activation(nrm[:, :], xt[:, :], ACT.Identity, bias=stat[:, 13:14], scale=stat[:, 8:9]
                                     ).then_inc(S["normed"], 1)
                    group_keep(act, t * TILE_GROUPS + q, q % 2)
                    if q == 1:
                        if first:
                            act.wait_ge(S["nrm_tr"], 1)
                            a.activation(nrm_t[:, :], bank[0][:, 0:D], ACT.Copy).then_inc(S["nrm_t_in"], 1)
                        else:
                            turn(t, ACT.Copy)
                    if q == groups - 1:
                        act.wait_ge(S["projected"], t + 1)
                        if not first:
                            act.wait_ge(S["z_out"], 16 * t)
                        a.activation(zt[:, :], bank[1][:, D:2 * D], ACT.Copy).then_inc(S["z1_in"], 1)
                        high(t, y[:, bass.ds(t, 1), D:2 * D].rearrange("p a n -> p (a n)"),
                             scl_i[:, 8:9].bitcast(F32))

            phase1(0, True)
            with act.Fori(1, NT - 1) as t:
                phase1(t)
            phase1(NT - 1, groups=NGROUP - (NT - 1) * TILE_GROUPS)

            act.wait_ge(S["flag_out"], 1)
            with act.If(act.value_load(flag_i[0:1, 0:1], min_val=0, max_val=1) == 1):
                act.sem_inc(S["all_kept"], 1)
                with act.Fori(0, NW) as wi:
                    act.wait_ge(S["all_window"], wi + 1)
                    a.activation(adj[:, :, bass.ds(wi * WD, WD)],
                                 counts_ps[:, 0, 0:KEYS].rearrange("p (b d) -> p b d", d=WD), ACT.Copy
                                 ).then_inc(S["all_kept"], 1)
                act.wait_ge(S["all_kept"], NW + 1)
                act.sem_inc(S["all_done"], 1)

            def phase2(t, first=False):
                turn(t + NT, ACT.Relu)
                if not first:
                    act.wait_ge(S["y2_out"], 32 * t)
                high(t + NT, yo[:, D:2 * D], scl_i[:, 9:10].bitcast(F32))

            phase2(0, True)
            with act.Fori(1, NT) as t:
                phase2(t)

            def phase3(t):
                act.wait_ge(S["nrm_tr"], t + 1 + 2 * NT)
                a.activation(nrm_t[:, :], bank[0][:, 0:D], ACT.Copy).then_inc(S["nrm_t_in"], 1)

            def powers(j):
                act.wait_ge(S["top"], j + 1)
                a.activation(ex, less, ACT.Exp).then_inc(S["expd"], 1)

            act.wait_ge(S["counted"], NGROUP)
            with act.Fori(0, (NT - 1) // KEPT) as i:
                for r in range(KEPT):
                    phase3(i * KEPT + r)
                    if r % BATCH == 1:
                        powers(i * 2 + r // BATCH)
            phase3(NT - 1)
            powers(NB - 1)

            pad_experts(act, range(NE // 2, NE))
            act.wait_ge(S["table"], 1)
            pairs = act.value_load(npair_i[0:1, 0:1], min_val=MIN_PAIRS, max_val=(MAX_TILES + 1) // 2)

            def turn_rows():
                for h in range(2):
                    a.activation(xe_t[h], counts_ps[:, h, 0:D], ACT.Copy).then_inc(S["xe_t_in"], 1)

            a.activation(scl[:, 14:15], scl[:, 8:9], ACT.Gelu)

            def gelu(i):
                for h in range(2):
                    act.wait_ge(S["hb_in"], i * 2 + h + 1)
                    a.activation(ge[h], hb[h], ACT.Gelu).then_inc(S["ge_in"], 1)

            act.wait_ge(S["xe_tr"], 1)
            turn_rows()
            gelu(0)
            act.wait_ge(S["xe_tr"], 2)
            turn_rows()
            with act.Fori(0, pairs) as i:
                for h in range(2):
                    act.wait_ge(S["ge_tr"], i * 2 + h + 1)
                    a.activation(ge_t[h], bank[h][:, 0:D], ACT.Copy).then_inc(S["ge_t_in"], 1)
                gelu(i + 1)
                act.wait_ge(S["xe_tr"], i + 3)
                turn_rows()


_INS = ["x", "src", "dst", "L0_gnn_W1_l", "L0_gnn_W1_r", "L0_gnn_b1", "L0_gnn_W2_l", "L0_gnn_W2_r", "L0_gnn_b2",
        "L0_ffn_router_w", "L0_ffn_w1", "L0_ffn_b1", "L0_ffn_w2", "L0_ffn_b2"]


def kernel(**inputs):
    import numpy as _np
    import concourse.bacc as _bacc
    from concourse import mybir as _mybir
    from concourse.bass_utils import run_bass_kernel_spmd as _run

    nc = _bacc.Bacc("TRN2", target_bir_lowering=False, num_devices=1)
    arrays, args = {}, []
    for name in _INS:
        a = _np.ascontiguousarray(inputs[name])
        arrays[f"in_{name}"] = a
        args.append(nc.dram_tensor(f"in_{name}", a.shape, _mybir.dt.from_np(a.dtype), kind="ExternalInput").ap())
    out = nc.dram_tensor("out_0", arrays["in_x"].shape, F32, kind="ExternalOutput").ap()
    with nc.allow_non_contiguous_dma(reason="a few first elements and columns"):
        build(nc, *args, out)
    r = _run(nc, [arrays], core_ids=[0])
    return r.results[0]["out_0"]
```
